# Optimizing a Trainium2 kernel written in Bass

```python
import numpy as np
import jax
import jax.numpy as jnp

def _softmax(x, axis=-1):
    return jax.nn.softmax(x, axis=axis)

def _gelu(x):
    return jax.nn.gelu(x, approximate=True)

def _silu(x):
    return jax.nn.silu(x)

def _sigmoid(x):
    return jax.nn.sigmoid(x)

def _layernorm(x, axis=-1, eps=1e-05):
    m = jnp.mean(x, axis=axis, keepdims=True)
    v = jnp.var(x, axis=axis, keepdims=True)
    return (x - m) / jnp.sqrt(v + eps)

def _scatter_add(tgt, idx, src, axis=0):
    return tgt.at[idx].add(src)

def _segment_sum(src, seg, n):
    return jax.ops.segment_sum(src, seg, n)
kernel_name = 'mk_seq_postln_d2_jaxref_r8_f1d74d'

def setup_inputs(seed: int=0):
    np.random.seed(seed)
    _w = jnp.asarray

    def _L0_attn_setup():
        import jax, jax.numpy as jnp
        import numpy as np
        from jax.scipy.linalg import solve_triangular
        H = 4
        CHUNK = 64
        NORM_EPS = 1e-05

        def _l2norm(x):
            return x / jnp.clip(jnp.linalg.norm(x, axis=-1, keepdims=True), 1e-12)

        def _deltanet_forward(hidden_states, conv_w, Wq, Wk, Wv, Wb, Wg, norm_w, Wo):
            B, L, D = hidden_states.shape
            Kc = conv_w.shape[1]
            dqh = Wq.shape[1] // H
            dvh = Wv.shape[1] // H
            xp = jnp.pad(hidden_states, ((0, 0), (Kc - 1, 0), (0, 0)))
            h = sum((conv_w[:, i] * xp[:, i:i + L, :] for i in range(Kc)))
            h = jax.nn.silu(h)
            q = (h @ Wq).reshape(B, L, H, dqh).transpose(0, 2, 1, 3)
            k = (h @ Wk).reshape(B, L, H, dqh).transpose(0, 2, 1, 3)
            v = (h @ Wv).reshape(B, L, H, dvh).transpose(0, 2, 1, 3)
            q = _l2norm(q)
            k = _l2norm(k)
            beta = jax.nn.sigmoid(h @ Wb).transpose(0, 2, 1)
            qm = q.reshape(B * H, L, dqh)
            km = k.reshape(B * H, L, dqh)
            vm = v.reshape(B * H, L, dvh)
            bm = beta.reshape(B * H, L)
            Nc = L // CHUNK
            eye = jnp.eye(CHUNK, dtype=q.dtype)

            def per_head(qh, kh, vh, bh):
                qs = qh.reshape(Nc, CHUNK, dqh)
                ks_ = kh.reshape(Nc, CHUNK, dqh)
                vs = vh.reshape(Nc, CHUNK, dvh)
                bs = bh.reshape(Nc, CHUNK)

                def step(S, xs):
                    qc, kc, vc, bc = xs
                    kb = kc * bc[:, None]
                    A = jnp.tril(kb @ kc.T, -1)
                    U = solve_triangular(eye + A, vc * bc[:, None] - kb @ S, lower=True)
                    o = qc @ S + jnp.tril(qc @ kc.T) @ U
                    return (S + kc.T @ U, o)
                S0 = jnp.zeros((dqh, dvh), qh.dtype)
                _, o = jax.lax.scan(step, S0, (qs, ks_, vs, bs))
                return o.reshape(L, dvh)
            o = jax.vmap(per_head)(qm, km, vm, bm)
            o = o.reshape(B, H, L, dvh).transpose(0, 2, 1, 3)
            g = (h @ Wg).reshape(B, L, H, dvh)
            rms = o * jax.lax.rsqrt(jnp.mean(o * o, axis=-1, keepdims=True) + NORM_EPS)
            out = rms * norm_w * (g * jax.nn.sigmoid(g))
            return out.reshape(B, L, H * dvh) @ Wo
        key = jax.random.key(seed)
        ks = jax.random.split(key, 9)
        B, L, D = (4, 512, 128)
        dk, dv = (64, 128)
        s = 0.02
        return {'hidden_states': jax.random.normal(ks[0], (B, L, D), jnp.float32), 'conv_w': jax.random.normal(ks[1], (D, 4), jnp.float32) * 0.2, 'Wq': jax.random.normal(ks[2], (D, dk), jnp.float32) * s, 'Wk': jax.random.normal(ks[3], (D, dk), jnp.float32) * s, 'Wv': jax.random.normal(ks[4], (D, dv), jnp.float32) * s, 'Wb': jax.random.normal(ks[5], (D, H), jnp.float32) * s, 'Wg': jax.random.normal(ks[6], (D, dv), jnp.float32) * s, 'norm_w': jnp.ones((dv // H,), jnp.float32), 'Wo': jax.random.normal(ks[7], (dv, D), jnp.float32) * s}
    _L0_attn_in = _L0_attn_setup()

    def _L0_ffn_setup():
        import jax, jax.numpy as jnp
        import numpy as np
        NUM_EXPERTS = 8
        N_EMBD = 128
        D_FF = 4 * N_EMBD
        B, S = (4, 256)
        key = jax.random.key(seed)
        ks = jax.random.split(key, 6)
        x = jax.random.normal(ks[0], (B, S, N_EMBD), dtype=jnp.float32)
        gate_w = jax.random.normal(ks[1], (N_EMBD, NUM_EXPERTS), dtype=jnp.float32) * 0.02
        w1 = jax.random.normal(ks[2], (NUM_EXPERTS, N_EMBD, D_FF), dtype=jnp.float32) * 0.02
        b1 = jnp.zeros((NUM_EXPERTS, D_FF), dtype=jnp.float32)
        w2 = jax.random.normal(ks[3], (NUM_EXPERTS, D_FF, N_EMBD), dtype=jnp.float32) * 0.02
        b2 = jnp.zeros((NUM_EXPERTS, N_EMBD), dtype=jnp.float32)
        return {'x': x, 'gate_w': gate_w, 'w1': w1, 'b1': b1, 'w2': w2, 'b2': b2}
    _L0_ffn_in = _L0_ffn_setup()

    def _L1_attn_setup():
        import jax, jax.numpy as jnp
        import numpy as np
        D_MODEL = 128
        N_HEADS = 16
        D_HEAD = D_MODEL // N_HEADS
        B, L = (2, 256)
        key = jax.random.key(seed)
        ks = jax.random.split(key, 9)
        s = 1.0 / np.sqrt(D_MODEL)
        inp = {'x': jax.random.normal(ks[0], (B, L, D_MODEL), dtype=jnp.float32)}
        for i, name in enumerate(['wq', 'wk', 'wv', 'wo']):
            inp[name + '_w'] = jax.random.normal(ks[1 + 2 * i], (D_MODEL, D_MODEL), dtype=jnp.float32) * s
            inp[name + '_b'] = jax.random.normal(ks[2 + 2 * i], (D_MODEL,), dtype=jnp.float32) * 0.01
        return inp
    _L1_attn_in = _L1_attn_setup()

    def _L1_ffn_setup():
        import jax, jax.numpy as jnp
        import numpy as np
        B, S, H, I, E, TOP_K = (1, 256, 128, 256, 8, 2)
        key = jax.random.key(seed)
        ks = jax.random.split(key, 6)
        x = jax.random.normal(ks[0], (B, S, H), dtype=jnp.float32)
        Wr = jax.random.normal(ks[1], (H, E), dtype=jnp.float32) * (1.0 / np.sqrt(H))
        br = jnp.zeros((E,), dtype=jnp.float32)
        W1 = jax.random.normal(ks[2], (E, H, I), dtype=jnp.float32) * (1.0 / np.sqrt(H))
        W3 = jax.random.normal(ks[3], (E, H, I), dtype=jnp.float32) * (1.0 / np.sqrt(H))
        W2 = jax.random.normal(ks[4], (E, I, H), dtype=jnp.float32) * (1.0 / np.sqrt(I))
        return {'x': x, 'Wr': Wr, 'br': br, 'W1': W1, 'W3': W3, 'W2': W2}
    _L1_ffn_in = _L1_ffn_setup()
    _d = {'L0_attn_hidden_states': _L0_attn_in['hidden_states'], 'L0_attn_conv_w': _L0_attn_in['conv_w'], 'L0_attn_Wq': _L0_attn_in['Wq'], 'L0_attn_Wk': _L0_attn_in['Wk'], 'L0_attn_Wv': _L0_attn_in['Wv'], 'L0_attn_Wb': _L0_attn_in['Wb'], 'L0_attn_Wg': _L0_attn_in['Wg'], 'L0_attn_norm_w': _L0_attn_in['norm_w'], 'L0_attn_Wo': _L0_attn_in['Wo'], 'L0_ffn_gate_w': _L0_ffn_in['gate_w'], 'L0_ffn_w1': _L0_ffn_in['w1'], 'L0_ffn_b1': _L0_ffn_in['b1'], 'L0_ffn_w2': _L0_ffn_in['w2'], 'L0_ffn_b2': _L0_ffn_in['b2'], 'L1_attn_wq_w': _L1_attn_in['wq_w'], 'L1_attn_wq_b': _L1_attn_in['wq_b'], 'L1_attn_wk_w': _L1_attn_in['wk_w'], 'L1_attn_wk_b': _L1_attn_in['wk_b'], 'L1_attn_wv_w': _L1_attn_in['wv_w'], 'L1_attn_wv_b': _L1_attn_in['wv_b'], 'L1_attn_wo_w': _L1_attn_in['wo_w'], 'L1_attn_wo_b': _L1_attn_in['wo_b'], 'L1_ffn_Wr': _L1_ffn_in['Wr'], 'L1_ffn_br': _L1_ffn_in['br'], 'L1_ffn_W1': _L1_ffn_in['W1'], 'L1_ffn_W3': _L1_ffn_in['W3'], 'L1_ffn_W2': _L1_ffn_in['W2']}
    _x0 = _d['L0_attn_hidden_states']
    _d['L0_attn_hidden_states'] = jax.random.normal(jax.random.fold_in(jax.random.key(seed), 1), (2, 2048, 128), dtype=_x0.dtype)
    del _x0
    return _d

def reference(L0_attn_hidden_states, L0_attn_conv_w, L0_attn_Wq, L0_attn_Wk, L0_attn_Wv, L0_attn_Wb, L0_attn_Wg, L0_attn_norm_w, L0_attn_Wo, L0_ffn_gate_w, L0_ffn_w1, L0_ffn_b1, L0_ffn_w2, L0_ffn_b2, L1_attn_wq_w, L1_attn_wq_b, L1_attn_wk_w, L1_attn_wk_b, L1_attn_wv_w, L1_attn_wv_b, L1_attn_wo_w, L1_attn_wo_b, L1_ffn_Wr, L1_ffn_br, L1_ffn_W1, L1_ffn_W3, L1_ffn_W2):

    def _L0_attn_ref(hidden_states, conv_w, Wq, Wk, Wv, Wb, Wg, norm_w, Wo):
        import jax, jax.numpy as jnp
        import numpy as np
        from jax.scipy.linalg import solve_triangular
        H = 4
        CHUNK = 64
        NORM_EPS = 1e-05

        def _l2norm(x):
            return x / jnp.clip(jnp.linalg.norm(x, axis=-1, keepdims=True), 1e-12)

        def _deltanet_forward(hidden_states, conv_w, Wq, Wk, Wv, Wb, Wg, norm_w, Wo):
            B, L, D = hidden_states.shape
            Kc = conv_w.shape[1]
            dqh = Wq.shape[1] // H
            dvh = Wv.shape[1] // H
            xp = jnp.pad(hidden_states, ((0, 0), (Kc - 1, 0), (0, 0)))
            h = sum((conv_w[:, i] * xp[:, i:i + L, :] for i in range(Kc)))
            h = jax.nn.silu(h)
            q = (h @ Wq).reshape(B, L, H, dqh).transpose(0, 2, 1, 3)
            k = (h @ Wk).reshape(B, L, H, dqh).transpose(0, 2, 1, 3)
            v = (h @ Wv).reshape(B, L, H, dvh).transpose(0, 2, 1, 3)
            q = _l2norm(q)
            k = _l2norm(k)
            beta = jax.nn.sigmoid(h @ Wb).transpose(0, 2, 1)
            qm = q.reshape(B * H, L, dqh)
            km = k.reshape(B * H, L, dqh)
            vm = v.reshape(B * H, L, dvh)
            bm = beta.reshape(B * H, L)
            Nc = L // CHUNK
            eye = jnp.eye(CHUNK, dtype=q.dtype)

            def per_head(qh, kh, vh, bh):
                qs = qh.reshape(Nc, CHUNK, dqh)
                ks_ = kh.reshape(Nc, CHUNK, dqh)
                vs = vh.reshape(Nc, CHUNK, dvh)
                bs = bh.reshape(Nc, CHUNK)

                def step(S, xs):
                    qc, kc, vc, bc = xs
                    kb = kc * bc[:, None]
                    A = jnp.tril(kb @ kc.T, -1)
                    U = solve_triangular(eye + A, vc * bc[:, None] - kb @ S, lower=True)
                    o = qc @ S + jnp.tril(qc @ kc.T) @ U
                    return (S + kc.T @ U, o)
                S0 = jnp.zeros((dqh, dvh), qh.dtype)
                _, o = jax.lax.scan(step, S0, (qs, ks_, vs, bs))
                return o.reshape(L, dvh)
            o = jax.vmap(per_head)(qm, km, vm, bm)
            o = o.reshape(B, H, L, dvh).transpose(0, 2, 1, 3)
            g = (h @ Wg).reshape(B, L, H, dvh)
            rms = o * jax.lax.rsqrt(jnp.mean(o * o, axis=-1, keepdims=True) + NORM_EPS)
            out = rms * norm_w * (g * jax.nn.sigmoid(g))
            return out.reshape(B, L, H * dvh) @ Wo
        return _deltanet_forward(hidden_states, conv_w, Wq, Wk, Wv, Wb, Wg, norm_w, Wo)

    def _L0_ffn_ref(x, gate_w, w1, b1, w2, b2):
        import jax, jax.numpy as jnp
        import numpy as np
        NUM_EXPERTS = 8
        N_EMBD = 128
        D_FF = 4 * N_EMBD
        B, S = (4, 256)
        Bb, Ss, D = x.shape
        x_flat = x.reshape(-1, D)
        router_logits = x_flat @ gate_w
        router_probs = jax.nn.softmax(router_logits, axis=-1)
        expert_idx = jnp.argmax(router_probs, axis=-1)
        expert_w = jnp.take_along_axis(router_probs, expert_idx[:, None], axis=1)[:, 0]
        out = jnp.zeros_like(x_flat)
        for e in range(NUM_EXPERTS):
            h = jax.nn.gelu(x_flat @ w1[e] + b1[e], approximate=False)
            y = h @ w2[e] + b2[e]
            sel = expert_idx == e
            out = out + jnp.where(sel, expert_w, 0.0)[:, None] * y
        return out.reshape(Bb, Ss, D)

    def _L1_attn_ref(x, wq_w, wq_b, wk_w, wk_b, wv_w, wv_b, wo_w, wo_b):
        import jax, jax.numpy as jnp
        import numpy as np
        D_MODEL = 128
        N_HEADS = 16
        D_HEAD = D_MODEL // N_HEADS
        B, L = (2, 256)
        b, l, d = x.shape
        h, dh = (N_HEADS, D_HEAD)

        def proj(w, bias):
            return (jnp.einsum('bld,ed->ble', x, w) + bias).reshape(b, l, h, dh).transpose(0, 2, 1, 3)
        Q, K, V = (proj(wq_w, wq_b), proj(wk_w, wk_b), proj(wv_w, wv_b))
        scores = jnp.einsum('bhld,bhsd->bhls', Q, K)
        causal = jnp.tril(jnp.ones((l, l), dtype=scores.dtype))
        out = jnp.einsum('bhls,bhsd->bhld', scores * causal, V)
        out = out.transpose(0, 2, 1, 3).reshape(b, l, d)
        return jnp.einsum('bld,ed->ble', out, wo_w) + wo_b

    def _L1_ffn_ref(x, Wr, br, W1, W3, W2):
        import jax, jax.numpy as jnp
        import numpy as np
        B, S, H, I, E, TOP_K = (1, 256, 128, 256, 8, 2)
        logits = jnp.einsum('bsh,he->bse', x, Wr) + br
        routing_weights, expert_indices = jax.lax.top_k(logits, TOP_K)
        routing_weights = jax.nn.softmax(routing_weights, axis=-1)
        c = jnp.sum(jax.nn.one_hot(expert_indices, E, dtype=x.dtype) * routing_weights[..., None], axis=-2)
        gate = jnp.einsum('bsh,ehi->besi', x, W1)
        up = jnp.einsum('bsh,ehi->besi', x, W3)
        h = jax.nn.silu(gate) * up
        y = jnp.einsum('besi,eih->besh', h, W2)
        out = jnp.einsum('bse,besh->bsh', c, y)
        return out
    x = L0_attn_hidden_states
    x = _layernorm(x + _L0_attn_ref(x, L0_attn_conv_w, L0_attn_Wq, L0_attn_Wk, L0_attn_Wv, L0_attn_Wb, L0_attn_Wg, L0_attn_norm_w, L0_attn_Wo), axis=-1)
    x = _layernorm(x + _L0_ffn_ref(x, L0_ffn_gate_w, L0_ffn_w1, L0_ffn_b1, L0_ffn_w2, L0_ffn_b2), axis=-1)
    x = _layernorm(x + _L1_attn_ref(x, L1_attn_wq_w, L1_attn_wq_b, L1_attn_wk_w, L1_attn_wk_b, L1_attn_wv_w, L1_attn_wv_b, L1_attn_wo_w, L1_attn_wo_b), axis=-1)
    x = _layernorm(x + _L1_ffn_ref(x, L1_ffn_Wr, L1_ffn_br, L1_ffn_W1, L1_ffn_W3, L1_ffn_W2), axis=-1)
    return x

_drawn_inputs = setup_inputs


def setup_inputs(seed=0):
    import zlib

    import numpy as np

    out = dict(_drawn_inputs(seed))
    spreads = {'L0_attn_norm_w': (1.0, 0.6),
     'L0_ffn_b1': (0.0, 0.306),
     'L0_ffn_b2': (0.0, 0.1),
     'L1_ffn_br': (0.0, 0.1)}
    factors = {'L0_attn_Wb': 109.195,
     'L1_attn_wk_b': 3.213,
     'L1_attn_wv_b': 2.775,
     'L1_attn_wo_b': 172.745}
    for name, (base, spread) in spreads.items():
        noise = np.random.default_rng([zlib.crc32(name.encode()), seed]).standard_normal(out[name].shape)
        drawn = base * np.exp(spread * noise) if base else spread * noise
        out[name] = jnp.asarray(drawn.astype(out[name].dtype))
    for name, factor in factors.items():
        out[name] = (out[name] * factor).astype(out[name].dtype)
    return out
```

```python
from contextlib import ExitStack

import concourse.bass as bass
from concourse import mybir

F32 = mybir.dt.float32
ALU = mybir.AluOpType
ACT = mybir.ActivationFunctionType
AX = mybir.AxisListType

P = 128
B, L, D = 2, 2048, 128
BLOCKS = B * L // P
PER = BLOCKS // B
H, DK, DV = 4, 16, 32
QK = H * DK
CH = 32
SUB = 16
NC = P // CH
KC = 3
WID = 2 * QK + 2 * D + H

RW = DV + DK
C_R, C_K = 0, H * RW
C_B, C_Q, C_KB = C_K + QK, C_K + QK + H, C_K + 2 * QK + H
TOKW = C_KB + QK
E = 8
EPS = 1e-5
YW = H * RW + P - RW


def spread(ap, n):
    return ap.unsqueeze(len(ap.shape)).broadcast_to([*ap.shape, n])


TAKEN = []


def take(nc, name):
    TAKEN.append(nc.alloc_semaphore(name))
    return TAKEN[-1]


def give_back(nc):
    with nc.Block() as block:
        @block.gpsimd
        def _(pool):
            nc.clear_and_free_semaphores(TAKEN)
    TAKEN.clear()


def kq_rows(tok, at):
    return tok[:, at, C_K:C_K + 2 * (QK + H)].rearrange("p n (a c) -> p n a c", a=2)[:, :, :, 0:QK]


def stage_project(nc, io, sb, ctx):
    with ExitStack() as st:
        def tmp(name, shp):
            return st.enter_context(nc.sbuf_tensor(name, shp, F32))

        def sem(name):
            return take(nc, name)

        xst = tmp("xst", [P, B, 4, D])
        xT = tmp("xT", [D, B, KC + L])
        conv = tmp("conv", [D, B, 512])
        hT = tmp("hT", [D, B, 512])
        wall = tmp("wall", [D, WID])
        cw = tmp("cw", [D, KC + 1])
        sq = tmp("sq", [P, 2, 2, 2 * QK])
        n2 = tmp("n2", [P, BLOCKS, 2 * H])
        rn = tmp("rn", [P, BLOCKS, 2 * H])
        bl = tmp("bl", [P, BLOCKS, H])
        th = tmp("th", [P, BLOCKS, H])
        psT = [st.enter_context(nc.psum_tensor(f"p_psT{b}", [P, 512], F32)) for b in range(B)]
        psG = [st.enter_context(nc.psum_tensor(f"p_psG{b}", [P, 4, D], F32)) for b in range(B)]
        psP = [st.enter_context(nc.psum_tensor(f"p_psP{i}", [P, 2, 512], F32)) for i in range(2)]

        w_in, x_in, const = sem("w_in"), [sem(f"x_in{b}") for b in range(B)], sem("p_const")
        xT_ps, xT_sb, x_used = sem("xT_ps"), sem("xT_sb"), sem("x_used")
        conv_do, conv_done, h_done = sem("conv_do"), sem("conv_done"), sem("h_done")
        proj, gate_ps, sq_done, gate_done, kq_done, qkv_done, n2_done = (
            sem(n) for n in ("proj", "gate_ps", "sq_done", "gate_done", "kq_done", "qkv_done", "n2_done"))
        v_step, a_step, g_step, stored = sem("pv_step"), sem("pa_step"), sem("pg_step"), sem("p_stored")

        x_dram = io["x"].rearrange("b (t k p) d -> p b t k d", p=P, k=4)
        tok, gate, ident = sb["tok"], sb["gate"], sb["ident"]

        with nc.Block() as block:
            @block.sync
            def _(sp):
                for n, c in (("L0_Wk", 0), ("L0_Wq", QK), ("L0_Wv", 2 * QK), ("L0_Wb", 2 * QK + D), ("L0_Wg", 2 * QK + D + H)):
                    sp.dma_start(wall[:, c:c + io[n].shape[1]], io[n][:, :]).then_inc(w_in, 16)
                sp.dma_start(cw[:, :], io["L0_conv_w"][:, :]).then_inc(w_in, 16)
                for b in range(B):
                    sp.dma_start(xst[:, b], x_dram[:, b, 0]).then_inc(x_in[b], 16)
                with sp.Fori(1, PER // 4) as t:
                    for b in range(B):
                        sp.wait_ge(xT_ps, 2 * t - 1 + b)
                        sp.dma_start(xst[:, b], x_dram[:, b, bass.ds(t, 1)].rearrange("p a k d -> p (a k) d")).then_inc(x_in[b], 16)
                sp.wait_ge(v_step, 4)
                sp.dma_start(io["kb_dram"].rearrange("(n p) c -> p n c", p=P), tok[:, :, C_K:C_K + QK + H]).then_inc(stored, 16)
                sp.wait_ge(stored, 16)
                sp.dma_start(sb["kp"][:, :, :], io["kb_dram"].rearrange("(p i) c -> p i c", i=CH)).then_inc(stored, 16)
                sp.wait_ge(stored, 32)

            @block.gpsimd
            def _(pool):
                pool.memset(ident[:, :], 0.0).then_inc(g_step, 1)
                pool.wait_ge(g_step, 1)
                pool.affine_select(out=ident[:, :], in_=ident[:, :], compare_op=ALU.not_equal, fill=1.0,
                                   base=0, pattern=[[-1, P]], channel_multiplier=1).then_inc(const, 1)
                pool.memset(xT[:, :, 0:KC], 0.0).then_inc(const, 1)
                pool.wait_ge(v_step, 4)
                for b in range(B):
                    s = slice(b * PER, (b + 1) * PER)
                    r = tok[:, s, C_R:C_R + H * RW].rearrange("p n (h c) -> p n h c", h=H)
                    pool.tensor_tensor(r[:, :, :, 0:DV], r[:, :, :, 0:DV],
                                       spread(tok[:, s, C_B:C_B + H], DV), ALU.mult).then_inc(g_step, 1)

            @block.tensor
            def _(pe):
                pe.wait_ge(const, 2)
                pe.wait_ge(w_in, 16 * 6)
                with pe.Fori(0, PER // 4) as t:
                    for b in range(B):
                        pe.wait_ge(x_in[b], t * 16 + 16)
                        pe.wait_ge(xT_sb, 2 * t + b)
                        for k in range(4):
                            mm = nc.tensor.transpose(psT[b][:, k * P:(k + 1) * P], xst[:, b, k], ident[:, :])
                        mm.then_inc(xT_ps, 1)
                    for b in range(B):
                        pe.wait_ge(h_done, 2 * t + b + 1)
                        pe.wait_ge(gate_done, 2 * t + b)
                        for k in range(4):
                            mm = nc.tensor.matmul(psG[b][:, k], hT[:, b, k * P:(k + 1) * P], wall[:, WID - D:WID],
                                                  start=True, stop=True)
                        mm.then_inc(gate_ps, 1)
                        for half in range(2):
                            pe.wait_ge(qkv_done, 4 * t + 2 * b + half)
                            for j in range(2):
                                k = 2 * half + j
                                mm = nc.tensor.matmul(psP[half][:, j, 0:WID - D], hT[:, b, k * P:(k + 1) * P],
                                                      wall[:, 0:WID - D], start=True, stop=True)
                            mm.then_inc(proj, 1)

            @block.scalar
            def _(act):
                with act.Fori(0, PER // 4) as t:
                    for b in range(B):
                        act.wait_ge(xT_ps, 2 * t + b + 1)
                        act.activation(xT[:, b, bass.ds(t * 512 + KC, 512)], psT[b][:, :], ACT.Copy).then_inc(xT_sb, 1)
                    for b in range(B):
                        act.wait_ge(conv_done, 2 * t + b + 1)
                        act.activation(hT[:, b], conv[:, b], ACT.Silu).then_inc(h_done, 1)
                        act.wait_ge(gate_ps, 2 * t + b + 1)
                        act.activation(gate[:, bass.ds(4 * t + b * PER, 4)], psG[b][:, :, :], ACT.Silu).then_inc(gate_done, 1)
                        for half in range(2):
                            act.wait_ge(kq_done, 4 * t + 2 * b + half + 1)
                            act.wait_ge(n2_done, 4 * t + 2 * b + half)
                            act.activation(sq[:, half].rearrange("p n (a c) -> p n a c", a=2),
                                           kq_rows(tok, bass.ds(4 * t + (b * PER + 2 * half), 2)), ACT.Square).then_inc(sq_done, 1)
                act.wait_ge(qkv_done, BLOCKS // 2)
                act.activation(th[:, :, :], bl[:, :, :], ACT.Tanh, scale=0.5).then_inc(a_step, 1)
                act.wait_ge(v_step, 1)
                act.activation(rn[:, :, :], n2[:, :, :], ACT.Sqrt).then_inc(a_step, 1)

            @block.vector
            def _(dve):
                dve.wait_ge(w_in, 16 * 6)
                dve.wait_ge(const, 2)
                with dve.Fori(0, PER // 4) as t:
                    for b in range(B):
                        dve.wait_ge(xT_sb, 2 * t + b + 1)
                        dve.wait_ge(h_done, 2 * t + b)
                        nc.vector.tensor_scalar(conv[:, b], xT[:, b, bass.ds(t * 512, 512)], cw[:, 0:1], None,
                                                ALU.mult).then_inc(conv_do, 1)
                        for i in range(1, KC + 1):
                            dve.wait_ge(conv_do, (2 * t + b) * KC + i)
                            nc.vector.scalar_tensor_tensor(conv[:, b], xT[:, b, bass.ds(t * 512 + i, 512)], cw[:, i:i + 1],
                                                           conv[:, b], ALU.mult, ALU.add)\
                                .then_inc(conv_do if i < KC else conv_done, 1)
                    for b in range(B):
                        for half in range(2):
                            n = 4 * t + 2 * b + half
                            at = bass.ds(4 * t + (b * PER + 2 * half), 2)
                            dve.wait_ge(proj, n + 1)
                            ps = psP[half]
                            nc.vector.tensor_copy(kq_rows(tok, at), ps[:, :, 0:2 * QK].rearrange("p n (a c) -> p n a c", a=2))\
                                .then_inc(kq_done, 1)
                            r = tok[:, at, C_R:C_R + H * RW].rearrange("p n (h c) -> p n h c", h=H)
                            for j in range(2):
                                nc.vector.tensor_copy(r[:, j, :, 0:DV], ps[:, j, 2 * QK:2 * QK + D].rearrange("p (h c) -> p h c", h=H))
                            nc.vector.tensor_copy(bl[:, at], ps[:, :, 2 * QK + D:WID - D]).then_inc(qkv_done, 1)
                            dve.wait_ge(sq_done, n + 1)
                            nc.vector.tensor_reduce(n2[:, at], sq[:, half].rearrange("p n (h c) -> p (n h) c", c=DK),
                                                    AX.X, ALU.add).then_inc(n2_done, 1)
                dve.wait_ge(n2_done, BLOCKS // 2)
                nc.vector.tensor_scalar(n2[:, :, :], n2[:, :, :], 1e-24, None, ALU.max).then_inc(v_step, 1)
                dve.wait_ge(a_step, 2)
                nc.vector.reciprocal(n2[:, :, :], rn[:, :, :]).then_inc(v_step, 1)
                nc.vector.tensor_scalar(tok[:, :, C_B:C_B + H], th[:, :, :], 0.5, 0.5, ALU.mult, ALU.add)
                dve.wait_ge(v_step, 2)
                for b in range(B):
                    s = slice(b * PER, (b + 1) * PER)
                    k = tok[:, s, C_K:C_K + QK].rearrange("p n (h c) -> p n h c", h=H)
                    last = nc.vector.tensor_tensor(k, k, spread(n2[:, s, 0:H], DK), ALU.mult)
                    last.then_inc(v_step, 1)
                for b in range(B):
                    s = slice(b * PER, (b + 1) * PER)
                    q = tok[:, s, C_Q:C_Q + QK].rearrange("p n (h c) -> p n h c", h=H)
                    nc.vector.tensor_tensor(q, q, spread(n2[:, s, H:2 * H], DK), ALU.mult)
                dve.wait_ge(v_step, 4)
                for b in range(B):
                    s = slice(b * PER, (b + 1) * PER)
                    k = tok[:, s, C_K:C_K + QK].rearrange("p n (h c) -> p n h c", h=H)
                    beta = spread(tok[:, s, C_B:C_B + H], DK)
                    nc.vector.tensor_tensor(tok[:, s, C_KB:C_KB + QK].rearrange("p n (h c) -> p n h c", h=H), k, beta, ALU.mult)
                    r = tok[:, s, C_R:C_R + H * RW].rearrange("p n (h c) -> p n h c", h=H)
                    nc.vector.tensor_tensor(r[:, :, :, DV:RW], k, beta, ALU.mult)


def stage_invert(nc, io, sb, ctx):
    SU = CH // SUB
    with ExitStack() as st:
        def tmp(name, shp):
            return st.enter_context(nc.sbuf_tensor(name, shp, F32))

        def sem(name):
            return take(nc, name)

        kp = sb["kp"]
        kb = tmp("kb", [P, CH, QK])
        prod = [tmp(f"i_prod{i}", [P, SU, SUB, QK]) for i in range(2)]
        nA = tmp("nA", [P, SU, H, SUB, SUB])
        T = tmp("T", [P, SU, H, SUB, SUB])
        nw = tmp("nw", [P, DV])
        TT = tmp("TT", [P, SU, SUB, H, SUB])
        chain, mul_v, mul_g, red, t_ready, stored, fwd, nw_in = (sem(n) for n in (
            "i_chain", "mul_v", "mul_g", "red", "t_ready", "i_stored", "fwd", "nw_in"))
        t_flat, a_flat = (x.rearrange("p c h i j -> p (c h) i j") for x in (T[:, :, :, :, :], nA[:, :, :, :, :]))
        p_flat = prod[0][:, :, :, :].rearrange("p c i f -> p (c i f)")

        def lagged(eng, lag, signal):
            n = SUB - lag
            for c in range(SU):
                i0 = c * SUB
                ins = eng.tensor_tensor(prod[lag % 2][:, c, 0:n], kb[:, i0 + lag:i0 + SUB], kp[:, i0:i0 + n, 0:QK], ALU.mult)
            ins.then_inc(signal, 1)

        with nc.Block() as block:
            @block.gpsimd
            def _(pool):
                pool.memset(T[:, :, :, :, :], 0.0).then_inc(chain, 1)
                pool.wait_ge(chain, 1)
                pool.memset(T[:, :, :, :, :].rearrange("p c h i j -> p (c h) (i j)")[:, :, 0:SUB * SUB:SUB + 1], 1.0).then_inc(chain, 1)
                pool.wait_ge(mul_v, 1)
                for lag in range(2, SUB, 2):
                    if lag > 2:
                        pool.wait_ge(red, lag - 2)
                    lagged(nc.gpsimd, lag, mul_g)
                pool.wait_ge(nw_in, 16)
                for b in range(B):
                    g = sb["gate"][:, b * PER:(b + 1) * PER].rearrange("p n (h c) -> p (n h) c", c=DV)
                    pool.tensor_tensor(g, g, nw[:, :].unsqueeze(1).broadcast_to([P, PER * H, DV]), ALU.mult).then_inc(chain, 1)

            @block.vector
            def _(dve):
                for h in range(H):
                    last = nc.vector.scalar_tensor_tensor(kb[:, :, h * DK:(h + 1) * DK], kp[:, :, h * DK:(h + 1) * DK], -1.0,
                                                          spread(kp[:, :, QK + h], DK), ALU.mult, ALU.mult)
                last.then_inc(mul_v, 1)
                dve.wait_ge(mul_v, 1)
                for lag in range(1, SUB):
                    n = SUB - lag
                    if lag % 2:
                        if lag > 2:
                            dve.wait_ge(red, lag - 2)
                        lagged(nc.vector, lag, mul_v)
                        dve.wait_ge(mul_v, 1 + (lag + 1) // 2)
                    else:
                        dve.wait_ge(mul_g, lag // 2)
                    for c in range(SU):
                        out = nA[:, c].rearrange("p h i j -> p h (i j)")[:, :, lag * SUB:(n + lag - 1) * SUB + n:SUB + 1]
                        ins = nc.vector.tensor_reduce(out.rearrange("p h i -> p i h"),
                                                      prod[lag % 2][:, c, 0:n].rearrange("p i (h d) -> p i h d", h=H), AX.X, ALU.add)
                    ins.then_inc(red, 1)
                dve.wait_ge(red, SUB - 1)
                dve.wait_ge(chain, 2)
                for i in range(1, SUB):
                    out = p_flat[:, 0:SU * H * i * i].rearrange("p (g j m) -> p g j m", j=i, m=i)
                    nc.vector.tensor_tensor(out, a_flat[:, :, i:i + 1, 0:i].broadcast_to([P, SU * H, i, i]),
                                            t_flat[:, :, 0:i, 0:i].rearrange("p g m j -> p g j m"), ALU.mult).then_inc(fwd, 1)
                    dve.wait_ge(fwd, 2 * i - 1)
                    nc.vector.tensor_reduce(t_flat[:, :, i, 0:i], out, AX.X, ALU.add).then_inc(fwd, 1)
                    dve.wait_ge(fwd, 2 * i)
                for c in range(SU):
                    nc.vector.tensor_copy(TT[:, c], T[:, c].rearrange("p h i j -> p j h i")).then_inc(t_ready, 1)

            @block.sync
            def _(sp):
                sp.dma_start(nw[:, :], io["L0_norm_w"].rearrange("(a n) -> a n", a=1).broadcast_to([P, DV])).then_inc(nw_in, 16)
                sp.wait_ge(t_ready, SU)
                sp.dma_start(io["t_dram"].rearrange("(p i) c -> p (i c)", i=CH), TT[:, :, :, :, :].rearrange("p c j h i -> p (c j h i)")).then_inc(stored, 16)
                sp.wait_ge(stored, 16)
                sp.dma_start(sb["tinv"][:, :, :], io["t_dram"].rearrange("(n p) c -> p n c", p=P)).then_inc(stored, 16)
                sp.wait_ge(stored, 32)


def stage_delta(nc, io, sb, ctx):
    N16, HR = P // SUB, H * RW
    with ExitStack() as st:
        def tmp(name, shp):
            return st.enter_context(nc.sbuf_tensor(name, shp, F32))

        def pair(name, shp):
            return [tmp(f"{name}{b}", shp) for b in range(B)]

        def sem(name):
            return take(nc, name)

        def sems(name):
            return [sem(f"{name}{b}") for b in range(B)]

        def bank(name, shp):
            return st.enter_context(nc.psum_tensor(name, shp, F32))

        tok, tinv, o, ident = sb["tok"], sb["tinv"], sb["o"], sb["ident"]
        row = pair("d_row", [P, TOKW])
        kqT = pair("kqT", [P, 3, P])
        kTx = pair("kTx", [P, H, P])
        tbd = pair("tbd", [P, H, N16, SUB])
        kc = pair("kc", [P, NC, QK])
        pa = pair("pa", [P, H, 2, P])
        y0, zz, uw = pair("y0", [P, YW]), pair("zz", [P, YW]), pair("uw", [P, YW])
        qe, qeT, oi = pair("qe", [P, P]), pair("qeT", [P, P]), pair("oi", [P, H, DV])
        w, mt = pair("w", [P, QK]), pair("mt", [P, NC, QK])
        S = [[tmp(f"S{b}{i}", [P, H, DV]) for i in range(2)] for b in range(B)]
        mask_g, mask_m = tmp("mask_g", [P, 2, P]), tmp("mask_m", [QK, H, DK])
        mask_h, mask_c, mask_s = tmp("mask_h", [QK, H]), tmp("mask_c", [P, NC]), tmp("mask_s", [P, N16])
        zero = tmp("d_zero", [P, P])
        psT = [bank(f"d_psT{b}", [P, 512]) for b in range(B)]
        psG = bank("d_psG", [P, B, 512])
        psY = [bank(f"d_psY{b}", [P, 512]) for b in range(B)]
        acc = [bank(f"d_acc{b}", [P, 512]) for b in range(B)]
        g_all = psG[:, :, :].rearrange("p b (h a l) -> p (b h) a l", h=2, a=2)

        const = sem("d_const")
        loaded, t_ps, kq_sb, ktx, expanded, kc_done, g_ps, pa_done = (sems(n) for n in (
            "d_loaded", "t_ps", "kq_sb", "ktx", "expanded", "kc_done", "g_ps", "pa_done"))
        y_ps, y_used, qt_ps, qt_sb, m_ps, m_done, s_ps, s_sb, o_ps, o_done, w_done = (sems(n) for n in (
            "y_ps", "y_used", "qt_ps", "qt_sb", "m_ps", "m_done", "s_ps", "s_sb", "o_ps", "o_done", "w_done"))

        def by_head(t):
            return t[:, 0:HR].rearrange("p (h c) -> p h c", h=H)

        def heads(ps):
            return ps[:, :].rearrange("p (h c) -> p h c", h=H)[:, :, 0:RW]

        def blk(t, b):
            return bass.ds(t + b * PER, 1)

        def keep_where(pool, ap, base, pattern, mult, op=ALU.is_ge):
            pool.wait_ge(const, keep_where.n)
            pool.affine_select(out=ap, in_=ap, compare_op=op, fill=0.0, base=base, pattern=pattern,
                               channel_multiplier=mult).then_inc(const, 1)
            keep_where.n += 1

        with nc.Block() as block:
            @block.sync
            def _(sp):
                for b in range(B):
                    sp.dma_start(row[b][:, :], tok[:, b * PER]).then_inc(loaded[b], 16)
                with sp.Fori(1, PER) as t:
                    for b in range(B):
                        sp.wait_ge(y_used[b], 4 * t)
                        sp.wait_ge(kc_done[b], t)
                        sp.dma_start(row[b][:, :], tok[:, blk(t, b)].rearrange("p a c -> p (a c)")).then_inc(loaded[b], 16)

            @block.gpsimd
            def _(pool):
                pool.memset(zero[:, :], 0.0)
                for b in range(B):
                    for whole in (S[b][0], S[b][1], kqT[b], kTx[b], mt[b], qeT[b], qe[b], y0[b], zz[b], uw[b]):
                        pool.memset(whole[:], 0.0)
                for m, v in ((mask_g, 0.0), (mask_m, -1.0), (mask_h, 1.0), (mask_c, 1.0), (mask_s, 1.0)):
                    pool.memset(m[:], v).then_inc(const, 1)
                pool.wait_ge(const, 5)
                off = mask_g[:, 1].rearrange("p (c i) -> p c i", c=NC)
                cau = mask_g[:, 0].rearrange("p (c i) -> p c i", c=NC)
                pool.memset(off[:, :, SUB:CH], 1.0).then_inc(const, 1)
                pool.memset(cau, 1.0).then_inc(const, 1)
                keep_where.n = 7
                keep_where(pool, off, 0, [[-CH, NC], [0, CH]], 1)
                keep_where(pool, off, SUB - 1, [[CH, NC], [0, CH]], -1)
                keep_where(pool, cau, 0, [[-CH, NC], [0, CH]], 1)
                keep_where(pool, cau, 0, [[CH, NC], [1, CH]], -1)
                keep_where(pool, mask_m[:, :, :], 0, [[-DK, H], [0, DK]], 1)
                keep_where(pool, mask_m[:, :, :], DK - 1, [[DK, H], [0, DK]], -1)
                keep_where(pool, mask_h[:, :], 0, [[-DK, H]], 1)
                keep_where(pool, mask_h[:, :], DK - 1, [[DK, H]], -1)
                keep_where(pool, mask_c[:, :], 0, [[-CH, NC]], 1)
                keep_where(pool, mask_c[:, :], CH - 1, [[CH, NC]], -1)
                keep_where(pool, mask_s[:, :], 0, [[-SUB, N16]], 1)
                keep_where(pool, mask_s[:, :], SUB - 1, [[SUB, N16]], -1)
                pool.wait_ge(const, 19)
                with pool.Fori(0, PER) as t:
                    for b in range(B):
                        pool.wait_ge(kq_sb[b], t + 1)
                        pool.tensor_tensor(kTx[b][0:QK], kqT[b][0:QK, 0:1].broadcast_to([QK, H, P]), spread(mask_h[:, :], P),
                                           ALU.mult).then_inc(ktx[b], 1)
                    for b in range(B):
                        pool.wait_ge(s_ps[b], NC * t)
                        src = tinv[:, blk(t, b)].rearrange("p a (h i) -> p (a h) i", h=H)
                        pool.tensor_tensor(tbd[b][:, :, :, :], src.unsqueeze(2).broadcast_to([P, H, N16, SUB]),
                                           spread(mask_s[:, :], SUB).unsqueeze(1).broadcast_to([P, H, N16, SUB]),
                                           ALU.mult).then_inc(expanded[b], 1)
                    for b in range(B):
                        pool.wait_ge(loaded[b], 16 * t + 16)
                        pool.tensor_tensor(kc[b][:, :, :], row[b][:, C_K:C_K + QK].unsqueeze(1).broadcast_to([P, NC, QK]),
                                           spread(mask_c[:, :], QK), ALU.mult).then_inc(kc_done[b], 1)

            @block.tensor
            def _(pe):
                pe.wait_ge(const, 19)
                for b in range(B):
                    nc.tensor.matmul(acc[b][0:QK, 0:H * DV], zero[:, 0:QK], zero[:, :], start=True, stop=True)
                with pe.Fori(0, PER) as t:
                    for b in range(B):
                        pe.wait_ge(loaded[b], 16 * t + 16)
                        pe.wait_ge(o_done[b], t)
                        for i, c in enumerate((C_K, C_Q, C_KB)):
                            n = min(P, TOKW - c)
                            mm = nc.tensor.transpose(psT[b][0:n, i * P:(i + 1) * P], row[b][:, c:c + n], ident[:, :])
                        mm.then_inc(t_ps[b], 1)

                    def products(k, b, left, right):
                        pe.wait_ge(y_used[b], 4 * t + k)
                        for h in range(H):
                            mm = nc.tensor.matmul(psY[b][:, h * P:(h + 1) * P], left(h), right[:, h * RW:h * RW + P],
                                                  start=True, stop=True)
                        mm.then_inc(y_ps[b], 1)

                    for b in range(B):
                        pe.wait_ge(ktx[b], t + 1)
                        if b == 0:
                            pe.wait_ge(m_done[0], t)
                            pe.wait_ge(m_done[1], t)
                        else:
                            pe.wait_ge(pa_done[0], t + 1)
                        for h in range(H):
                            mm = nc.tensor.matmul(g_all[:, h], kTx[b][:, h], kqT[b][:, 1:3], start=True, stop=True)
                        mm.then_inc(g_ps[b], 1)
                        pe.wait_ge(expanded[b], t + 1)
                        products(0, b, lambda h: tbd[b][:, h].rearrange("p s i -> p (s i)"), row[b])
                    for b in range(B):
                        pe.wait_ge(pa_done[b], t + 1)
                        products(1, b, lambda h: pa[b][:, h, 1], y0[b])
                    for b in range(B):
                        products(2, b, lambda h: tbd[b][:, h].rearrange("p s i -> p (s i)"),
                                 zz[b])
                    for b in range(B):
                        products(3, b, lambda h: pa[b][:, h, 0], uw[b])
                    for b in range(B):
                        pe.wait_ge(kc_done[b], t + 1)
                        pe.wait_ge(w_done[b], t + 1)
                        nc.tensor.matmul(psG[0:QK, b, 0:NC * QK], w[b][:, :], kc[b][:, :, :],
                                         start=True, stop=True).then_inc(m_ps[b], 1)
                    for b in range(B):
                        pe.wait_ge(y_used[b], 4 * t + 4)
                        nc.tensor.transpose(psT[b][:, 0:P], qe[b][:, :], ident[:, :]).then_inc(qt_ps[b], 1)
                    for c in range(NC):
                        for b in range(B):
                            s_now = S[b][c % 2][:, :, :].rearrange("p h c -> p (h c)")
                            if c == 0:
                                pe.wait_ge(m_done[b], t + 1)
                                pe.wait_ge(qt_sb[b], t + 1)
                            pe.wait_ge(s_sb[b], NC * t + c)
                            nc.tensor.matmul(acc[b][0:QK, 0:H * DV], kc[b][:, c], by_head(uw[b])[:, :, 0:DV], start=False, stop=True,
                                             skip_group_check=True)
                            nc.tensor.matmul(acc[b][0:QK, 0:H * DV], mt[b][:, c], s_now, start=False, stop=True,
                                             skip_group_check=True).then_inc(s_ps[b], 1)
                            mm = nc.tensor.matmul(psT[b][c * CH:(c + 1) * CH, 0:H * DV], qeT[b][:, c * CH:(c + 1) * CH], s_now,
                                                  start=True, stop=True)
                            if c == NC - 1:
                                mm.then_inc(o_ps[b], 1)

            @block.scalar
            def _(act):
                with act.Fori(0, PER) as t:
                    for b in range(B):
                        act.wait_ge(t_ps[b], t + 1)
                        act.activation(kqT[b][0:QK].rearrange("p a l -> p (a l)"), psT[b][0:QK, 0:3 * P], ACT.Copy)\
                            .then_inc(kq_sb[b], 1)
                    for k, dst in ((0, y0), (1, zz)):
                        for b in range(B):
                            act.wait_ge(y_ps[b], 4 * t + k + 1)
                            act.activation(by_head(dst[b]), heads(psY[b]), ACT.Copy).then_inc(y_used[b], 1)
                    for b in range(B):
                        act.wait_ge(y_used[b], 4 * t + 3)
                        act.activation(w[b][:, :].rearrange("p (h c) -> p h c", h=H), by_head(uw[b])[:, :, DV:RW], ACT.Copy)\
                            .then_inc(w_done[b], 1)
                    for b in range(B):
                        act.wait_ge(qt_ps[b], t + 1)
                        act.activation(qeT[b][0:QK], psT[b][0:QK, 0:P], ACT.Copy).then_inc(qt_sb[b], 1)

            @block.vector
            def _(dve):
                dve.wait_ge(const, 19)
                with dve.Fori(0, PER) as t:
                    for b in range(B):
                        dve.wait_ge(g_ps[b], t + 1)
                        nc.vector.tensor_tensor(pa[b][:, :, :, :].rearrange("p h a l -> p h (a l)"),
                                                g_all.rearrange("p h a l -> p h (a l)"),
                                                mask_g[:, :, :].rearrange("p a l -> p (a l)").unsqueeze(1).broadcast_to([P, H, 2 * P]),
                                                ALU.mult).then_inc(pa_done[b], 1)
                    for b in range(B):
                        dve.wait_ge(y_ps[b], 4 * t + 3)
                        nc.vector.tensor_tensor(by_head(uw[b]), by_head(y0[b]), heads(psY[b]), ALU.subtract).then_inc(y_used[b], 1)
                    for b in range(B):
                        dve.wait_ge(y_ps[b], 4 * t + 4)
                        y = heads(psY[b])
                        nc.vector.tensor_copy(oi[b][:, :, :], y[:, :, 0:DV])
                        nc.vector.tensor_tensor(qe[b][:, 0:QK].rearrange("p (h c) -> p h c", h=H),
                                                row[b][:, C_Q:C_Q + QK].rearrange("p (h c) -> p h c", h=H), y[:, :, DV:RW],
                                                ALU.subtract).then_inc(y_used[b], 1)
                    for b in range(B):
                        dve.wait_ge(m_ps[b], t + 1)
                        nc.vector.tensor_tensor(mt[b][0:QK], psG[0:QK, b, 0:NC * QK].rearrange("p (c d) -> p c d", c=NC),
                                                mask_m[:, :, :].rearrange("p h d -> p (h d)").unsqueeze(1).broadcast_to([QK, NC, QK]),
                                                ALU.mult).then_inc(m_done[b], 1)
                    for c in range(NC):
                        for b in range(B):
                            dve.wait_ge(s_ps[b], NC * t + c + 1)
                            nc.vector.tensor_tensor(S[b][(c + 1) % 2][0:QK],
                                                    acc[b][0:QK, 0:H * DV].rearrange("p (h e) -> p h e", h=H),
                                                    spread(mask_h[:, :], DV), ALU.mult).then_inc(s_sb[b], 1)
                    for b in range(B):
                        dve.wait_ge(o_ps[b], t + 1)
                        dve.wait_ge(y_used[b], 4 * t + 4)
                        nc.vector.tensor_tensor(o[:, blk(t, b)].rearrange("p a d -> p (a d)"), psT[b][:, 0:H * DV],
                                                oi[b][:, :, :].rearrange("p h c -> p (h c)"), ALU.add).then_inc(o_done[b], 1)


def group(t, b):
    return bass.ds(4 * t + b * PER, 4)


def stage_close_delta(nc, io, sb, ctx):
    with ExitStack() as st:
        def tmp(name, shp):
            return st.enter_context(nc.sbuf_tensor(name, shp, F32))

        def sem(name):
            return take(nc, name)

        def sems(name):
            return [sem(f"{name}{b}") for b in range(B)]

        o, gate, r, ident = sb["o"], sb["gate"], sb["r"], sb["ident"]
        wo = tmp("c_wo", [H * DV, D])
        sq = tmp("c_sq", [P, BLOCKS, D])
        ms, rs = tmp("c_ms", [P, BLOCKS, H]), tmp("c_rs", [P, BLOCKS, H])
        xin = [tmp(f"c_x{b}", [P, 4, D]) for b in range(B)]
        on = [tmp(f"c_on{b}", [P, 4, D]) for b in range(B)]
        og = [tmp(f"c_og{b}", [P, 4, D]) for b in range(B)]
        oT = [tmp(f"c_oT{b}", [P, 4, P]) for b in range(B)]
        psT = [st.enter_context(nc.psum_tensor(f"c_psT{b}", [P, 512], F32)) for b in range(B)]
        psO = [st.enter_context(nc.psum_tensor(f"c_psO{b}", [P, 4, D], F32)) for b in range(B)]
        x_in, t_ps, t_sb, o_ps, r_done, on_done, og_done = (sems(f"c_{n}") for n in (
            "x_in", "t_ps", "t_sb", "o_ps", "r_done", "on_done", "og_done"))
        w_in, squared, rooted, v_step = (sem(f"c_{n}") for n in ("w_in", "squared", "rooted", "v_step"))
        x_dram = io["x"].rearrange("b (t k p) d -> p b t k d", p=P, k=4)

        with nc.Block() as block:
            @block.sync
            def _(sp):
                sp.dma_start(wo[:, :], io["L0_Wo"][:, :]).then_inc(w_in, 16)
                for b in range(B):
                    sp.dma_start(xin[b][:, :, :], x_dram[:, b, 0]).then_inc(x_in[b], 16)
                with sp.Fori(1, PER // 4) as t:
                    for b in range(B):
                        sp.wait_ge(r_done[b], t)
                        sp.dma_start(xin[b][:, :, :], x_dram[:, b, bass.ds(t, 1)].rearrange("p a k d -> p (a k) d"))\
                            .then_inc(x_in[b], 16)

            @block.scalar
            def _(act):
                for b in range(B):
                    act.activation(sq[:, b * PER:(b + 1) * PER], o[:, b * PER:(b + 1) * PER], ACT.Square).then_inc(squared, 1)
                act.wait_ge(v_step, B + 1)
                act.activation(rs[:, :, :], ms[:, :, :], ACT.Sqrt).then_inc(rooted, 1)
                with act.Fori(0, PER // 4) as t:
                    for b in range(B):
                        act.wait_ge(t_ps[b], t + 1)
                        act.activation(oT[b][:, :, :], psT[b][:, :].rearrange("p (k l) -> p k l", k=4), ACT.Copy)\
                            .then_inc(t_sb[b], 1)

            @block.vector
            def _(dve):
                for b in range(B):
                    s = slice(b * PER, (b + 1) * PER)
                    dve.wait_ge(squared, b + 1)
                    nc.vector.tensor_reduce(ms[:, s], sq[:, s].rearrange("p n (h c) -> p n h c", h=H), AX.X, ALU.add)\
                        .then_inc(v_step, 1)
                dve.wait_ge(v_step, B)
                nc.vector.tensor_scalar(ms[:, :, :], ms[:, :, :], 1.0 / DV, EPS, ALU.mult, ALU.add).then_inc(v_step, 1)
                dve.wait_ge(rooted, 1)
                nc.vector.reciprocal(rs[:, :, :], rs[:, :, :]).then_inc(v_step, 1)
                dve.wait_ge(v_step, B + 2)
                with dve.Fori(0, PER // 4) as t:
                    for b in range(B):
                        heads = on[b][:, :, :].rearrange("p k (h c) -> p k h c", h=H)
                        dve.wait_ge(og_done[b], t)
                        nc.vector.tensor_tensor(heads, o[:, group(t, b)].rearrange("p k (h c) -> p k h c", h=H),
                                                spread(rs[:, group(t, b)], DV), ALU.mult).then_inc(on_done[b], 1)
                    for b in range(B):
                        dve.wait_ge(on_done[b], t + 1)
                        dve.wait_ge(t_ps[b], t)
                        nc.vector.tensor_tensor(og[b][:, :, :], on[b][:, :, :], gate[:, group(t, b)], ALU.mult)\
                            .then_inc(og_done[b], 1)
                    for b in range(B):
                        dve.wait_ge(o_ps[b], t + 1)
                        dve.wait_ge(x_in[b], 16 * t + 16)
                        nc.vector.tensor_tensor(r[:, group(t, b)], psO[b][:, :, :], xin[b][:, :, :], ALU.add)\
                            .then_inc(r_done[b], 1)

            @block.tensor
            def _(pe):
                pe.wait_ge(w_in, 16)
                with pe.Fori(0, PER // 4) as t:
                    for b in range(B):
                        pe.wait_ge(t_sb[b], t)
                        pe.wait_ge(og_done[b], t + 1)
                        for k in range(4):
                            mm = nc.tensor.transpose(psT[b][:, k * P:(k + 1) * P], og[b][:, k], ident[:, :])
                        mm.then_inc(t_ps[b], 1)
                    for b in range(B):
                        pe.wait_ge(r_done[b], t)
                        pe.wait_ge(t_sb[b], t + 1)
                        for k in range(4):
                            mm = nc.tensor.matmul(psO[b][:, k], oT[b][:, k], wo[:, :], start=True, stop=True)
                        mm.then_inc(o_ps[b], 1)


def stage_norm(nc, io, sb, tag, router=None):
    with ExitStack() as st:
        def tmp(name, shp):
            return st.enter_context(nc.sbuf_tensor(f"{tag}_{name}", shp, F32))

        def sem(name):
            return take(nc, f"{tag}_{name}")

        def sems(name):
            return [sem(f"{name}{b}") for b in range(B)]

        r, x, xT, ident = sb["r"], sb["x"], sb["xT"], sb["ident"]
        stats = [tmp(f"stats{b}", [P, 4, 6]) for b in range(B)]
        mean, gap, m2 = ([tmp(f"{n}{b}", [P, 4]) for b in range(B)] for n in ("mean", "gap", "m2"))
        ve = [tmp(f"ve{b}", [P, 4]) for b in range(B)]
        sd = [tmp(f"sd{b}", [P, 4]) for b in range(B)]
        rstd = [tmp(f"rstd{b}", [P, 4]) for b in range(B)]
        xn = [tmp(f"xn{b}", [P, 4, D]) for b in range(B)]
        step, rooted, n_done, copied, t_ps, t_sb, t_out, l_ps, l_done, sent = (sems(n) for n in (
            "step", "rooted", "n_done", "copied", "t_ps", "t_sb", "t_out", "l_ps", "l_done", "sent"))
        w_in, padded = sem("w_in"), sem("padded")
        if router is not None:
            xs = [tmp(f"xs{b}", [P, 4, P]) for b in range(B)]
            wr = tmp("wr", [D, P])
            psT = [st.enter_context(nc.psum_tensor(f"{tag}_psT{b}", [P, 512], F32)) for b in range(B)]
            psL = [st.enter_context(nc.psum_tensor(f"{tag}_psL{b}", [P, 4, P], F32)) for b in range(B)]
            logits = sb["logits"]

        with nc.Block() as block:
            @block.vector
            def _(dve):
                with dve.Fori(0, PER // 4) as t:
                    for b in range(B):
                        for k in range(4):
                            src = r[:, bass.ds(4 * t + (b * PER + k), 1)].rearrange("p a d -> p (a d)")
                            ins = nc.vector.bn_stats(stats[b][:, k], src)
                        ins.then_inc(step[b], 1)
                        dve.wait_ge(step[b], 4 * t + 1)
                        s4 = stats[b]
                        nc.vector.tensor_tensor(mean[b][:, :], s4[:, :, 1], s4[:, :, 4], ALU.add)
                        nc.vector.tensor_tensor(gap[b][:, :], s4[:, :, 1], s4[:, :, 4], ALU.subtract)
                        nc.vector.tensor_tensor(m2[b][:, :], s4[:, :, 2], s4[:, :, 5], ALU.add).then_inc(step[b], 1)
                        dve.wait_ge(step[b], 4 * t + 2)
                        nc.vector.tensor_scalar(mean[b][:, :], mean[b][:, :], 0.5, None, ALU.mult)
                        nc.vector.scalar_tensor_tensor(gap[b][:, :], gap[b][:, :], 0.25, gap[b][:, :], ALU.mult, ALU.mult)
                        nc.vector.tensor_scalar(m2[b][:, :], m2[b][:, :], 1.0 / D, EPS, ALU.mult, ALU.add).then_inc(step[b], 1)
                        dve.wait_ge(step[b], 4 * t + 3)
                        nc.vector.tensor_tensor(ve[b][:, :], m2[b][:, :], gap[b][:, :], ALU.add).then_inc(step[b], 1)
                    for b in range(B):
                        dve.wait_ge(rooted[b], t + 1)
                        nc.vector.reciprocal(rstd[b][:, :], sd[b][:, :]).then_inc(l_done[b], 1)
                        dve.wait_ge(l_done[b], t + 1)
                        if router is not None:
                            dve.wait_ge(t_ps[b], t)
                            dve.wait_ge(copied[b], t)
                        else:
                            dve.wait_ge(sent[b], 16 * t)
                        for k in range(4):
                            src = r[:, bass.ds(4 * t + (b * PER + k), 1)].rearrange("p a d -> p (a d)")
                            ins = nc.vector.tensor_scalar(xn[b][:, k], src, mean[b][:, k:k + 1], rstd[b][:, k:k + 1],
                                                          ALU.subtract, ALU.mult)
                        ins.then_inc(n_done[b], 1)
                    if router is not None:
                        for b in range(B):
                            dve.wait_ge(l_ps[b], t + 1)
                            nc.vector.tensor_copy(logits[:, group(t, b)], psL[b][:, :, 0:E]).then_inc(sent[b], 1)

            @block.scalar
            def _(act):
                with act.Fori(0, PER // 4) as t:
                    for b in range(B):
                        act.wait_ge(step[b], 4 * t + 4)
                        act.wait_ge(l_done[b], t)
                        act.activation(sd[b][:, :], ve[b][:, :], ACT.Sqrt).then_inc(rooted[b], 1)
                    if router is not None:
                        for b in range(B):
                            act.wait_ge(t_ps[b], t + 1)
                            act.activation(xs[b][:, :, :].rearrange("p k l -> p (k l)"), psT[b][:, :], ACT.Copy).then_inc(t_sb[b], 1)
                            act.activation(xT[:, bass.ds(512 * t + b * L, 512)], psT[b][:, :], ACT.Copy).then_inc(t_out[b], 1)

            if router is None:
                @block.sync
                def _(sp):
                    out = io["out"].rearrange("b (t k p) d -> p b t k d", p=P, k=4)
                    with sp.Fori(0, PER // 4) as t:
                        for b in range(B):
                            sp.wait_ge(n_done[b], t + 1)
                            sp.dma_start(out[:, b, bass.ds(t, 1)].rearrange("p a k d -> p (a k) d"), xn[b][:, :, :])\
                                .then_inc(sent[b], 16)
                    for b in range(B):
                        sp.wait_ge(sent[b], 16 * (PER // 4))
            else:
                @block.sync
                def _(sp):
                    sp.wait_ge(padded, 1)
                    sp.dma_start(wr[:, 0:E], router[:, :]).then_inc(w_in, 16)

                @block.gpsimd
                def _(pool):
                    pool.memset(wr[:, :], 0.0).then_inc(padded, 1)
                    with pool.Fori(0, PER // 4) as t:
                        for b in range(B):
                            pool.wait_ge(n_done[b], t + 1)
                            pool.tensor_copy(x[:, group(t, b)], xn[b][:, :, :]).then_inc(copied[b], 1)

                @block.tensor
                def _(pe):
                    pe.wait_ge(w_in, 16)
                    with pe.Fori(0, PER // 4) as t:
                        for b in range(B):
                            pe.wait_ge(t_out[b], t)
                            pe.wait_ge(n_done[b], t + 1)
                            for k in range(4):
                                mm = nc.tensor.transpose(psT[b][:, k * P:(k + 1) * P], xn[b][:, k], ident[:, :])
                            mm.then_inc(t_ps[b], 1)
                        for b in range(B):
                            pe.wait_ge(sent[b], t)
                            pe.wait_ge(t_sb[b], t + 1)
                            for k in range(4):
                                mm = nc.tensor.matmul(psL[b][:, k], xs[b][:, k], wr[:, :], start=True, stop=True)
                            mm.then_inc(l_ps[b], 1)


def stage_route(nc, io, sb, tag, top2, bias=None, b2=None):
    with ExitStack() as st:
        def tmp(name, shp):
            return st.enter_context(nc.sbuf_tensor(f"{tag}_{name}", shp, F32))

        def sem(name):
            return take(nc, f"{tag}_{name}")

        lg, coef, x, r, ident = sb["logits"], sb["coef"], sb["x"], sb["r"], sb["ident"]
        rank, eq = tmp("rank", [P, E]), tmp("eq", [P, BLOCKS, E])
        sel = [tmp(f"sel{i}", [P, BLOCKS, E]) for i in range(2)]
        top = [tmp(f"top{i}", [P, BLOCKS]) for i in range(2)]
        key, ex, den = tmp("key", [P, BLOCKS]), tmp("ex", [P, BLOCKS, E]), tmp("den", [P, BLOCKS])
        step, exped, ready, w_in, c_done, g_step = (sem(n) for n in ("step", "exped", "ready", "w_in", "c_done", "g_step"))
        br = tmp("br", [P, E]) if bias is not None else None
        if b2 is not None:
            b2r, b2x = tmp("b2r", [P, D]), tmp("b2x", [P, PER, D])
            mine = tmp("mine", [P, PER])
            cT = [tmp(f"cT{b}", [P, P]) for b in range(B)]
            psC = [st.enter_context(nc.psum_tensor(f"{tag}_psC{b}", [P, 512], F32)) for b in range(B)]
            psB = [st.enter_context(nc.psum_tensor(f"{tag}_psB{i}", [P, 4, D], F32)) for i in range(4)]
            t_ps, t_sb, b_ps, b_done = (sem(n) for n in ("t_ps", "t_sb", "b_ps", "b_done"))

        with nc.Block() as block:
            @block.gpsimd
            def _(pool):
                for e in range(E):
                    ins = pool.memset(rank[:, e:e + 1], float(E - e))
                ins.then_inc(ready, 1)
                if b2 is not None:
                    pool.memset(mine[:, :], 1.0).then_inc(g_step, 1)
                    for n, (base, pattern, mult) in enumerate(((0, [[-E, PER]], 1), (E - 1, [[E, PER]], -1))):
                        pool.wait_ge(g_step, n + 1)
                        pool.affine_select(out=mine[:, :], in_=mine[:, :], compare_op=ALU.is_ge, fill=0.0, base=base,
                                           pattern=pattern, channel_multiplier=mult).then_inc(g_step, 1)
                    pool.wait_ge(g_step, 3)
                    pool.wait_ge(w_in, 16)
                    pool.tensor_tensor(b2x[:, :, :], b2r[:, :].unsqueeze(1).broadcast_to([P, PER, D]), spread(mine[:, :], D),
                                       ALU.mult).then_inc(ready, 1)

            @block.sync
            def _(sp):
                if bias is not None:
                    sp.dma_start(br[:, :], bias.rearrange("(a e) -> a e", a=1).broadcast_to([P, E])).then_inc(w_in, 16)
                if b2 is not None:
                    sp.dma_start(b2r[:, :], b2.unsqueeze(0).broadcast_to([PER, E, D])).then_inc(w_in, 16)

            @block.scalar
            def _(act):
                if top2:
                    act.wait_ge(step, 9)
                    act.activation(den[:, :], key[:, :], ACT.Exp).then_inc(exped, 1)
                else:
                    act.wait_ge(step, 5)
                    act.activation(ex[:, :, :], ex[:, :, :], ACT.Exp).then_inc(exped, 1)
                if b2 is not None:
                    for b in range(B):
                        act.wait_ge(t_ps, b + 1)
                        act.activation(cT[b][:, :], psC[b][:, 0:P], ACT.Copy).then_inc(t_sb, 1)

            @block.vector
            def _(dve):
                count = 0

                def link(ins):
                    nonlocal count
                    count += 1
                    ins.then_inc(step, 1)
                    dve.wait_ge(step, count)

                def choose(i):
                    link(nc.vector.tensor_reduce(top[i][:, :], lg[:, :, :], AX.X, ALU.max))
                    link(nc.vector.tensor_tensor(eq[:, :, :], lg[:, :, :], spread(top[i][:, :], E), ALU.is_equal))
                    link(nc.vector.tensor_tensor(eq[:, :, :], eq[:, :, :], rank[:, :].unsqueeze(1).broadcast_to([P, BLOCKS, E]), ALU.mult))
                    link(nc.vector.tensor_reduce(key[:, :], eq[:, :, :], AX.X, ALU.max))

                dve.wait_ge(ready, 1)
                if bias is not None:
                    dve.wait_ge(w_in, 16)
                    nc.vector.tensor_tensor(lg[:, :, :], lg[:, :, :], br[:, :].unsqueeze(1).broadcast_to([P, BLOCKS, E]),
                                            ALU.add).then_inc(exped, 1)
                    dve.wait_ge(exped, 1)
                choose(0)
                if top2:
                    nc.vector.tensor_tensor(sel[0][:, :, :], eq[:, :, :], spread(key[:, :], E), ALU.is_equal).then_inc(c_done, 1)
                    dve.wait_ge(c_done, 1)
                    nc.vector.scalar_tensor_tensor(lg[:, :, :], sel[0][:, :, :], -3.0e38, lg[:, :, :], ALU.mult, ALU.add).then_inc(c_done, 1)
                    dve.wait_ge(c_done, 2)
                    choose(1)
                    nc.vector.tensor_tensor(sel[1][:, :, :], eq[:, :, :], spread(key[:, :], E), ALU.is_equal).then_inc(c_done, 1)
                    dve.wait_ge(c_done, 3)
                    link(nc.vector.tensor_tensor(key[:, :], top[1][:, :], top[0][:, :], ALU.subtract))
                    dve.wait_ge(exped, 2)
                    link(nc.vector.tensor_scalar(top[0][:, :], den[:, :], 1.0, None, ALU.add))
                    link(nc.vector.reciprocal(top[0][:, :], top[0][:, :]))
                    link(nc.vector.tensor_tensor(top[1][:, :], den[:, :], top[0][:, :], ALU.mult))
                    nc.vector.tensor_tensor(sel[0][:, :, :], sel[0][:, :, :], spread(top[0][:, :], E), ALU.mult)
                    link(nc.vector.tensor_tensor(sel[1][:, :, :], sel[1][:, :, :], spread(top[1][:, :], E), ALU.mult))
                    link(nc.vector.tensor_tensor(coef[:, :, :], sel[0][:, :, :], sel[1][:, :, :], ALU.add))
                else:
                    link(nc.vector.tensor_tensor(ex[:, :, :], lg[:, :, :], spread(top[0][:, :], E), ALU.subtract))
                    nc.vector.tensor_tensor(sel[0][:, :, :], eq[:, :, :], spread(key[:, :], E), ALU.is_equal)
                    dve.wait_ge(exped, 1)
                    link(nc.vector.tensor_reduce(den[:, :], ex[:, :, :], AX.X, ALU.add))
                    link(nc.vector.reciprocal(den[:, :], den[:, :]))
                    nc.vector.tensor_tensor(coef[:, :, :], sel[0][:, :, :], spread(den[:, :], E), ALU.mult).then_inc(c_done, 1)
                if b2 is not None:
                    for n in range(BLOCKS // 4):
                        dve.wait_ge(b_ps, n + 1)
                        nc.vector.tensor_tensor(r[:, 4 * n:4 * n + 4], psB[n % 4][:, :, :], x[:, 4 * n:4 * n + 4], ALU.add)\
                            .then_inc(b_done, 1)

            if b2 is not None:
                @block.tensor
                def _(pe):
                    pe.wait_ge(c_done, 1)
                    for b in range(B):
                        nc.tensor.transpose(psC[b][:, 0:P], coef[:, b * PER:(b + 1) * PER].rearrange("p n e -> p (n e)"), ident[:, :])\
                            .then_inc(t_ps, 1)
                    pe.wait_ge(ready, 2)
                    for n in range(BLOCKS // 4):
                        b, k = divmod(n, PER // 4)
                        pe.wait_ge(t_sb, b + 1)
                        if n >= 4:
                            pe.wait_ge(b_done, n - 3)
                        for j in range(4):
                            mm = nc.tensor.matmul(psB[n % 4][:, j], cT[b][:, :], b2x[:, 4 * k + j], start=True, stop=True)
                        mm.then_inc(b_ps, 1)


def stage_experts(nc, io, sb, tag, gated, w1, w2, b1=None, w3=None):
    F = w1.shape[2]
    NF = F // P
    UP = 2 * NF if gated else NF
    GROUPS = B * L // 512
    with ExitStack() as st:
        def tmp(name, shp):
            return st.enter_context(nc.sbuf_tensor(f"{tag}_{name}", shp, F32))

        def sem(name):
            return take(nc, f"{tag}_{name}")

        xT, coef, r, base, ident = sb["xT"], sb["coef"], sb["r"], sb["r"] if not gated else sb["x"], sb["ident"]
        wa = tmp("wa", [D, E, F])
        wc = tmp("wc", [D, E, F]) if gated else None
        wb = tmp("wb", [P, E, NF, D])
        hT = [tmp(f"hT{i}", [P, NF, 512]) for i in range(2)]
        acc = tmp("acc", [P, 4, D])
        psH = [st.enter_context(nc.psum_tensor(f"{tag}_psH{i}", [P, 512], F32)) for i in range(UP)]
        psY = [st.enter_context(nc.psum_tensor(f"{tag}_psY{i}", [P, 4, D], F32)) for i in range(2)]
        w_in, b_in, b_ps, b_sb = sem("w_in"), sem("b_in"), sem("b_ps"), sem("b_sb")
        h_ps, h_act, h_done, y_ps, a_done = (sem(n) for n in ("h_ps", "h_act", "h_done", "y_ps", "a_done"))
        if gated:
            sg = [tmp(f"sg{i}", [P, NF, 512]) for i in range(2)]
        else:
            b1s, b1T = tmp("b1s", [E * NF, P]), tmp("b1T", [P, E * NF])
            psb = st.enter_context(nc.psum_tensor(f"{tag}_psb", [P, 512], F32))

        with nc.Block() as block:
            @block.sync
            def _(sp):
                if not gated:
                    sp.dma_start(b1s[:, :], b1.rearrange("e (f p) -> (e f) p", p=P)).then_inc(b_in, 16)
                for e in range(E):
                    sp.dma_start(wa[:, e], w1[e]).then_inc(w_in, 16)
                    if gated:
                        sp.dma_start(wc[:, e], w3[e]).then_inc(w_in, 16)
                    sp.dma_start(wb[:, e], w2[e].rearrange("(f p) d -> p f d", p=P)).then_inc(w_in, 16)

            @block.tensor
            def _(pe):
                if not gated:
                    pe.wait_ge(b_in, 16)
                    nc.tensor.transpose(psb[:, 0:E * NF], b1s[:, :], ident[0:E * NF, 0:E * NF]).then_inc(b_ps, 1)
                pe.wait_ge(w_in, 16 * E * (3 if gated else 2))
                with pe.Fori(0, GROUPS) as g:
                    def up(e):
                        for f in range(UP):
                            if e > 0:
                                pe.wait_ge(h_done, g * (E * NF) + (e - 1) * NF + f % NF + 1)
                            w = wc if f >= NF else wa
                            nc.tensor.matmul(psH[f][:, :], w[:, e, (f % NF) * P:(f % NF + 1) * P], xT[:, bass.ds(512 * g, 512)],
                                             start=True, stop=True).then_inc(h_ps, 1)

                    up(0)
                    for e in range(E):
                        if e + 1 < E:
                            up(e + 1)
                        pe.wait_ge(h_done, g * (E * NF) + (e + 1) * NF)
                        pe.wait_ge(a_done, g * E + max(e - 1, 0))
                        for k in range(4):
                            for f in range(NF):
                                mm = nc.tensor.matmul(psY[e % 2][:, k], hT[e % 2][:, f, k * P:(k + 1) * P], wb[:, e, f],
                                                      start=(f == 0), stop=(f == NF - 1))
                        mm.then_inc(y_ps, 1)

            @block.scalar
            def _(act):
                if not gated:
                    act.wait_ge(b_ps, 1)
                    act.activation(b1T[:, :], psb[:, 0:E * NF], ACT.Copy).then_inc(b_sb, 1)
                    act.wait_ge(b_sb, 1)
                with act.Fori(0, GROUPS) as g:
                    for e in range(E):
                        act.wait_ge(y_ps, g * E + max(e - 1, 0))
                        for f in range(NF):
                            act.wait_ge(h_ps, (g * E + e) * UP + f + 1)
                            if gated:
                                act.activation(sg[e % 2][:, f], psH[f][:, :], ACT.Silu).then_inc(h_act, 1)
                            else:
                                act.activation(hT[e % 2][:, f], psH[f][:, :], ACT.Gelu, bias=b1T[:, e * NF + f:e * NF + f + 1])\
                                    .then_inc(h_done, 1)

            @block.vector
            def _(dve):
                with dve.Fori(0, GROUPS) as g:
                    for e in range(E):
                        if gated:
                            for f in range(NF):
                                dve.wait_ge(h_act, (g * E + e) * NF + f + 1)
                                dve.wait_ge(h_ps, (g * E + e) * UP + NF + f + 1)
                                nc.vector.tensor_tensor(hT[e % 2][:, f], sg[e % 2][:, f], psH[NF + f][:, :], ALU.mult).then_inc(h_done, 1)
                        dve.wait_ge(y_ps, g * E + e + 1)
                        dve.wait_ge(a_done, g * E + e)
                        for k in range(4):
                            at = bass.ds(4 * g + k, 1)
                            so_far = base[:, at].rearrange("p a d -> p (a d)") if e == 0 else acc[:, k]
                            to = r[:, at].rearrange("p a d -> p (a d)") if e == E - 1 else acc[:, k]
                            ins = nc.vector.scalar_tensor_tensor(to, psY[e % 2][:, k], coef[:, at, e], so_far, ALU.mult, ALU.add)
                        ins.then_inc(a_done, 1)


def stage_linear_attention(nc, io, sb):
    NH = 16
    DH = D // NH
    HF = NH // 2 * DH * DH
    with ExitStack() as st:
        def tmp(name, shp):
            return st.enter_context(nc.sbuf_tensor(f"l_{name}", shp, F32))

        def pair(name, shp):
            return [tmp(f"{name}{b}", shp) for b in range(B)]

        def sem(name):
            return take(nc, f"l_{name}")

        def sems(name):
            return [sem(f"{name}{b}") for b in range(B)]

        def bank(name):
            return st.enter_context(nc.psum_tensor(f"l_{name}", [P, 512], F32))

        x, xT, r, ident = sb["x"], sb["xT"], sb["r"], sb["ident"]
        w_raw = tmp("w_raw", [D, 4, D])
        wT = tmp("wT", [D, 4, D])
        b_qkv, b_o = tmp("b_qkv", [P, 3, D]), tmp("b_o", [P, D])
        tri, mask, zero = tmp("tri", [P, P]), tmp("mask", [P, NH, DH]), tmp("zero", [P, P])
        xs, qkv, kv = pair("xs", [P, P]), pair("qkv", [P, 3, D]), pair("kv", [P, 2, HF])
        S, qT, prod = pair("S", [P, NH, DH]), pair("qT", [P, P]), pair("prod", [P, 2, HF])
        intra, out, oT = pair("intra", [P, D]), pair("out", [P, D]), pair("oT", [P, P])
        ps_a, ps_c, ps_s = [bank(f"a{b}") for b in range(B)], [bank(f"c{b}") for b in range(B)], [bank(f"s{b}") for b in range(B)]
        ps_t = st.enter_context(nc.psum_tensor("l_t", [P, 2, 512], F32))
        const, w_in, b_in, w_ps, w_sb, r_init = (sem(n) for n in ("const", "w_in", "b_in", "w_ps", "w_sb", "r_init"))
        (x_in, qkv_ps, qkv_sb, kv_done, t_ps, prod_done, s_ps, s_sb, q_ps, q_sb, c_ps, sum_done, out_done, o_ps, o_sb, y_ps,
         r_done, red_done) = (sems(n) for n in ("x_in", "qkv_ps", "qkv_sb", "kv_done", "t_ps", "prod_done", "s_ps", "s_sb", "q_ps",
                                                "q_sb", "c_ps", "sum_done", "out_done", "o_ps", "o_sb", "y_ps", "r_done", "red_done"))

        def blk(t, b):
            return bass.ds(t + b * PER, 1)

        def flat(ap):
            return ap.rearrange("p a d -> p (a d)")

        with nc.Block() as block:
            @block.sync
            def _(sp):
                for i, n in enumerate(("wq", "wk", "wv", "wo")):
                    sp.dma_start(w_raw[:, i], io[f"L1_{n}_w"][:, :]).then_inc(w_in, 16)
                for i, n in enumerate(("wq", "wk", "wv", "wo")):
                    to = b_qkv[:, i] if i < 3 else b_o[:, :]
                    sp.dma_start(to, io[f"L1_{n}_b"].rearrange("(a e) -> a e", a=1).broadcast_to([P, D])).then_inc(b_in, 16)
                with sp.Fori(0, PER) as t:
                    for b in range(B):
                        sp.wait_ge(qkv_ps[b], t)
                        sp.dma_start(xs[b][:, :], xT[:, bass.ds(P * t + b * L, P)]).then_inc(x_in[b], 16)

            @block.gpsimd
            def _(pool):
                pool.memset(zero[:, :], 0.0).then_inc(const, 1)
                pool.memset(tri[:, :], 1.0).then_inc(const, 1)
                pool.memset(mask[:, :, :], 1.0).then_inc(const, 1)
                for b in range(B):
                    pool.memset(S[b][:, :, :], 0.0).then_inc(const, 1)
                n = 3 + B
                for ap, base, pattern, mult in ((tri[:, :], 0, [[1, P]], -1), (mask[:, :, :], 0, [[-DH, NH], [0, DH]], 1),
                                                (mask[:, :, :], DH - 1, [[DH, NH], [0, DH]], -1)):
                    pool.wait_ge(const, n)
                    pool.affine_select(out=ap, in_=ap, compare_op=ALU.is_ge, fill=0.0, base=base, pattern=pattern,
                                       channel_multiplier=mult).then_inc(const, 1)
                    n += 1
                with pool.Fori(0, PER) as t:
                    for b in range(B):
                        pool.wait_ge(qkv_sb[b], t + 1)
                        pool.wait_ge(t_ps[b], t)
                        for i in range(2):
                            hs = slice(i * D // 2, (i + 1) * D // 2)
                            k = qkv[b][:, 1, hs].rearrange("p (h c) -> p h c", c=DH)
                            v = qkv[b][:, 2, hs].rearrange("p (h c) -> p h c", c=DH)
                            ins = pool.tensor_tensor(kv[b][:, i].rearrange("p (h e d) -> p h e d", e=DH, d=DH),
                                                     k.unsqueeze(2).broadcast_to([P, NH // 2, DH, DH]), spread(v, DH), ALU.mult)
                        ins.then_inc(kv_done[b], 1)

            @block.tensor
            def _(pe):
                pe.wait_ge(const, 6 + B)
                pe.wait_ge(w_in, 64)
                for i in range(4):
                    mm = nc.tensor.transpose(ps_a[0][:, i * D:(i + 1) * D], w_raw[:, i], ident[:, :])
                mm.then_inc(w_ps, 1)
                for b in range(B):
                    nc.tensor.matmul(ps_s[b][:, 0:D], zero[:, :], zero[:, :], start=True, stop=True)
                pe.wait_ge(w_sb, 1)
                with pe.Fori(0, PER) as t:
                    for b in range(B):
                        pe.wait_ge(x_in[b], 16 * t + 16)
                        pe.wait_ge(o_sb[b], t)
                        nc.tensor.matmul(ps_a[b][:, 0:3 * D], xs[b][:, :], wT[:, 0:3].rearrange("p a e -> p (a e)"),
                                         start=True, stop=True).then_inc(qkv_ps[b], 1)
                    for b in range(B):
                        pe.wait_ge(qkv_sb[b], t + 1)
                        nc.tensor.transpose(ps_a[b][:, 0:P], qkv[b][:, 0], ident[:, :]).then_inc(q_ps[b], 1)
                    for b in range(B):
                        pe.wait_ge(kv_done[b], t + 1)
                        if b == 0:
                            pe.wait_ge(prod_done[1], t)
                        else:
                            pe.wait_ge(prod_done[0], t + 1)
                        for i in range(2):
                            mm = nc.tensor.matmul(ps_t[:, i], tri[:, :], kv[b][:, i], start=True, stop=True)
                        mm.then_inc(t_ps[b], 1)
                        pe.wait_ge(q_sb[b], t + 1)
                        pe.wait_ge(r_done[b], t)
                        nc.tensor.matmul(ps_c[b][:, 0:D], qT[b][:, :], S[b][:, :, :].rearrange("p h c -> p (h c)"),
                                         start=True, stop=True).then_inc(c_ps[b], 1)
                        pe.wait_ge(s_sb[b], t)
                        nc.tensor.matmul(ps_s[b][:, 0:D], qkv[b][:, 1], qkv[b][:, 2], start=False, stop=True,
                                         skip_group_check=True).then_inc(s_ps[b], 1)
                    for b in range(B):
                        pe.wait_ge(out_done[b], t + 1)
                        nc.tensor.transpose(ps_a[b][:, 0:P], out[b][:, :], ident[:, :]).then_inc(o_ps[b], 1)
                    for b in range(B):
                        pe.wait_ge(o_sb[b], t + 1)
                        nc.tensor.matmul(ps_c[b][:, 0:D], oT[b][:, :], wT[:, 3], start=True, stop=True).then_inc(y_ps[b], 1)

            @block.scalar
            def _(act):
                act.wait_ge(w_ps, 1)
                act.activation(wT[:, :, :].rearrange("p a e -> p (a e)"), ps_a[0][:, :], ACT.Copy).then_inc(w_sb, 1)
                with act.Fori(0, PER) as t:
                    for b in range(B):
                        act.wait_ge(q_ps[b], t + 1)
                        act.activation(qT[b][:, :], ps_a[b][:, 0:P], ACT.Copy).then_inc(q_sb[b], 1)
                    for b in range(B):
                        act.wait_ge(o_ps[b], t + 1)
                        act.activation(oT[b][:, :], ps_a[b][:, 0:P], ACT.Copy).then_inc(o_sb[b], 1)

            @block.vector
            def _(dve):
                dve.wait_ge(b_in, 64)
                dve.wait_ge(const, 6 + B)
                for b in range(B):
                    s = slice(b * PER, (b + 1) * PER)
                    nc.vector.tensor_tensor(r[:, s], x[:, s], b_o[:, :].unsqueeze(1).broadcast_to([P, PER, D]), ALU.add)\
                        .then_inc(r_init, 1)
                dve.wait_ge(r_init, B)
                with dve.Fori(0, PER) as t:
                    for b in range(B):
                        dve.wait_ge(qkv_ps[b], t + 1)
                        dve.wait_ge(kv_done[b], t)
                        nc.vector.tensor_tensor(qkv[b][:, :, :], ps_a[b][:, 0:3 * D].rearrange("p (a e) -> p a e", a=3),
                                                b_qkv[:, :, :], ALU.add).then_inc(qkv_sb[b], 1)
                    for b in range(B):
                        dve.wait_ge(t_ps[b], t + 1)
                        for i in range(2):
                            q = qkv[b][:, 0, i * D // 2:(i + 1) * D // 2].rearrange("p (h c) -> p h c", c=DH)
                            ins = nc.vector.tensor_tensor(prod[b][:, i].rearrange("p (h e d) -> p h e d", e=DH, d=DH),
                                                          ps_t[:, i].rearrange("p (h e d) -> p h e d", e=DH, d=DH),
                                                          q.unsqueeze(2).broadcast_to([P, NH // 2, DH, DH]), ALU.mult)
                        ins.then_inc(prod_done[b], 1)
                        dve.wait_ge(s_ps[b], t + 1)
                        dve.wait_ge(c_ps[b], t + 1)
                        nc.vector.tensor_tensor(S[b][:, :, :], ps_s[b][:, 0:D].rearrange("p (h c) -> p h c", c=DH), mask[:, :, :],
                                                ALU.mult).then_inc(s_sb[b], 1)
                        dve.wait_ge(prod_done[b], t + 1)
                        nc.vector.tensor_reduce(intra[b][:, :], prod[b][:, :, :].rearrange("p i (g d) -> p (i g) d", d=DH), AX.X,
                                                ALU.add).then_inc(red_done[b], 1)
                    for b in range(B):
                        dve.wait_ge(red_done[b], t + 1)
                        nc.vector.tensor_tensor(out[b][:, :], intra[b][:, :], ps_c[b][:, 0:D], ALU.add).then_inc(out_done[b], 1)
                    for b in range(B):
                        dve.wait_ge(y_ps[b], t + 1)
                        nc.vector.tensor_tensor(flat(r[:, blk(t, b)]), flat(r[:, blk(t, b)]), ps_c[b][:, 0:D], ALU.add)\
                            .then_inc(r_done[b], 1)


_INS = ["L0_attn_hidden_states", "L0_attn_conv_w", "L0_attn_Wq", "L0_attn_Wk", "L0_attn_Wv", "L0_attn_Wb", "L0_attn_Wg",
        "L0_attn_norm_w", "L0_attn_Wo", "L0_ffn_gate_w", "L0_ffn_w1", "L0_ffn_b1", "L0_ffn_w2", "L0_ffn_b2",
        "L1_attn_wq_w", "L1_attn_wq_b", "L1_attn_wk_w", "L1_attn_wk_b", "L1_attn_wv_w", "L1_attn_wv_b",
        "L1_attn_wo_w", "L1_attn_wo_b", "L1_ffn_Wr", "L1_ffn_br", "L1_ffn_W1", "L1_ffn_W3", "L1_ffn_W2"]


def build(nc, io):
    TAKEN.clear()
    io["kb_dram"] = nc.dram_tensor("kb_dram", [B * L, QK + H], F32, kind="Internal").ap()
    io["t_dram"] = nc.dram_tensor("t_dram", [B * L, H * SUB], F32, kind="Internal").ap()
    with ExitStack() as ctx:
        def keep(name, shp):
            return ctx.enter_context(nc.sbuf_tensor(name, shp, F32))

        sb = {"ident": keep("ident", [P, P]), "r": keep("r", [P, BLOCKS, D])}
        with ExitStack() as delta:
            def held(name, shp):
                return delta.enter_context(nc.sbuf_tensor(name, shp, F32))

            sb["tok"] = held("tok", [P, BLOCKS, TOKW])
            sb["gate"] = held("gate", [P, BLOCKS, D])
            sb["kp"] = held("kp", [P, CH, QK + H])
            stage_project(nc, io, sb, delta)
            if LAST_STAGE >= 2:
                sb["tinv"] = held("tinv", [P, BLOCKS, H * SUB])
                stage_invert(nc, io, sb, delta)
            if LAST_STAGE >= 3:
                sb["o"] = held("o", [P, BLOCKS, D])
                stage_delta(nc, io, sb, delta)
            if LAST_STAGE >= 4:
                stage_close_delta(nc, io, sb, delta)
        give_back(nc)
        if LAST_STAGE >= 5:
            sb["x"], sb["xT"] = keep("x", [P, BLOCKS, D]), keep("xT_all", [D, B * L])
            sb["logits"] = keep("logits", [P, BLOCKS, E])
            stage_norm(nc, io, sb, "n0", io["L0_ffn_gate_w"])
        if LAST_STAGE >= 6:
            sb["coef"] = keep("coef", [P, BLOCKS, E])
            stage_route(nc, io, sb, "g0", False, b2=io["L0_ffn_b2"])
            stage_experts(nc, io, sb, "e0", False, io["L0_ffn_w1"], io["L0_ffn_w2"], b1=io["L0_ffn_b1"])
        if LAST_STAGE >= 7:
            stage_norm(nc, io, sb, "n1", io["L1_ffn_Wr"])
        give_back(nc)
        if LAST_STAGE >= 8:
            stage_linear_attention(nc, io, sb)
        if LAST_STAGE >= 9:
            stage_norm(nc, io, sb, "n2", io["L1_ffn_Wr"])
        if LAST_STAGE >= 10:
            stage_route(nc, io, sb, "g1", True, bias=io["L1_ffn_br"])
            stage_experts(nc, io, sb, "e1", True, io["L1_ffn_W1"], io["L1_ffn_W2"], w3=io["L1_ffn_W3"])
        if LAST_STAGE >= 11:
            stage_norm(nc, io, sb, "n3")


LAST_STAGE = 99


def kernel(**inputs):
    import numpy as _np
    import concourse.bacc as _bacc
    from concourse.bass_utils import run_bass_kernel_spmd as _run

    nc = _bacc.Bacc("TRN2", target_bir_lowering=False, num_devices=1)
    arrays, io = {}, {}
    for name in _INS:
        a = _np.ascontiguousarray(inputs[name])
        arrays[f"in_{name}"] = a
        short = name.replace("_attn_", "_").replace("L0_hidden_states", "x")
        io[short] = nc.dram_tensor(f"in_{name}", a.shape, mybir.dt.from_np(a.dtype), kind="ExternalInput").ap()
    io["out"] = nc.dram_tensor("out_0", (B, L, D), F32, kind="ExternalOutput").ap()
    build(nc, io)
    r = _run(nc, [arrays], core_ids=[0])
    return r.results[0]["out_0"]
```

```python
from contextlib import ExitStack

import concourse.bass as bass
from concourse import mybir

F32 = mybir.dt.float32
U32 = mybir.dt.uint32
I32 = mybir.dt.int32
ALU = mybir.AluOpType
ACT = mybir.ActivationFunctionType
AX = mybir.AxisListType

P = 128
B, L, D = 2, 2048, 128
BLOCKS = B * L // P
PER = BLOCKS // B
H, DK, DV = 4, 16, 32
QK = H * DK
CH = 32
SUB = 16
NC = P // CH
KC = 3
WID = 2 * QK + 2 * D + H

RW = DV + DK
C_R, C_K = 0, H * RW
C_B, C_Q, C_KB = C_K + QK, C_K + QK + H, C_K + 2 * QK + H
TOKW = C_KB + QK
E = 8
EPS = 1e-5
YW = H * RW + P - RW


def spread(ap, n):
    return ap.unsqueeze(len(ap.shape)).broadcast_to([*ap.shape, n])


TAKEN = []


def take(nc, name):
    TAKEN.append(nc.alloc_semaphore(name))
    return TAKEN[-1]


def give_back(nc):
    with nc.Block() as block:
        @block.gpsimd
        def _(pool):
            nc.clear_and_free_semaphores(TAKEN)
    TAKEN.clear()


def kq_rows(tok, at):
    return tok[:, at, C_K:C_K + 2 * (QK + H)].rearrange("p n (a c) -> p n a c", a=2)[:, :, :, 0:QK]


def stage_project(nc, io, sb, ctx):
    with ExitStack() as st:
        def tmp(name, shp):
            return st.enter_context(nc.sbuf_tensor(name, shp, F32))

        def sem(name):
            return take(nc, name)

        xst = tmp("xst", [P, B, 4, D])
        xT = tmp("xT", [D, B, KC + L])
        conv = tmp("conv", [D, B, 512])
        hT = tmp("hT", [D, B, 512])
        wall = tmp("wall", [D, WID])
        cw = tmp("cw", [D, KC + 1])
        sq = tmp("sq", [P, 2, 2, 2 * QK])
        n2 = tmp("n2", [P, BLOCKS, 2 * H])
        rn = tmp("rn", [P, BLOCKS, 2 * H])
        bl = tmp("bl", [P, BLOCKS, H])
        th = tmp("th", [P, BLOCKS, H])
        psT = [st.enter_context(nc.psum_tensor(f"p_psT{b}", [P, 512], F32)) for b in range(B)]
        psG = [st.enter_context(nc.psum_tensor(f"p_psG{b}", [P, 4, D], F32)) for b in range(B)]
        psP = [st.enter_context(nc.psum_tensor(f"p_psP{i}", [P, 2, 512], F32)) for i in range(2)]

        w_in, x_in, const = sem("w_in"), [sem(f"x_in{b}") for b in range(B)], sem("p_const")
        xT_ps, xT_sb, x_used = sem("xT_ps"), sem("xT_sb"), sem("x_used")
        conv_do, conv_done, h_done = sem("conv_do"), sem("conv_done"), sem("h_done")
        proj, gate_ps, sq_done, gate_done, kq_done, qkv_done, n2_done = (
            sem(n) for n in ("proj", "gate_ps", "sq_done", "gate_done", "kq_done", "qkv_done", "n2_done"))
        v_step, a_step, g_step, stored = sem("pv_step"), sem("pa_step"), sem("pg_step"), sem("p_stored")

        x_dram = io["x"].rearrange("b (t k p) d -> p b t k d", p=P, k=4)
        tok, gate, ident = sb["tok"], sb["gate"], sb["ident"]

        with nc.Block() as block:
            @block.sync
            def _(sp):
                for n, c in (("L0_Wk", 0), ("L0_Wq", QK), ("L0_Wv", 2 * QK), ("L0_Wb", 2 * QK + D), ("L0_Wg", 2 * QK + D + H)):
                    sp.dma_start(wall[:, c:c + io[n].shape[1]], io[n][:, :]).then_inc(w_in, 16)
                sp.dma_start(cw[:, :], io["L0_conv_w"][:, :]).then_inc(w_in, 16)
                for b in range(B):
                    sp.dma_start(xst[:, b], x_dram[:, b, 0]).then_inc(x_in[b], 16)
                with sp.Fori(1, PER // 4) as t:
                    for b in range(B):
                        sp.wait_ge(xT_ps, 2 * t - 1 + b)
                        sp.dma_start(xst[:, b], x_dram[:, b, bass.ds(t, 1)].rearrange("p a k d -> p (a k) d")).then_inc(x_in[b], 16)
                sp.wait_ge(v_step, 4)
                sp.dma_start(io["kb_dram"].rearrange("(n p) c -> p n c", p=P), tok[:, :, C_K:C_K + QK + H]).then_inc(stored, 16)
                sp.wait_ge(stored, 16)
                sp.dma_start(sb["kp"][:, :, :], io["kb_dram"].rearrange("(p i) c -> p i c", i=CH)).then_inc(stored, 16)
                sp.wait_ge(stored, 32)

            @block.gpsimd
            def _(pool):
                pool.memset(ident[:, :], 0.0).then_inc(g_step, 1)
                pool.wait_ge(g_step, 1)
                pool.affine_select(out=ident[:, :], in_=ident[:, :], compare_op=ALU.not_equal, fill=1.0,
                                   base=0, pattern=[[-1, P]], channel_multiplier=1).then_inc(const, 1)
                pool.memset(xT[:, :, 0:KC], 0.0).then_inc(const, 1)
                pool.wait_ge(v_step, 4)
                for b in range(B):
                    s = slice(b * PER, (b + 1) * PER)
                    r = tok[:, s, C_R:C_R + H * RW].rearrange("p n (h c) -> p n h c", h=H)
                    pool.tensor_tensor(r[:, :, :, 0:DV], r[:, :, :, 0:DV],
                                       spread(tok[:, s, C_B:C_B + H], DV), ALU.mult).then_inc(g_step, 1)

            @block.tensor
            def _(pe):
                pe.wait_ge(const, 2)
                pe.wait_ge(w_in, 16 * 6)
                with pe.Fori(0, PER // 4) as t:
                    for b in range(B):
                        pe.wait_ge(x_in[b], t * 16 + 16)
                        pe.wait_ge(xT_sb, 2 * t + b)
                        for k in range(4):
                            mm = nc.tensor.transpose(psT[b][:, k * P:(k + 1) * P], xst[:, b, k], ident[:, :])
                        mm.then_inc(xT_ps, 1)
                    for b in range(B):
                        pe.wait_ge(h_done, 2 * t + b + 1)
                        pe.wait_ge(gate_done, 2 * t + b)
                        for k in range(4):
                            mm = nc.tensor.matmul(psG[b][:, k], hT[:, b, k * P:(k + 1) * P], wall[:, WID - D:WID],
                                                  start=True, stop=True)
                        mm.then_inc(gate_ps, 1)
                        for half in range(2):
                            pe.wait_ge(qkv_done, 4 * t + 2 * b + half)
                            for j in range(2):
                                k = 2 * half + j
                                mm = nc.tensor.matmul(psP[half][:, j, 0:WID - D], hT[:, b, k * P:(k + 1) * P],
                                                      wall[:, 0:WID - D], start=True, stop=True)
                            mm.then_inc(proj, 1)

            @block.scalar
            def _(act):
                with act.Fori(0, PER // 4) as t:
                    for b in range(B):
                        act.wait_ge(xT_ps, 2 * t + b + 1)
                        act.activation(xT[:, b, bass.ds(t * 512 + KC, 512)], psT[b][:, :], ACT.Copy).then_inc(xT_sb, 1)
                    for b in range(B):
                        act.wait_ge(conv_done, 2 * t + b + 1)
                        act.activation(hT[:, b], conv[:, b], ACT.Silu).then_inc(h_done, 1)
                        act.wait_ge(gate_ps, 2 * t + b + 1)
                        act.activation(gate[:, bass.ds(4 * t + b * PER, 4)], psG[b][:, :, :], ACT.Silu).then_inc(gate_done, 1)
                        for half in range(2):
                            act.wait_ge(kq_done, 4 * t + 2 * b + half + 1)
                            act.wait_ge(n2_done, 4 * t + 2 * b + half)
                            act.activation(sq[:, half].rearrange("p n (a c) -> p n a c", a=2),
                                           kq_rows(tok, bass.ds(4 * t + (b * PER + 2 * half), 2)), ACT.Square).then_inc(sq_done, 1)
                act.wait_ge(qkv_done, BLOCKS // 2)
                act.activation(th[:, :, :], bl[:, :, :], ACT.Tanh, scale=0.5).then_inc(a_step, 1)
                act.wait_ge(v_step, 1)
                act.activation(rn[:, :, :], n2[:, :, :], ACT.Sqrt).then_inc(a_step, 1)

            @block.vector
            def _(dve):
                dve.wait_ge(w_in, 16 * 6)
                dve.wait_ge(const, 2)
                with dve.Fori(0, PER // 4) as t:
                    for b in range(B):
                        dve.wait_ge(xT_sb, 2 * t + b + 1)
                        dve.wait_ge(h_done, 2 * t + b)
                        nc.vector.tensor_scalar(conv[:, b], xT[:, b, bass.ds(t * 512, 512)], cw[:, 0:1], None,
                                                ALU.mult).then_inc(conv_do, 1)
                        for i in range(1, KC + 1):
                            dve.wait_ge(conv_do, (2 * t + b) * KC + i)
                            nc.vector.scalar_tensor_tensor(conv[:, b], xT[:, b, bass.ds(t * 512 + i, 512)], cw[:, i:i + 1],
                                                           conv[:, b], ALU.mult, ALU.add)\
                                .then_inc(conv_do if i < KC else conv_done, 1)
                    for b in range(B):
                        for half in range(2):
                            n = 4 * t + 2 * b + half
                            at = bass.ds(4 * t + (b * PER + 2 * half), 2)
                            dve.wait_ge(proj, n + 1)
                            ps = psP[half]
                            nc.vector.tensor_copy(kq_rows(tok, at), ps[:, :, 0:2 * QK].rearrange("p n (a c) -> p n a c", a=2))\
                                .then_inc(kq_done, 1)
                            r = tok[:, at, C_R:C_R + H * RW].rearrange("p n (h c) -> p n h c", h=H)
                            for j in range(2):
                                nc.vector.tensor_copy(r[:, j, :, 0:DV], ps[:, j, 2 * QK:2 * QK + D].rearrange("p (h c) -> p h c", h=H))
                            nc.vector.tensor_copy(bl[:, at], ps[:, :, 2 * QK + D:WID - D]).then_inc(qkv_done, 1)
                            dve.wait_ge(sq_done, n + 1)
                            nc.vector.tensor_reduce(n2[:, at], sq[:, half].rearrange("p n (h c) -> p (n h) c", c=DK),
                                                    AX.X, ALU.add).then_inc(n2_done, 1)
                dve.wait_ge(n2_done, BLOCKS // 2)
                nc.vector.tensor_scalar(n2[:, :, :], n2[:, :, :], 1e-24, None, ALU.max).then_inc(v_step, 1)
                dve.wait_ge(a_step, 2)
                nc.vector.reciprocal(n2[:, :, :], rn[:, :, :]).then_inc(v_step, 1)
                nc.vector.tensor_scalar(tok[:, :, C_B:C_B + H], th[:, :, :], 0.5, 0.5, ALU.mult, ALU.add)
                dve.wait_ge(v_step, 2)
                for b in range(B):
                    s = slice(b * PER, (b + 1) * PER)
                    k = tok[:, s, C_K:C_K + QK].rearrange("p n (h c) -> p n h c", h=H)
                    last = nc.vector.tensor_tensor(k, k, spread(n2[:, s, 0:H], DK), ALU.mult)
                    last.then_inc(v_step, 1)
                for b in range(B):
                    s = slice(b * PER, (b + 1) * PER)
                    q = tok[:, s, C_Q:C_Q + QK].rearrange("p n (h c) -> p n h c", h=H)
                    nc.vector.tensor_tensor(q, q, spread(n2[:, s, H:2 * H], DK), ALU.mult)
                dve.wait_ge(v_step, 4)
                for b in range(B):
                    s = slice(b * PER, (b + 1) * PER)
                    k = tok[:, s, C_K:C_K + QK].rearrange("p n (h c) -> p n h c", h=H)
                    beta = spread(tok[:, s, C_B:C_B + H], DK)
                    nc.vector.tensor_tensor(tok[:, s, C_KB:C_KB + QK].rearrange("p n (h c) -> p n h c", h=H), k, beta, ALU.mult)
                    r = tok[:, s, C_R:C_R + H * RW].rearrange("p n (h c) -> p n h c", h=H)
                    nc.vector.tensor_tensor(r[:, :, :, DV:RW], k, beta, ALU.mult)


def stage_invert(nc, io, sb, ctx):
    SU = CH // SUB
    with ExitStack() as st:
        def tmp(name, shp):
            return st.enter_context(nc.sbuf_tensor(name, shp, F32))

        def sem(name):
            return take(nc, name)

        kp = sb["kp"]
        kb = tmp("kb", [P, CH, QK])
        prod = [tmp(f"i_prod{i}", [P, SU, SUB, QK]) for i in range(2)]
        nA = tmp("nA", [P, SU, H, SUB, SUB])
        T = tmp("T", [P, SU, H, SUB, SUB])
        nw = tmp("nw", [P, DV])
        TT = tmp("TT", [P, SU, SUB, H, SUB])
        chain, mul_v, mul_g, red, t_ready, stored, fwd, nw_in = (sem(n) for n in (
            "i_chain", "mul_v", "mul_g", "red", "t_ready", "i_stored", "fwd", "nw_in"))
        t_flat, a_flat = (x.rearrange("p c h i j -> p (c h) i j") for x in (T[:, :, :, :, :], nA[:, :, :, :, :]))
        p_flat = prod[0][:, :, :, :].rearrange("p c i f -> p (c i f)")

        def lagged(eng, lag, signal):
            n = SUB - lag
            for c in range(SU):
                i0 = c * SUB
                ins = eng.tensor_tensor(prod[lag % 2][:, c, 0:n], kb[:, i0 + lag:i0 + SUB], kp[:, i0:i0 + n, 0:QK], ALU.mult)
            ins.then_inc(signal, 1)

        with nc.Block() as block:
            @block.gpsimd
            def _(pool):
                pool.memset(T[:, :, :, :, :], 0.0).then_inc(chain, 1)
                pool.wait_ge(chain, 1)
                pool.memset(T[:, :, :, :, :].rearrange("p c h i j -> p (c h) (i j)")[:, :, 0:SUB * SUB:SUB + 1], 1.0).then_inc(chain, 1)
                pool.wait_ge(mul_v, 1)
                for lag in range(2, SUB, 2):
                    if lag > 2:
                        pool.wait_ge(red, lag - 2)
                    lagged(nc.gpsimd, lag, mul_g)
                pool.wait_ge(nw_in, 16)
                for b in range(B):
                    g = sb["gate"][:, b * PER:(b + 1) * PER].rearrange("p n (h c) -> p (n h) c", c=DV)
                    pool.tensor_tensor(g, g, nw[:, :].unsqueeze(1).broadcast_to([P, PER * H, DV]), ALU.mult).then_inc(chain, 1)

            @block.vector
            def _(dve):
                for h in range(H):
                    last = nc.vector.scalar_tensor_tensor(kb[:, :, h * DK:(h + 1) * DK], kp[:, :, h * DK:(h + 1) * DK], -1.0,
                                                          spread(kp[:, :, QK + h], DK), ALU.mult, ALU.mult)
                last.then_inc(mul_v, 1)
                dve.wait_ge(mul_v, 1)
                for lag in range(1, SUB):
                    n = SUB - lag
                    if lag % 2:
                        if lag > 2:
                            dve.wait_ge(red, lag - 2)
                        lagged(nc.vector, lag, mul_v)
                        dve.wait_ge(mul_v, 1 + (lag + 1) // 2)
                    else:
                        dve.wait_ge(mul_g, lag // 2)
                    for c in range(SU):
                        out = nA[:, c].rearrange("p h i j -> p h (i j)")[:, :, lag * SUB:(n + lag - 1) * SUB + n:SUB + 1]
                        ins = nc.vector.tensor_reduce(out.rearrange("p h i -> p i h"),
                                                      prod[lag % 2][:, c, 0:n].rearrange("p i (h d) -> p i h d", h=H), AX.X, ALU.add)
                    ins.then_inc(red, 1)
                dve.wait_ge(red, SUB - 1)
                dve.wait_ge(chain, 2)
                for i in range(1, SUB):
                    out = p_flat[:, 0:SU * H * i * i].rearrange("p (g j m) -> p g j m", j=i, m=i)
                    nc.vector.tensor_tensor(out, a_flat[:, :, i:i + 1, 0:i].broadcast_to([P, SU * H, i, i]),
                                            t_flat[:, :, 0:i, 0:i].rearrange("p g m j -> p g j m"), ALU.mult).then_inc(fwd, 1)
                    dve.wait_ge(fwd, 2 * i - 1)
                    nc.vector.tensor_reduce(t_flat[:, :, i, 0:i], out, AX.X, ALU.add).then_inc(fwd, 1)
                    dve.wait_ge(fwd, 2 * i)
                for c in range(SU):
                    nc.vector.tensor_copy(TT[:, c], T[:, c].rearrange("p h i j -> p j h i")).then_inc(t_ready, 1)

            @block.sync
            def _(sp):
                sp.dma_start(nw[:, :], io["L0_norm_w"].rearrange("(a n) -> a n", a=1).broadcast_to([P, DV])).then_inc(nw_in, 16)
                sp.wait_ge(t_ready, SU)
                sp.dma_start(io["t_dram"].rearrange("(p i) c -> p (i c)", i=CH), TT[:, :, :, :, :].rearrange("p c j h i -> p (c j h i)")).then_inc(stored, 16)
                sp.wait_ge(stored, 16)
                sp.dma_start(sb["tinv"][:, :, :], io["t_dram"].rearrange("(n p) c -> p n c", p=P)).then_inc(stored, 16)
                sp.wait_ge(stored, 32)


def stage_delta(nc, io, sb, ctx):
    N16, HR = P // SUB, H * RW
    with ExitStack() as st:
        def tmp(name, shp):
            return st.enter_context(nc.sbuf_tensor(name, shp, F32))

        def pair(name, shp):
            return [tmp(f"{name}{b}", shp) for b in range(B)]

        def sem(name):
            return take(nc, name)

        def sems(name):
            return [sem(f"{name}{b}") for b in range(B)]

        def bank(name, shp):
            return st.enter_context(nc.psum_tensor(name, shp, F32))

        tok, tinv, o, ident = sb["tok"], sb["tinv"], sb["o"], sb["ident"]
        row = pair("d_row", [P, TOKW])
        kqT = pair("kqT", [P, 3, P])
        kTx = pair("kTx", [P, H, P])
        tbd = pair("tbd", [P, H, N16, SUB])
        kc = pair("kc", [P, NC, QK])
        pa = pair("pa", [P, H, 2, P])
        y0, zz, uw = pair("y0", [P, YW]), pair("zz", [P, YW]), pair("uw", [P, YW])
        qe, qeT, oi = pair("qe", [P, P]), pair("qeT", [P, P]), pair("oi", [P, H, DV])
        w, mt = pair("w", [P, QK]), pair("mt", [P, NC, QK])
        S = [[tmp(f"S{b}{i}", [P, H, DV]) for i in range(2)] for b in range(B)]
        mask_g, mask_m = tmp("mask_g", [P, 2, P]), tmp("mask_m", [QK, H, DK])
        mask_h, mask_c, mask_s = tmp("mask_h", [QK, H]), tmp("mask_c", [P, NC]), tmp("mask_s", [P, N16])
        zero = tmp("d_zero", [P, P])
        psT = [bank(f"d_psT{b}", [P, 512]) for b in range(B)]
        psG = bank("d_psG", [P, B, 512])
        psY = [bank(f"d_psY{b}", [P, 512]) for b in range(B)]
        acc = [bank(f"d_acc{b}", [P, 512]) for b in range(B)]
        g_all = psG[:, :, :].rearrange("p b (h a l) -> p (b h) a l", h=2, a=2)

        const = sem("d_const")
        loaded, t_ps, kq_sb, ktx, expanded, kc_done, g_ps, pa_done = (sems(n) for n in (
            "d_loaded", "t_ps", "kq_sb", "ktx", "expanded", "kc_done", "g_ps", "pa_done"))
        y_ps, y_used, qt_ps, qt_sb, m_ps, m_done, s_ps, s_sb, o_ps, o_done, w_done = (sems(n) for n in (
            "y_ps", "y_used", "qt_ps", "qt_sb", "m_ps", "m_done", "s_ps", "s_sb", "o_ps", "o_done", "w_done"))

        def by_head(t):
            return t[:, 0:HR].rearrange("p (h c) -> p h c", h=H)

        def heads(ps):
            return ps[:, :].rearrange("p (h c) -> p h c", h=H)[:, :, 0:RW]

        def blk(t, b):
            return bass.ds(t + b * PER, 1)

        def keep_where(pool, ap, base, pattern, mult, op=ALU.is_ge):
            pool.wait_ge(const, keep_where.n)
            pool.affine_select(out=ap, in_=ap, compare_op=op, fill=0.0, base=base, pattern=pattern,
                               channel_multiplier=mult).then_inc(const, 1)
            keep_where.n += 1

        with nc.Block() as block:
            @block.sync
            def _(sp):
                for b in range(B):
                    sp.dma_start(row[b][:, :], tok[:, b * PER]).then_inc(loaded[b], 16)
                with sp.Fori(1, PER) as t:
                    for b in range(B):
                        sp.wait_ge(y_used[b], 4 * t)
                        sp.wait_ge(kc_done[b], t)
                        sp.dma_start(row[b][:, :], tok[:, blk(t, b)].rearrange("p a c -> p (a c)")).then_inc(loaded[b], 16)

            @block.gpsimd
            def _(pool):
                pool.memset(zero[:, :], 0.0)
                for b in range(B):
                    for whole in (S[b][0], S[b][1], kqT[b], kTx[b], mt[b], qeT[b], qe[b], y0[b], zz[b], uw[b]):
                        pool.memset(whole[:], 0.0)
                for m, v in ((mask_g, 0.0), (mask_m, -1.0), (mask_h, 1.0), (mask_c, 1.0), (mask_s, 1.0)):
                    pool.memset(m[:], v).then_inc(const, 1)
                pool.wait_ge(const, 5)
                off = mask_g[:, 1].rearrange("p (c i) -> p c i", c=NC)
                cau = mask_g[:, 0].rearrange("p (c i) -> p c i", c=NC)
                pool.memset(off[:, :, SUB:CH], 1.0).then_inc(const, 1)
                pool.memset(cau, 1.0).then_inc(const, 1)
                keep_where.n = 7
                keep_where(pool, off, 0, [[-CH, NC], [0, CH]], 1)
                keep_where(pool, off, SUB - 1, [[CH, NC], [0, CH]], -1)
                keep_where(pool, cau, 0, [[-CH, NC], [0, CH]], 1)
                keep_where(pool, cau, 0, [[CH, NC], [1, CH]], -1)
                keep_where(pool, mask_m[:, :, :], 0, [[-DK, H], [0, DK]], 1)
                keep_where(pool, mask_m[:, :, :], DK - 1, [[DK, H], [0, DK]], -1)
                keep_where(pool, mask_h[:, :], 0, [[-DK, H]], 1)
                keep_where(pool, mask_h[:, :], DK - 1, [[DK, H]], -1)
                keep_where(pool, mask_c[:, :], 0, [[-CH, NC]], 1)
                keep_where(pool, mask_c[:, :], CH - 1, [[CH, NC]], -1)
                keep_where(pool, mask_s[:, :], 0, [[-SUB, N16]], 1)
                keep_where(pool, mask_s[:, :], SUB - 1, [[SUB, N16]], -1)
                pool.wait_ge(const, 19)
                with pool.Fori(0, PER) as t:
                    for b in range(B):
                        pool.wait_ge(kq_sb[b], t + 1)
                        pool.tensor_tensor(kTx[b][0:QK], kqT[b][0:QK, 0:1].broadcast_to([QK, H, P]), spread(mask_h[:, :], P),
                                           ALU.mult).then_inc(ktx[b], 1)
                    for b in range(B):
                        pool.wait_ge(s_ps[b], NC * t)
                        src = tinv[:, blk(t, b)].rearrange("p a (h i) -> p (a h) i", h=H)
                        pool.tensor_tensor(tbd[b][:, :, :, :], src.unsqueeze(2).broadcast_to([P, H, N16, SUB]),
                                           spread(mask_s[:, :], SUB).unsqueeze(1).broadcast_to([P, H, N16, SUB]),
                                           ALU.mult).then_inc(expanded[b], 1)
                    for b in range(B):
                        pool.wait_ge(loaded[b], 16 * t + 16)
                        pool.tensor_tensor(kc[b][:, :, :], row[b][:, C_K:C_K + QK].unsqueeze(1).broadcast_to([P, NC, QK]),
                                           spread(mask_c[:, :], QK), ALU.mult).then_inc(kc_done[b], 1)

            @block.tensor
            def _(pe):
                pe.wait_ge(const, 19)
                for b in range(B):
                    nc.tensor.matmul(acc[b][0:QK, 0:H * DV], zero[:, 0:QK], zero[:, :], start=True, stop=True)
                with pe.Fori(0, PER) as t:
                    for b in range(B):
                        pe.wait_ge(loaded[b], 16 * t + 16)
                        pe.wait_ge(o_done[b], t)
                        for i, c in enumerate((C_K, C_Q, C_KB)):
                            n = min(P, TOKW - c)
                            mm = nc.tensor.transpose(psT[b][0:n, i * P:(i + 1) * P], row[b][:, c:c + n], ident[:, :])
                        mm.then_inc(t_ps[b], 1)

                    def products(k, b, left, right):
                        pe.wait_ge(y_used[b], 4 * t + k)
                        for h in range(H):
                            mm = nc.tensor.matmul(psY[b][:, h * P:(h + 1) * P], left(h), right[:, h * RW:h * RW + P],
                                                  start=True, stop=True)
                        mm.then_inc(y_ps[b], 1)

                    for b in range(B):
                        pe.wait_ge(ktx[b], t + 1)
                        if b == 0:
                            pe.wait_ge(m_done[0], t)
                            pe.wait_ge(m_done[1], t)
                        else:
                            pe.wait_ge(pa_done[0], t + 1)
                        for h in range(H):
                            mm = nc.tensor.matmul(g_all[:, h], kTx[b][:, h], kqT[b][:, 1:3], start=True, stop=True)
                        mm.then_inc(g_ps[b], 1)
                        pe.wait_ge(expanded[b], t + 1)
                        products(0, b, lambda h: tbd[b][:, h].rearrange("p s i -> p (s i)"), row[b])
                    for b in range(B):
                        pe.wait_ge(pa_done[b], t + 1)
                        products(1, b, lambda h: pa[b][:, h, 1], y0[b])
                    for b in range(B):
                        products(2, b, lambda h: tbd[b][:, h].rearrange("p s i -> p (s i)"),
                                 zz[b])
                    for b in range(B):
                        products(3, b, lambda h: pa[b][:, h, 0], uw[b])
                    for b in range(B):
                        pe.wait_ge(kc_done[b], t + 1)
                        pe.wait_ge(w_done[b], t + 1)
                        nc.tensor.matmul(psG[0:QK, b, 0:NC * QK], w[b][:, :], kc[b][:, :, :],
                                         start=True, stop=True).then_inc(m_ps[b], 1)
                    for b in range(B):
                        pe.wait_ge(y_used[b], 4 * t + 4)
                        nc.tensor.transpose(psT[b][:, 0:P], qe[b][:, :], ident[:, :]).then_inc(qt_ps[b], 1)
                    for c in range(NC):
                        for b in range(B):
                            s_now = S[b][c % 2][:, :, :].rearrange("p h c -> p (h c)")
                            if c == 0:
                                pe.wait_ge(m_done[b], t + 1)
                                pe.wait_ge(qt_sb[b], t + 1)
                            pe.wait_ge(s_sb[b], NC * t + c)
                            nc.tensor.matmul(acc[b][0:QK, 0:H * DV], kc[b][:, c], by_head(uw[b])[:, :, 0:DV], start=False, stop=True,
                                             skip_group_check=True)
                            nc.tensor.matmul(acc[b][0:QK, 0:H * DV], mt[b][:, c], s_now, start=False, stop=True,
                                             skip_group_check=True).then_inc(s_ps[b], 1)
                            mm = nc.tensor.matmul(psT[b][c * CH:(c + 1) * CH, 0:H * DV], qeT[b][:, c * CH:(c + 1) * CH], s_now,
                                                  start=True, stop=True)
                            if c == NC - 1:
                                mm.then_inc(o_ps[b], 1)

            @block.scalar
            def _(act):
                with act.Fori(0, PER) as t:
                    for b in range(B):
                        act.wait_ge(t_ps[b], t + 1)
                        act.activation(kqT[b][0:QK].rearrange("p a l -> p (a l)"), psT[b][0:QK, 0:3 * P], ACT.Copy)\
                            .then_inc(kq_sb[b], 1)
                    for k, dst in ((0, y0), (1, zz)):
                        for b in range(B):
                            act.wait_ge(y_ps[b], 4 * t + k + 1)
                            act.activation(by_head(dst[b]), heads(psY[b]), ACT.Copy).then_inc(y_used[b], 1)
                    for b in range(B):
                        act.wait_ge(y_used[b], 4 * t + 3)
                        act.activation(w[b][:, :].rearrange("p (h c) -> p h c", h=H), by_head(uw[b])[:, :, DV:RW], ACT.Copy)\
                            .then_inc(w_done[b], 1)
                    for b in range(B):
                        act.wait_ge(qt_ps[b], t + 1)
                        act.activation(qeT[b][0:QK], psT[b][0:QK, 0:P], ACT.Copy).then_inc(qt_sb[b], 1)

            @block.vector
            def _(dve):
                dve.wait_ge(const, 19)
                with dve.Fori(0, PER) as t:
                    for b in range(B):
                        dve.wait_ge(g_ps[b], t + 1)
                        nc.vector.tensor_tensor(pa[b][:, :, :, :].rearrange("p h a l -> p h (a l)"),
                                                g_all.rearrange("p h a l -> p h (a l)"),
                                                mask_g[:, :, :].rearrange("p a l -> p (a l)").unsqueeze(1).broadcast_to([P, H, 2 * P]),
                                                ALU.mult).then_inc(pa_done[b], 1)
                    for b in range(B):
                        dve.wait_ge(y_ps[b], 4 * t + 3)
                        nc.vector.tensor_tensor(by_head(uw[b]), by_head(y0[b]), heads(psY[b]), ALU.subtract).then_inc(y_used[b], 1)
                    for b in range(B):
                        dve.wait_ge(y_ps[b], 4 * t + 4)
                        y = heads(psY[b])
                        nc.vector.tensor_copy(oi[b][:, :, :], y[:, :, 0:DV])
                        nc.vector.tensor_tensor(qe[b][:, 0:QK].rearrange("p (h c) -> p h c", h=H),
                                                row[b][:, C_Q:C_Q + QK].rearrange("p (h c) -> p h c", h=H), y[:, :, DV:RW],
                                                ALU.subtract).then_inc(y_used[b], 1)
                    for b in range(B):
                        dve.wait_ge(m_ps[b], t + 1)
                        nc.vector.tensor_tensor(mt[b][0:QK], psG[0:QK, b, 0:NC * QK].rearrange("p (c d) -> p c d", c=NC),
                                                mask_m[:, :, :].rearrange("p h d -> p (h d)").unsqueeze(1).broadcast_to([QK, NC, QK]),
                                                ALU.mult).then_inc(m_done[b], 1)
                    for c in range(NC):
                        for b in range(B):
                            dve.wait_ge(s_ps[b], NC * t + c + 1)
                            nc.vector.tensor_tensor(S[b][(c + 1) % 2][0:QK],
                                                    acc[b][0:QK, 0:H * DV].rearrange("p (h e) -> p h e", h=H),
                                                    spread(mask_h[:, :], DV), ALU.mult).then_inc(s_sb[b], 1)
                    for b in range(B):
                        dve.wait_ge(o_ps[b], t + 1)
                        dve.wait_ge(y_used[b], 4 * t + 4)
                        nc.vector.tensor_tensor(o[:, blk(t, b)].rearrange("p a d -> p (a d)"), psT[b][:, 0:H * DV],
                                                oi[b][:, :, :].rearrange("p h c -> p (h c)"), ALU.add).then_inc(o_done[b], 1)


def group(t, b):
    return bass.ds(4 * t + b * PER, 4)


def stage_close_delta(nc, io, sb, ctx):
    with ExitStack() as st:
        def tmp(name, shp):
            return st.enter_context(nc.sbuf_tensor(name, shp, F32))

        def sem(name):
            return take(nc, name)

        def sems(name):
            return [sem(f"{name}{b}") for b in range(B)]

        o, gate, r, ident = sb["o"], sb["gate"], sb["r"], sb["ident"]
        wo = tmp("c_wo", [H * DV, D])
        sq = tmp("c_sq", [P, BLOCKS, D])
        ms, rs = tmp("c_ms", [P, BLOCKS, H]), tmp("c_rs", [P, BLOCKS, H])
        xin = [tmp(f"c_x{b}", [P, 4, D]) for b in range(B)]
        on = [tmp(f"c_on{b}", [P, 4, D]) for b in range(B)]
        og = [tmp(f"c_og{b}", [P, 4, D]) for b in range(B)]
        oT = [tmp(f"c_oT{b}", [P, 4, P]) for b in range(B)]
        psT = [st.enter_context(nc.psum_tensor(f"c_psT{b}", [P, 512], F32)) for b in range(B)]
        psO = [st.enter_context(nc.psum_tensor(f"c_psO{b}", [P, 4, D], F32)) for b in range(B)]
        x_in, t_ps, t_sb, o_ps, r_done, on_done, og_done = (sems(f"c_{n}") for n in (
            "x_in", "t_ps", "t_sb", "o_ps", "r_done", "on_done", "og_done"))
        w_in, squared, rooted, v_step = (sem(f"c_{n}") for n in ("w_in", "squared", "rooted", "v_step"))
        x_dram = io["x"].rearrange("b (t k p) d -> p b t k d", p=P, k=4)

        with nc.Block() as block:
            @block.sync
            def _(sp):
                sp.dma_start(wo[:, :], io["L0_Wo"][:, :]).then_inc(w_in, 16)
                for b in range(B):
                    sp.dma_start(xin[b][:, :, :], x_dram[:, b, 0]).then_inc(x_in[b], 16)
                with sp.Fori(1, PER // 4) as t:
                    for b in range(B):
                        sp.wait_ge(r_done[b], t)
                        sp.dma_start(xin[b][:, :, :], x_dram[:, b, bass.ds(t, 1)].rearrange("p a k d -> p (a k) d"))\
                            .then_inc(x_in[b], 16)

            @block.scalar
            def _(act):
                for b in range(B):
                    act.activation(sq[:, b * PER:(b + 1) * PER], o[:, b * PER:(b + 1) * PER], ACT.Square).then_inc(squared, 1)
                act.wait_ge(v_step, B + 1)
                act.activation(rs[:, :, :], ms[:, :, :], ACT.Sqrt).then_inc(rooted, 1)
                with act.Fori(0, PER // 4) as t:
                    for b in range(B):
                        act.wait_ge(t_ps[b], t + 1)
                        act.activation(oT[b][:, :, :], psT[b][:, :].rearrange("p (k l) -> p k l", k=4), ACT.Copy)\
                            .then_inc(t_sb[b], 1)

            @block.vector
            def _(dve):
                for b in range(B):
                    s = slice(b * PER, (b + 1) * PER)
                    dve.wait_ge(squared, b + 1)
                    nc.vector.tensor_reduce(ms[:, s], sq[:, s].rearrange("p n (h c) -> p n h c", h=H), AX.X, ALU.add)\
                        .then_inc(v_step, 1)
                dve.wait_ge(v_step, B)
                nc.vector.tensor_scalar(ms[:, :, :], ms[:, :, :], 1.0 / DV, EPS, ALU.mult, ALU.add).then_inc(v_step, 1)
                dve.wait_ge(rooted, 1)
                nc.vector.reciprocal(rs[:, :, :], rs[:, :, :]).then_inc(v_step, 1)
                dve.wait_ge(v_step, B + 2)
                with dve.Fori(0, PER // 4) as t:
                    for b in range(B):
                        heads = on[b][:, :, :].rearrange("p k (h c) -> p k h c", h=H)
                        dve.wait_ge(og_done[b], t)
                        nc.vector.tensor_tensor(heads, o[:, group(t, b)].rearrange("p k (h c) -> p k h c", h=H),
                                                spread(rs[:, group(t, b)], DV), ALU.mult).then_inc(on_done[b], 1)
                    for b in range(B):
                        dve.wait_ge(on_done[b], t + 1)
                        dve.wait_ge(t_ps[b], t)
                        nc.vector.tensor_tensor(og[b][:, :, :], on[b][:, :, :], gate[:, group(t, b)], ALU.mult)\
                            .then_inc(og_done[b], 1)
                    for b in range(B):
                        dve.wait_ge(o_ps[b], t + 1)
                        dve.wait_ge(x_in[b], 16 * t + 16)
                        nc.vector.tensor_tensor(r[:, group(t, b)], psO[b][:, :, :], xin[b][:, :, :], ALU.add)\
                            .then_inc(r_done[b], 1)

            @block.tensor
            def _(pe):
                pe.wait_ge(w_in, 16)
                with pe.Fori(0, PER // 4) as t:
                    for b in range(B):
                        pe.wait_ge(t_sb[b], t)
                        pe.wait_ge(og_done[b], t + 1)
                        for k in range(4):
                            mm = nc.tensor.transpose(psT[b][:, k * P:(k + 1) * P], og[b][:, k], ident[:, :])
                        mm.then_inc(t_ps[b], 1)
                    for b in range(B):
                        pe.wait_ge(r_done[b], t)
                        pe.wait_ge(t_sb[b], t + 1)
                        for k in range(4):
                            mm = nc.tensor.matmul(psO[b][:, k], oT[b][:, k], wo[:, :], start=True, stop=True)
                        mm.then_inc(o_ps[b], 1)


def stage_norm(nc, io, sb, tag, router=None):
    with ExitStack() as st:
        def tmp(name, shp):
            return st.enter_context(nc.sbuf_tensor(f"{tag}_{name}", shp, F32))

        def sem(name):
            return take(nc, f"{tag}_{name}")

        def sems(name):
            return [sem(f"{name}{b}") for b in range(B)]

        r, x, xT, ident = sb["r"], sb["x"], sb.get("xT"), sb["ident"]
        stats = [tmp(f"stats{b}", [P, 4, 6]) for b in range(B)]
        mean, gap, m2 = ([tmp(f"{n}{b}", [P, 4]) for b in range(B)] for n in ("mean", "gap", "m2"))
        ve = [tmp(f"ve{b}", [P, 4]) for b in range(B)]
        sd = [tmp(f"sd{b}", [P, 4]) for b in range(B)]
        rstd = [tmp(f"rstd{b}", [P, 4]) for b in range(B)]
        xn = [tmp(f"xn{b}", [P, 4, D]) for b in range(B)]
        step, rooted, n_done, copied, t_ps, t_sb, t_out, l_ps, l_done, sent = (sems(n) for n in (
            "step", "rooted", "n_done", "copied", "t_ps", "t_sb", "t_out", "l_ps", "l_done", "sent"))
        w_in, padded = sem("w_in"), sem("padded")
        if router is not None:
            xs = [tmp(f"xs{b}", [P, 4, P]) for b in range(B)]
            wr = tmp("wr", [D, P])
            psT = [st.enter_context(nc.psum_tensor(f"{tag}_psT{b}", [P, 512], F32)) for b in range(B)]
            psL = [st.enter_context(nc.psum_tensor(f"{tag}_psL{b}", [P, 4, P], F32)) for b in range(B)]
            logits = sb["logits"]

        with nc.Block() as block:
            @block.vector
            def _(dve):
                with dve.Fori(0, PER // 4) as t:
                    for b in range(B):
                        for k in range(4):
                            src = r[:, bass.ds(4 * t + (b * PER + k), 1)].rearrange("p a d -> p (a d)")
                            ins = nc.vector.bn_stats(stats[b][:, k], src)
                        ins.then_inc(step[b], 1)
                        dve.wait_ge(step[b], 4 * t + 1)
                        s4 = stats[b]
                        nc.vector.tensor_tensor(mean[b][:, :], s4[:, :, 1], s4[:, :, 4], ALU.add)
                        nc.vector.tensor_tensor(gap[b][:, :], s4[:, :, 1], s4[:, :, 4], ALU.subtract)
                        nc.vector.tensor_tensor(m2[b][:, :], s4[:, :, 2], s4[:, :, 5], ALU.add).then_inc(step[b], 1)
                        dve.wait_ge(step[b], 4 * t + 2)
                        nc.vector.tensor_scalar(mean[b][:, :], mean[b][:, :], 0.5, None, ALU.mult)
                        nc.vector.scalar_tensor_tensor(gap[b][:, :], gap[b][:, :], 0.25, gap[b][:, :], ALU.mult, ALU.mult)
                        nc.vector.tensor_scalar(m2[b][:, :], m2[b][:, :], 1.0 / D, EPS, ALU.mult, ALU.add).then_inc(step[b], 1)
                        dve.wait_ge(step[b], 4 * t + 3)
                        nc.vector.tensor_tensor(ve[b][:, :], m2[b][:, :], gap[b][:, :], ALU.add).then_inc(step[b], 1)
                    for b in range(B):
                        dve.wait_ge(rooted[b], t + 1)
                        nc.vector.reciprocal(rstd[b][:, :], sd[b][:, :]).then_inc(l_done[b], 1)
                        dve.wait_ge(l_done[b], t + 1)
                        if router is not None:
                            dve.wait_ge(t_ps[b], t)
                            dve.wait_ge(copied[b], t)
                        else:
                            dve.wait_ge(sent[b], 16 * t)
                        for k in range(4):
                            src = r[:, bass.ds(4 * t + (b * PER + k), 1)].rearrange("p a d -> p (a d)")
                            ins = nc.vector.tensor_scalar(xn[b][:, k], src, mean[b][:, k:k + 1], rstd[b][:, k:k + 1],
                                                          ALU.subtract, ALU.mult)
                        ins.then_inc(n_done[b], 1)
                    if router is not None:
                        for b in range(B):
                            dve.wait_ge(l_ps[b], t + 1)
                            nc.vector.tensor_copy(logits[:, group(t, b)], psL[b][:, :, 0:E]).then_inc(sent[b], 1)

            @block.scalar
            def _(act):
                with act.Fori(0, PER // 4) as t:
                    for b in range(B):
                        act.wait_ge(step[b], 4 * t + 4)
                        act.wait_ge(l_done[b], t)
                        act.activation(sd[b][:, :], ve[b][:, :], ACT.Sqrt).then_inc(rooted[b], 1)
                    if router is not None:
                        for b in range(B):
                            act.wait_ge(t_ps[b], t + 1)
                            act.activation(xs[b][:, :, :].rearrange("p k l -> p (k l)"), psT[b][:, :], ACT.Copy).then_inc(t_sb[b], 1)
                            if xT is not None:
                                act.activation(xT[:, bass.ds(512 * t + b * L, 512)], psT[b][:, :], ACT.Copy).then_inc(t_out[b], 1)

            if router is None:
                @block.sync
                def _(sp):
                    out = io["out"].rearrange("b (t k p) d -> p b t k d", p=P, k=4)
                    with sp.Fori(0, PER // 4) as t:
                        for b in range(B):
                            sp.wait_ge(n_done[b], t + 1)
                            sp.dma_start(out[:, b, bass.ds(t, 1)].rearrange("p a k d -> p (a k) d"), xn[b][:, :, :])\
                                .then_inc(sent[b], 16)
                    for b in range(B):
                        sp.wait_ge(sent[b], 16 * (PER // 4))
            else:
                @block.sync
                def _(sp):
                    sp.wait_ge(padded, 1)
                    sp.dma_start(wr[:, 0:E], router[:, :]).then_inc(w_in, 16)

                @block.gpsimd
                def _(pool):
                    pool.memset(wr[:, :], 0.0).then_inc(padded, 1)
                    with pool.Fori(0, PER // 4) as t:
                        for b in range(B):
                            pool.wait_ge(n_done[b], t + 1)
                            pool.tensor_copy(x[:, group(t, b)], xn[b][:, :, :]).then_inc(copied[b], 1)

                @block.tensor
                def _(pe):
                    pe.wait_ge(w_in, 16)
                    with pe.Fori(0, PER // 4) as t:
                        for b in range(B):
                            pe.wait_ge(t_out[b] if xT is not None else t_sb[b], t)
                            pe.wait_ge(n_done[b], t + 1)
                            for k in range(4):
                                mm = nc.tensor.transpose(psT[b][:, k * P:(k + 1) * P], xn[b][:, k], ident[:, :])
                            mm.then_inc(t_ps[b], 1)
                        for b in range(B):
                            pe.wait_ge(sent[b], t)
                            pe.wait_ge(t_sb[b], t + 1)
                            for k in range(4):
                                mm = nc.tensor.matmul(psL[b][:, k], xs[b][:, k], wr[:, :], start=True, stop=True)
                            mm.then_inc(l_ps[b], 1)

STEPS = [2 * -(-(w * BLOCKS + E - 1) // 2) for w in (1, 2)]
AHEAD = 3


def stage_route(nc, io, sb, tag, ways, rows_dram, zeroed, bias=None):
    tiles = STEPS[ways - 1] + AHEAD
    with ExitStack() as st:
        def tmp(name, shp, dt=F32):
            return st.enter_context(nc.sbuf_tensor(f"{tag}_{name}", shp, dt))

        def sem(name):
            return take(nc, f"{tag}_{name}")

        lg, x = sb["logits"], sb["x"]
        weight, slot = sb["weight"], sb["slot"]
        eq, rank = tmp("eq", [P, BLOCKS, E]), tmp("rank", [P, E])
        sel = [tmp(f"sel{i}", [P, BLOCKS, E]) for i in range(2)]
        both = tmp("both", [P, BLOCKS, E])
        top = [tmp(f"top{i}", [P, BLOCKS]) for i in range(2)]
        key, ex, den = tmp("key", [P, BLOCKS]), tmp("ex", [P, BLOCKS, E]), tmp("den", [P, BLOCKS])
        br = tmp("br", [P, E])
        before, ones = tmp("before", [P, P]), tmp("ones", [P, P])
        seen = [tmp(f"seen{i}", [P, BLOCKS + 1, E]) for i in range(2)]
        place = tmp("place", [P, BLOCKS, E])
        picked = tmp("picked", [P, BLOCKS, E])
        slot_f = tmp("slot_f", [P, BLOCKS])
        steps, filled, first = tmp("steps", [P, BLOCKS]), tmp("filled", [P, E, BLOCKS]), tmp("first", [P, E])
        count, ends, upto = tmp("count", [P, E]), tmp("ends", [P, E]), tmp("upto", [P, E, E])
        tri_e = tmp("tri_e", [P, E, E])
        it, over = tmp("it", [P, tiles]), tmp("over", [P, tiles, E])
        exp_f = tmp("exp_f", [P, tiles])
        ps_in = st.enter_context(nc.psum_tensor(f"{tag}_in", [P, 512], F32))
        ps_all = st.enter_context(nc.psum_tensor(f"{tag}_all", [P, 512], F32))
        step, exped, const, b_in, chosen, counted, slots, sent = (sem(n) for n in (
            "step", "exped", "const", "b_in", "chosen", "counted", "slots", "sent"))

        def every(ap, n):
            return ap.unsqueeze(1).broadcast_to([P, n, ap.shape[1]])

        with nc.Block() as block:
            @block.gpsimd
            def _(pool):
                pool.iota(steps[:, :], pattern=[[P, BLOCKS]], base=0, channel_multiplier=0, allow_small_or_imprecise_dtypes=True)
                pool.iota(it[:, :], pattern=[[1, tiles]], base=0, channel_multiplier=0, allow_small_or_imprecise_dtypes=True)
                pool.iota(rank[:, :], pattern=[[-1, E]], base=E, channel_multiplier=0, allow_small_or_imprecise_dtypes=True)
                pool.memset(ones[:, :], 1.0)
                pool.memset(before[:, :], 1.0)
                pool.memset(tri_e[:, :, :], 1.0).then_inc(const, 1)
                pool.wait_ge(const, 1)
                pool.affine_select(out=before[:, :], in_=before[:, :], compare_op=ALU.is_ge, fill=0.0, base=-1,
                                   pattern=[[1, P]], channel_multiplier=-1).then_inc(const, 1)
                pool.affine_select(out=tri_e[:, :, :], in_=tri_e[:, :, :], compare_op=ALU.is_ge, fill=0.0, base=0,
                                   pattern=[[1, E], [-1, E]], channel_multiplier=0).then_inc(const, 1)
                pool.wait_ge(const, 3)
                if zeroed is not None:
                    pool.wait_ge(zeroed, 16)
                for w in range(ways):
                    pool.wait_ge(slots, w + 1)
                    for n in range(BLOCKS):
                        pool.indirect_dma_start(out=rows_dram, out_offset=bass.IndirectOffsetOnAxis(ap=slot[w][:, n:n + 1], axis=0),
                                                in_=x[:, n], in_offset=None).then_inc(sent, 16)
                pool.wait_ge(sent, 16 * ways * BLOCKS)

            @block.sync
            def _(sp):
                if bias is not None:
                    sp.dma_start(br[:, :], bias.rearrange("(a e) -> a e", a=1).broadcast_to([P, E])).then_inc(b_in, 16)

            @block.scalar
            def _(act):
                act.wait_ge(exped, 1)
                if ways == 2:
                    act.activation(den[:, :], key[:, :], ACT.Exp).then_inc(exped, 1)
                else:
                    act.activation(ex[:, :, :], ex[:, :, :], ACT.Exp).then_inc(exped, 1)

            @block.tensor
            def _(pe):
                pe.wait_ge(const, 3)
                pe.wait_ge(*((chosen, 1) if ways == 2 else (step, 5 + (bias is not None))))
                rhs = (both if ways == 2 else sel[0])[:, :, :].rearrange("p n e -> p (n e)")
                nc.tensor.matmul(ps_in[:, 0:BLOCKS * E], before[:, :], rhs, start=True, stop=True).then_inc(counted, 1)
                nc.tensor.matmul(ps_all[:, 0:BLOCKS * E], ones[:, :], rhs, start=True, stop=True).then_inc(counted, 1)

            @block.vector
            def _(dve):
                v = nc.vector
                count_v = 0

                def link(ins):
                    nonlocal count_v
                    count_v += 1
                    ins.then_inc(step, 1)
                    dve.wait_ge(step, count_v)

                def choose(i):
                    link(v.tensor_reduce(top[i][:, :], lg[:, :, :], AX.X, ALU.max))
                    link(v.tensor_tensor(eq[:, :, :], lg[:, :, :], spread(top[i][:, :], E), ALU.is_equal))
                    link(v.tensor_tensor(eq[:, :, :], eq[:, :, :], every(rank[:, :], BLOCKS), ALU.mult))
                    link(v.tensor_reduce(key[:, :], eq[:, :, :], AX.X, ALU.max))
                    link(v.tensor_tensor(sel[i][:, :, :], eq[:, :, :], spread(key[:, :], E), ALU.is_equal))

                dve.wait_ge(const, 3)
                if bias is not None:
                    dve.wait_ge(b_in, 16)
                    link(v.tensor_tensor(lg[:, :, :], lg[:, :, :], every(br[:, :], BLOCKS), ALU.add))
                choose(0)
                if ways == 2:
                    link(v.scalar_tensor_tensor(lg[:, :, :], sel[0][:, :, :], -3.0e38, lg[:, :, :], ALU.mult, ALU.add))
                    choose(1)
                    v.tensor_tensor(both[:, :, :], sel[0][:, :, :], sel[1][:, :, :], ALU.add).then_inc(chosen, 1)
                    v.tensor_tensor(key[:, :], top[1][:, :], top[0][:, :], ALU.subtract).then_inc(exped, 1)
                else:
                    v.tensor_tensor(ex[:, :, :], lg[:, :, :], spread(top[0][:, :], E), ALU.subtract).then_inc(exped, 1)
                dve.wait_ge(counted, 2)
                v.memset(seen[0][:, 0], 0.0)
                link(v.tensor_copy(seen[0][:, 1:], ps_all[:, 0:BLOCKS * E].rearrange("p (n e) -> p n e", e=E)))
                a, d = 0, 1
                while d < BLOCKS + 1:
                    v.tensor_copy(seen[1 - a][:, 0:d], seen[a][:, 0:d])
                    link(v.tensor_tensor(seen[1 - a][:, d:], seen[a][:, d:], seen[a][:, 0:BLOCKS + 1 - d], ALU.add))
                    a, d = 1 - a, 2 * d
                total = seen[a][:, BLOCKS]
                link(v.tensor_tensor(filled[:, :, :], spread(total, BLOCKS), every(steps[:, :], E), ALU.is_gt))
                link(v.tensor_reduce(count[:, :], filled[:, :, :], AX.X, ALU.add))
                link(v.tensor_tensor(upto[:, :, :], every(count[:, :], E), tri_e[:, :, :], ALU.mult))
                link(v.tensor_reduce(ends[:, :], upto[:, :, :], AX.X, ALU.add))
                link(v.tensor_tensor(first[:, :], ends[:, :], count[:, :], ALU.subtract))
                link(v.tensor_scalar(first[:, :], first[:, :], float(P), None, ALU.mult))
                link(v.tensor_tensor(place[:, :, :], seen[a][:, 0:BLOCKS], ps_in[:, 0:BLOCKS * E].rearrange("p (n e) -> p n e", e=E),
                                     ALU.add))
                link(v.tensor_tensor(place[:, :, :], place[:, :, :], every(first[:, :], BLOCKS), ALU.add))
                for w in range(ways):
                    link(v.tensor_tensor(picked[:, :, :], place[:, :, :], sel[w][:, :, :], ALU.mult))
                    link(v.tensor_reduce(slot_f[:, :], picked[:, :, :], AX.X, ALU.add))
                    v.tensor_copy(slot[w][:, :], slot_f[:, :]).then_inc(slots, 1)
                if ways == 1:
                    dve.wait_ge(exped, 2)
                    link(v.tensor_reduce(den[:, :], ex[:, :, :], AX.X, ALU.add))
                    link(v.reciprocal(weight[0][:, :], den[:, :]))
                else:
                    dve.wait_ge(exped, 2)
                    link(v.tensor_scalar(top[0][:, :], den[:, :], 1.0, None, ALU.add))
                    link(v.reciprocal(weight[0][:, :], top[0][:, :]))
                    link(v.tensor_tensor(weight[1][:, :], den[:, :], weight[0][:, :], ALU.mult))
                link(v.tensor_tensor(over[:, :, :], spread(it[:, :], E), every(ends[:, :], tiles), ALU.is_ge))
                link(v.tensor_reduce(exp_f[:, :], over[:, :, :], AX.X, ALU.add))
                link(v.tensor_scalar(sb["expert_of"][:, 0:tiles], exp_f[:, :], float(E - 1), None, ALU.min))


def stage_tiles(nc, io, sb, tag, gated, rows_dram, out_dram, w_in, wa, wb, wc=None, b1=None, b2=None):
    tiles = STEPS[int(gated)]
    F = wa.shape[2]
    NF = F // P
    with ExitStack() as st:
        def tmp(name, shp, dt=F32):
            return st.enter_context(nc.sbuf_tensor(f"{tag}_{name}", shp, dt))

        def pair(name, shp):
            return [tmp(f"{name}{i}", shp) for i in range(2)]

        def sem(name):
            return take(nc, f"{tag}_{name}")

        def bank(name):
            return st.enter_context(nc.psum_tensor(f"{tag}_{name}", [P, 512], F32))

        ident, expert_of = sb["ident"], sb["expert_of"]
        row, xT, pre, h = pair("row", [P, D]), pair("xT", [D, P]), pair("pre", [P, F]), pair("h", [P, F])
        hT, y = pair("hT", [P, NF, P]), pair("y", [P, D])
        psX, psH, psT, psY = ([bank(f"{n}{i}") for i in range(2)] for n in ("psX", "psH", "psT", "psY"))
        l_in = [sem(f"l_in{i}") for i in range(2)]
        x_ps, x_sb, h_ps, pre_done, h_done, t_ps, t_sb, y_ps, y_sb = (sem(n) for n in (
            "x_ps", "x_sb", "h_ps", "pre_done", "h_done", "t_ps", "t_sb", "y_ps", "y_sb"))
        stored = [sem(f"stored{i}") for i in range(2)]
        rows_t, out_t = (a.rearrange("(n p) d -> p n d", p=P) for a in (rows_dram, out_dram))

        with nc.Block() as block:
            @block.gpsimd
            def _(pool):
                def load(i, p):
                    pool.dma_start(row[p][:, :], rows_t[:, bass.ds(i, 1)].rearrange("p a d -> p (a d)")).then_inc(l_in[p], 16)

                load(0, 0)
                load(1, 1)
                with pool.Fori(0, tiles, 2) as i0:
                    for p in range(2):
                        pool.wait_ge(x_ps, i0 + p + 1)
                        load(i0 + p + 2, p)
                pool.wait_ge(x_ps, tiles + 1)
                load(tiles + 2, 0)
                for p in range(2):
                    pool.wait_ge(l_in[p], 8 * tiles + 32 - 16 * p)

            @block.sync
            def _(sp):
                for p in range(2):
                    sp.sem_inc(stored[p], 1)
                with sp.Fori(0, tiles, 2) as i0:
                    for p in range(2):
                        sp.wait_ge(y_sb, i0 + p + 2)
                        sp.dma_start(out_t[:, bass.ds(i0 + p, 1)].rearrange("p a d -> p (a d)"), y[p][:, :]).then_inc(stored[p], 16)
                for p in range(2):
                    sp.wait_ge(stored[p], 8 * tiles + 1)

            @block.tensor
            def _(pe):
                def x_up(i, p, seen):
                    pe.wait_ge(l_in[p], seen)
                    nc.tensor.transpose(psX[p][:, 0:P], row[p][:, :], ident[:, :]).then_inc(x_ps, 1)

                def up(i, p):
                    e = pe.value_load(expert_of[0:1, bass.ds(i, 1)], min_val=0, max_val=E - 1)
                    pe.wait_ge(x_sb, i + 1)
                    if gated:
                        nc.tensor.matmul(psH[p][:, 0:F], xT[p][:, :], wa[:, bass.ds(e, 1)].rearrange("p a f -> p (a f)"),
                                         start=True, stop=True)
                        nc.tensor.matmul(psH[p][:, F:2 * F], xT[p][:, :], wc[:, bass.ds(e, 1)].rearrange("p a f -> p (a f)"),
                                         start=True, stop=True).then_inc(h_ps, 1)
                    else:
                        nc.tensor.matmul(psH[p][:, :], xT[p][:, :], wa[:, bass.ds(e, 1)].rearrange("p a f -> p (a f)"),
                                         start=True, stop=True).then_inc(h_ps, 1)

                if w_in is not None:
                    pe.wait_ge(w_in, 16 * 4)
                x_up(0, 0, 16)
                x_up(1, 1, 16)
                up(0, 0)
                up(1, 1)
                x_up(2, 0, 32)
                with pe.Fori(0, tiles, 2) as i0:
                    for p in range(2):
                        i = i0 + p
                        pe.wait_ge(h_done, i + 1)
                        pe.wait_ge(t_sb, i + 1)
                        for f in range(NF):
                            mm = nc.tensor.transpose(psT[p][:, f * P:(f + 1) * P], h[p][:, f * P:(f + 1) * P], ident[:, :])
                        mm.then_inc(t_ps, 1)
                        up(i + 2, p)
                        e = pe.value_load(expert_of[0:1, bass.ds(i, 1)], min_val=0, max_val=E - 1)
                        pe.wait_ge(t_sb, i + 2)
                        pe.wait_ge(y_sb, i + 1)
                        for f in range(NF):
                            mm = nc.tensor.matmul(psY[p][:, 0:D], hT[p][:, f], wb[:, bass.ds(e * NF + f, 1)].rearrange("p a d -> p (a d)"),
                                                  start=(f == 0), stop=(f == NF - 1))
                        mm.then_inc(y_ps, 1)
                        x_up(i + 3, 1 - p, 8 * i0 + 16 * ((p + 3) // 2 + 1))

            @block.scalar
            def _(act):
                def x_copy(i, p):
                    act.wait_ge(x_ps, i + 1)
                    act.activation(xT[p][:, :], psX[p][:, 0:P], ACT.Copy).then_inc(x_sb, 1)

                def act_h(i, p):
                    if gated:
                        act.wait_ge(h_ps, i + 1)
                        act.activation(pre[p][:, :], psH[p][:, 0:F], ACT.Silu).then_inc(pre_done, 1)
                    else:
                        act.wait_ge(pre_done, i + 1)
                        act.activation(h[p][:, :], pre[p][:, :], ACT.Gelu).then_inc(h_done, 1)

                act.sem_inc(t_sb, 1)
                x_copy(0, 0)
                x_copy(1, 1)
                act_h(0, 0)
                act_h(1, 1)
                x_copy(2, 0)
                with act.Fori(0, tiles, 2) as i0:
                    for p in range(2):
                        i = i0 + p
                        act.wait_ge(t_ps, i + 1)
                        act.activation(hT[p][:, :, :].rearrange("p f l -> p (f l)"), psT[p][:, 0:F], ACT.Copy).then_inc(t_sb, 1)
                        act_h(i + 2, p)
                        x_copy(i + 3, 1 - p)

            @block.vector
            def _(dve):
                def vec_h(i, p):
                    if gated:
                        dve.wait_ge(pre_done, i + 1)
                        nc.vector.tensor_tensor(h[p][:, :], pre[p][:, :], psH[p][:, F:2 * F], ALU.mult).then_inc(h_done, 1)
                    else:
                        e = dve.value_load(expert_of[0:1, bass.ds(i, 1)], min_val=0, max_val=E - 1)
                        dve.wait_ge(h_ps, i + 1)
                        nc.vector.tensor_tensor(pre[p][:, :], psH[p][:, :], b1[:, bass.ds(e, 1)].rearrange("p a f -> p (a f)"),
                                                ALU.add).then_inc(pre_done, 1)

                dve.sem_inc(y_sb, 1)
                if w_in is not None:
                    dve.wait_ge(w_in, 16 * 4)
                vec_h(0, 0)
                vec_h(1, 1)
                with dve.Fori(0, tiles, 2) as i0:
                    for p in range(2):
                        i = i0 + p
                        dve.wait_ge(t_ps, i + 1)
                        vec_h(i + 2, p)
                        if not gated:
                            e = dve.value_load(expert_of[0:1, bass.ds(i, 1)], min_val=0, max_val=E - 1)
                        dve.wait_ge(stored[p], 8 * i0 + 1)
                        dve.wait_ge(y_ps, i + 1)
                        if gated:
                            nc.vector.tensor_copy(y[p][:, :], psY[p][:, 0:D]).then_inc(y_sb, 1)
                        else:
                            nc.vector.tensor_tensor(y[p][:, :], psY[p][:, 0:D], b2[:, bass.ds(e, 1)].rearrange("p a d -> p (a d)"),
                                                    ALU.add).then_inc(y_sb, 1)


def stage_combine(nc, io, sb, tag, ways, out_dram, pending=()):
    with ExitStack() as st:
        y = [st.enter_context(nc.sbuf_tensor(f"{tag}_y{w}", [P, BLOCKS, D], F32)) for w in range(ways)]
        got = [take(nc, f"{tag}_got{k}") for k in range(4)]
        done = take(nc, f"{tag}_done")
        r, x = sb["r"], sb["x"]
        with nc.Block() as block:
            @block.sync
            def _(sp):
                for signal, total in pending:
                    sp.wait_ge(signal, total)

            @block.gpsimd
            def _(pool):
                for n in range(BLOCKS):
                    for w in range(ways):
                        i = n * ways + w
                        if i >= 4:
                            pool.wait_ge(got[i % 4], 16 * (i // 4))
                        pool.indirect_dma_start(out=y[w][:, n], out_offset=None, in_=out_dram[0:STEPS[ways - 1] * P, :],
                                                in_offset=bass.IndirectOffsetOnAxis(ap=sb["slot"][w][:, n:n + 1], axis=0))\
                            .then_inc(got[i % 4], 16)

            @block.vector
            def _(dve):
                for n in range(BLOCKS):
                    for w in range(ways):
                        i = n * ways + w
                        dve.wait_ge(got[i % 4], 16 * (i // 4 + 1))
                        if w:
                            dve.wait_ge(done, i)
                        nc.vector.scalar_tensor_tensor(r[:, n], y[w][:, n], sb["weight"][w][:, n:n + 1], (r if w else x)[:, n],
                                                       ALU.mult, ALU.add).then_inc(done, 1)


def stage_linear_attention(nc, io, sb):
    NH = 16
    DH = D // NH
    HF = NH // 2 * DH * DH
    with ExitStack() as st:
        def tmp(name, shp):
            return st.enter_context(nc.sbuf_tensor(f"l_{name}", shp, F32))

        def pair(name, shp):
            return [tmp(f"{name}{b}", shp) for b in range(B)]

        def sem(name):
            return take(nc, f"l_{name}")

        def sems(name):
            return [sem(f"{name}{b}") for b in range(B)]

        def bank(name):
            return st.enter_context(nc.psum_tensor(f"l_{name}", [P, 512], F32))

        x, xT, r, ident = sb["x"], sb["xT"], sb["r"], sb["ident"]
        w_raw = tmp("w_raw", [D, 4, D])
        wT = tmp("wT", [D, 4, D])
        b_qkv, b_o = tmp("b_qkv", [P, 3, D]), tmp("b_o", [P, D])
        tri, mask, zero = tmp("tri", [P, P]), tmp("mask", [P, NH, DH]), tmp("zero", [P, P])
        xs, qkv, kv = pair("xs", [P, P]), pair("qkv", [P, 3, D]), pair("kv", [P, 2, HF])
        S, qT, prod = pair("S", [P, NH, DH]), pair("qT", [P, P]), pair("prod", [P, 2, HF])
        intra, out, oT = pair("intra", [P, D]), pair("out", [P, D]), pair("oT", [P, P])
        ps_a, ps_c, ps_s = [bank(f"a{b}") for b in range(B)], [bank(f"c{b}") for b in range(B)], [bank(f"s{b}") for b in range(B)]
        ps_t = st.enter_context(nc.psum_tensor("l_t", [P, 2, 512], F32))
        const, w_in, b_in, w_ps, w_sb, r_init = (sem(n) for n in ("const", "w_in", "b_in", "w_ps", "w_sb", "r_init"))
        (x_in, qkv_ps, qkv_sb, kv_done, t_ps, prod_done, s_ps, s_sb, q_ps, q_sb, c_ps, sum_done, out_done, o_ps, o_sb, y_ps,
         r_done, red_done) = (sems(n) for n in ("x_in", "qkv_ps", "qkv_sb", "kv_done", "t_ps", "prod_done", "s_ps", "s_sb", "q_ps",
                                                "q_sb", "c_ps", "sum_done", "out_done", "o_ps", "o_sb", "y_ps", "r_done", "red_done"))

        def blk(t, b):
            return bass.ds(t + b * PER, 1)

        def flat(ap):
            return ap.rearrange("p a d -> p (a d)")

        with nc.Block() as block:
            @block.sync
            def _(sp):
                for i, n in enumerate(("wq", "wk", "wv", "wo")):
                    sp.dma_start(w_raw[:, i], io[f"L1_{n}_w"][:, :]).then_inc(w_in, 16)
                for i, n in enumerate(("wq", "wk", "wv", "wo")):
                    to = b_qkv[:, i] if i < 3 else b_o[:, :]
                    sp.dma_start(to, io[f"L1_{n}_b"].rearrange("(a e) -> a e", a=1).broadcast_to([P, D])).then_inc(b_in, 16)
                with sp.Fori(0, PER) as t:
                    for b in range(B):
                        sp.wait_ge(qkv_ps[b], t)
                        sp.dma_start(xs[b][:, :], xT[:, bass.ds(P * t + b * L, P)]).then_inc(x_in[b], 16)

            @block.gpsimd
            def _(pool):
                pool.memset(zero[:, :], 0.0).then_inc(const, 1)
                pool.memset(tri[:, :], 1.0).then_inc(const, 1)
                pool.memset(mask[:, :, :], 1.0).then_inc(const, 1)
                for b in range(B):
                    pool.memset(S[b][:, :, :], 0.0).then_inc(const, 1)
                n = 3 + B
                for ap, base, pattern, mult in ((tri[:, :], 0, [[1, P]], -1), (mask[:, :, :], 0, [[-DH, NH], [0, DH]], 1),
                                                (mask[:, :, :], DH - 1, [[DH, NH], [0, DH]], -1)):
                    pool.wait_ge(const, n)
                    pool.affine_select(out=ap, in_=ap, compare_op=ALU.is_ge, fill=0.0, base=base, pattern=pattern,
                                       channel_multiplier=mult).then_inc(const, 1)
                    n += 1
                with pool.Fori(0, PER) as t:
                    for b in range(B):
                        pool.wait_ge(qkv_sb[b], t + 1)
                        pool.wait_ge(t_ps[b], t)
                        for i in range(2):
                            hs = slice(i * D // 2, (i + 1) * D // 2)
                            k = qkv[b][:, 1, hs].rearrange("p (h c) -> p h c", c=DH)
                            v = qkv[b][:, 2, hs].rearrange("p (h c) -> p h c", c=DH)
                            ins = pool.tensor_tensor(kv[b][:, i].rearrange("p (h e d) -> p h e d", e=DH, d=DH),
                                                     k.unsqueeze(2).broadcast_to([P, NH // 2, DH, DH]), spread(v, DH), ALU.mult)
                        ins.then_inc(kv_done[b], 1)

            @block.tensor
            def _(pe):
                pe.wait_ge(const, 6 + B)
                pe.wait_ge(w_in, 64)
                for i in range(4):
                    mm = nc.tensor.transpose(ps_a[0][:, i * D:(i + 1) * D], w_raw[:, i], ident[:, :])
                mm.then_inc(w_ps, 1)
                for b in range(B):
                    nc.tensor.matmul(ps_s[b][:, 0:D], zero[:, :], zero[:, :], start=True, stop=True)
                pe.wait_ge(w_sb, 1)
                with pe.Fori(0, PER) as t:
                    for b in range(B):
                        pe.wait_ge(x_in[b], 16 * t + 16)
                        pe.wait_ge(o_sb[b], t)
                        nc.tensor.matmul(ps_a[b][:, 0:3 * D], xs[b][:, :], wT[:, 0:3].rearrange("p a e -> p (a e)"),
                                         start=True, stop=True).then_inc(qkv_ps[b], 1)
                    for b in range(B):
                        pe.wait_ge(qkv_sb[b], t + 1)
                        nc.tensor.transpose(ps_a[b][:, 0:P], qkv[b][:, 0], ident[:, :]).then_inc(q_ps[b], 1)
                    for b in range(B):
                        pe.wait_ge(kv_done[b], t + 1)
                        if b == 0:
                            pe.wait_ge(prod_done[1], t)
                        else:
                            pe.wait_ge(prod_done[0], t + 1)
                        for i in range(2):
                            mm = nc.tensor.matmul(ps_t[:, i], tri[:, :], kv[b][:, i], start=True, stop=True)
                        mm.then_inc(t_ps[b], 1)
                        pe.wait_ge(q_sb[b], t + 1)
                        pe.wait_ge(r_done[b], t)
                        nc.tensor.matmul(ps_c[b][:, 0:D], qT[b][:, :], S[b][:, :, :].rearrange("p h c -> p (h c)"),
                                         start=True, stop=True).then_inc(c_ps[b], 1)
                        pe.wait_ge(s_sb[b], t)
                        nc.tensor.matmul(ps_s[b][:, 0:D], qkv[b][:, 1], qkv[b][:, 2], start=False, stop=True,
                                         skip_group_check=True).then_inc(s_ps[b], 1)
                    for b in range(B):
                        pe.wait_ge(out_done[b], t + 1)
                        nc.tensor.transpose(ps_a[b][:, 0:P], out[b][:, :], ident[:, :]).then_inc(o_ps[b], 1)
                    for b in range(B):
                        pe.wait_ge(o_sb[b], t + 1)
                        nc.tensor.matmul(ps_c[b][:, 0:D], oT[b][:, :], wT[:, 3], start=True, stop=True).then_inc(y_ps[b], 1)

            @block.scalar
            def _(act):
                act.wait_ge(w_ps, 1)
                act.activation(wT[:, :, :].rearrange("p a e -> p (a e)"), ps_a[0][:, :], ACT.Copy).then_inc(w_sb, 1)
                with act.Fori(0, PER) as t:
                    for b in range(B):
                        act.wait_ge(q_ps[b], t + 1)
                        act.activation(qT[b][:, :], ps_a[b][:, 0:P], ACT.Copy).then_inc(q_sb[b], 1)
                    for b in range(B):
                        act.wait_ge(o_ps[b], t + 1)
                        act.activation(oT[b][:, :], ps_a[b][:, 0:P], ACT.Copy).then_inc(o_sb[b], 1)

            @block.vector
            def _(dve):
                dve.wait_ge(b_in, 64)
                dve.wait_ge(const, 6 + B)
                for b in range(B):
                    s = slice(b * PER, (b + 1) * PER)
                    nc.vector.tensor_tensor(r[:, s], x[:, s], b_o[:, :].unsqueeze(1).broadcast_to([P, PER, D]), ALU.add)\
                        .then_inc(r_init, 1)
                dve.wait_ge(r_init, B)
                with dve.Fori(0, PER) as t:
                    for b in range(B):
                        dve.wait_ge(qkv_ps[b], t + 1)
                        dve.wait_ge(kv_done[b], t)
                        nc.vector.tensor_tensor(qkv[b][:, :, :], ps_a[b][:, 0:3 * D].rearrange("p (a e) -> p a e", a=3),
                                                b_qkv[:, :, :], ALU.add).then_inc(qkv_sb[b], 1)
                    for b in range(B):
                        dve.wait_ge(t_ps[b], t + 1)
                        for i in range(2):
                            q = qkv[b][:, 0, i * D // 2:(i + 1) * D // 2].rearrange("p (h c) -> p h c", c=DH)
                            ins = nc.vector.tensor_tensor(prod[b][:, i].rearrange("p (h e d) -> p h e d", e=DH, d=DH),
                                                          ps_t[:, i].rearrange("p (h e d) -> p h e d", e=DH, d=DH),
                                                          q.unsqueeze(2).broadcast_to([P, NH // 2, DH, DH]), ALU.mult)
                        ins.then_inc(prod_done[b], 1)
                        dve.wait_ge(s_ps[b], t + 1)
                        dve.wait_ge(c_ps[b], t + 1)
                        nc.vector.tensor_tensor(S[b][:, :, :], ps_s[b][:, 0:D].rearrange("p (h c) -> p h c", c=DH), mask[:, :, :],
                                                ALU.mult).then_inc(s_sb[b], 1)
                        dve.wait_ge(prod_done[b], t + 1)
                        nc.vector.tensor_reduce(intra[b][:, :], prod[b][:, :, :].rearrange("p i (g d) -> p (i g) d", d=DH), AX.X,
                                                ALU.add).then_inc(red_done[b], 1)
                    for b in range(B):
                        dve.wait_ge(red_done[b], t + 1)
                        nc.vector.tensor_tensor(out[b][:, :], intra[b][:, :], ps_c[b][:, 0:D], ALU.add).then_inc(out_done[b], 1)
                    for b in range(B):
                        dve.wait_ge(y_ps[b], t + 1)
                        nc.vector.tensor_tensor(flat(r[:, blk(t, b)]), flat(r[:, blk(t, b)]), ps_c[b][:, 0:D], ALU.add)\
                            .then_inc(r_done[b], 1)


_INS = ["L0_attn_hidden_states", "L0_attn_conv_w", "L0_attn_Wq", "L0_attn_Wk", "L0_attn_Wv", "L0_attn_Wb", "L0_attn_Wg",
        "L0_attn_norm_w", "L0_attn_Wo", "L0_ffn_gate_w", "L0_ffn_w1", "L0_ffn_b1", "L0_ffn_w2", "L0_ffn_b2",
        "L1_attn_wq_w", "L1_attn_wq_b", "L1_attn_wk_w", "L1_attn_wk_b", "L1_attn_wv_w", "L1_attn_wv_b",
        "L1_attn_wo_w", "L1_attn_wo_b", "L1_ffn_Wr", "L1_ffn_br", "L1_ffn_W1", "L1_ffn_W3", "L1_ffn_W2"]


def build(nc, io):
    TAKEN.clear()
    io["kb_dram"] = nc.dram_tensor("kb_dram", [B * L, QK + H], F32, kind="Internal").ap()
    io["t_dram"] = nc.dram_tensor("t_dram", [B * L, H * SUB], F32, kind="Internal").ap()
    with ExitStack() as ctx:
        def keep(name, shp):
            return ctx.enter_context(nc.sbuf_tensor(name, shp, F32))

        sb = {"ident": keep("ident", [P, P]), "r": keep("r", [P, BLOCKS, D])}
        with ExitStack() as delta:
            def held(name, shp):
                return delta.enter_context(nc.sbuf_tensor(name, shp, F32))

            sb["tok"] = held("tok", [P, BLOCKS, TOKW])
            sb["gate"] = held("gate", [P, BLOCKS, D])
            sb["kp"] = held("kp", [P, CH, QK + H])
            stage_project(nc, io, sb, delta)
            if LAST_STAGE >= 2:
                sb["tinv"] = held("tinv", [P, BLOCKS, H * SUB])
                stage_invert(nc, io, sb, delta)
            if LAST_STAGE >= 3:
                sb["o"] = held("o", [P, BLOCKS, D])
                stage_delta(nc, io, sb, delta)
            if LAST_STAGE >= 4:
                stage_close_delta(nc, io, sb, delta)
        give_back(nc)
        if LAST_STAGE < 5:
            return
        for w, steps in enumerate(STEPS):
            io[f"rows{w}"] = nc.dram_tensor(f"rows{w}_dram", [(steps + AHEAD) * P, D], F32, kind="Internal").ap()
            io[f"outs{w}"] = nc.dram_tensor(f"outs{w}_dram", [(steps + 1) * P, D], F32, kind="Internal").ap()
        F0, F1 = io["L0_ffn_w1"].shape[2], io["L1_ffn_W1"].shape[2]
        w = {"wa": keep("wa", [D, E, F0]), "wb": keep("wb", [P, E * (F0 // P), D]), "b1": keep("b1", [P, E, F0]), "b2": keep("b2", [P, E, D])}
        v = {"wa": keep("va", [D, E, F1]), "wc": keep("vc", [D, E, F1]), "wb": keep("vb", [P, E * (F1 // P), D])}
        zero = keep("zero", [P, D])
        w_in, v_in, zeroed = stage_weights(nc, io, w, v, zero)
        sb["x"], sb["logits"] = keep("x", [P, BLOCKS, D]), keep("logits", [P, BLOCKS, E])
        sb["weight"] = [keep(f"weight{i}", [P, BLOCKS]) for i in range(2)]
        for name, shp, dt in (("slot0", [P, BLOCKS], U32), ("slot1", [P, BLOCKS], U32), ("expert_of", [P, STEPS[1] + AHEAD], I32)):
            sb[name] = ctx.enter_context(nc.sbuf_tensor(name, shp, dt))
        sb["slot"] = [sb["slot0"], sb["slot1"]]
        stage_norm(nc, io, sb, "n0", io["L0_ffn_gate_w"])
        if LAST_STAGE < 6:
            return
        stage_route(nc, io, sb, "g0", 1, io["rows0"], zeroed[0])
        stage_tiles(nc, io, sb, "e0", False, io["rows0"], io["outs0"], w_in, **w)
        stage_combine(nc, io, sb, "c0", 1, io["outs0"], pending=((v_in, 16 * 3), (zeroed[1], 16)))
        give_back(nc)
        if LAST_STAGE < 7:
            return
        with ExitStack() as attention:
            sb["xT"] = attention.enter_context(nc.sbuf_tensor("xT_all", [D, B * L], F32))
            stage_norm(nc, io, sb, "n1", io["L1_ffn_Wr"])
            if LAST_STAGE < 8:
                return
            stage_linear_attention(nc, io, sb)
            del sb["xT"]
        give_back(nc)
        if LAST_STAGE < 9:
            return
        stage_norm(nc, io, sb, "n2", io["L1_ffn_Wr"])
        if LAST_STAGE < 10:
            return
        stage_route(nc, io, sb, "g1", 2, io["rows1"], None, bias=io["L1_ffn_br"])
        stage_tiles(nc, io, sb, "e1", True, io["rows1"], io["outs1"], None, **v)
        stage_combine(nc, io, sb, "c1", 2, io["outs1"])
        if LAST_STAGE >= 11:
            give_back(nc)
            stage_norm(nc, io, sb, "n3")


def stage_weights(nc, io, w, v, zero):
    w_in, v_in, zeroed, const = take(nc, "m_w_in"), take(nc, "m_v_in"), [take(nc, f"zeroed{i}") for i in range(2)], take(nc, "zero_set")

    def zero_rows(sp, i):
        to = io[f"rows{i}"].rearrange("(n p) d -> p n d", p=P)
        sp.dma_start(to, zero[:, :].unsqueeze(1).broadcast_to([P, STEPS[i] + AHEAD, D])).then_inc(zeroed[i], 16)

    with nc.Block() as block:
        @block.gpsimd
        def _(pool):
            pool.memset(zero[:, :], 0.0).then_inc(const, 1)

        @block.sync
        def _(sp):
            sp.wait_ge(const, 1)
            zero_rows(sp, 0)
            for to, name in ((w["b1"], "L0_ffn_b1"), (w["b2"], "L0_ffn_b2")):
                sp.dma_start(to[:, :, :], io[name].unsqueeze(0).broadcast_to([P, *io[name].shape])).then_inc(w_in, 16)
            sp.dma_start(w["wa"][:, :, :], io["L0_ffn_w1"].rearrange("e d f -> d e f")).then_inc(w_in, 16)
            sp.dma_start(w["wb"][:, :, :], io["L0_ffn_w2"].rearrange("e (f p) d -> p (e f) d", p=P)).then_inc(w_in, 16)
            sp.dma_start(v["wa"][:, :, :], io["L1_ffn_W1"].rearrange("e d f -> d e f")).then_inc(v_in, 16)
            sp.dma_start(v["wc"][:, :, :], io["L1_ffn_W3"].rearrange("e d f -> d e f")).then_inc(v_in, 16)
            sp.dma_start(v["wb"][:, :, :], io["L1_ffn_W2"].rearrange("e (f p) d -> p (e f) d", p=P)).then_inc(v_in, 16)
            zero_rows(sp, 1)
    return w_in, v_in, zeroed


LAST_STAGE = 99


def kernel(**inputs):
    import numpy as _np
    import concourse.bacc as _bacc
    from concourse.bass_utils import run_bass_kernel_spmd as _run

    nc = _bacc.Bacc("TRN2", target_bir_lowering=False, num_devices=1)
    arrays, io = {}, {}
    for name in _INS:
        a = _np.ascontiguousarray(inputs[name])
        arrays[f"in_{name}"] = a
        short = name.replace("_attn_", "_").replace("L0_hidden_states", "x")
        io[short] = nc.dram_tensor(f"in_{name}", a.shape, mybir.dt.from_np(a.dtype), kind="ExternalInput").ap()
    io["out"] = nc.dram_tensor("out_0", (B, L, D), F32, kind="ExternalOutput").ap()
    build(nc, io)
    r = _run(nc, [arrays], core_ids=[0])
    return r.results[0]["out_0"]
```

```python
from contextlib import ExitStack

import concourse.bass as bass
from concourse import mybir

F32 = mybir.dt.float32
U32 = mybir.dt.uint32
I32 = mybir.dt.int32
ALU = mybir.AluOpType
ACT = mybir.ActivationFunctionType
AX = mybir.AxisListType

P = 128
B, L, D = 2, 2048, 128
BLOCKS = B * L // P
PER = BLOCKS // B
H, DK, DV = 4, 16, 32
QK = H * DK
CH = 32
SUB = 16
NC = P // CH
KC = 3
WID = 2 * QK + 2 * D + H

RW = DV + DK
C_R, C_K = 0, H * RW
C_B, C_Q, C_KB = C_K + QK, C_K + QK + H, C_K + 2 * QK + H
TOKW = C_KB + QK
E = 8
EPS = 1e-5
ROWK, ROWQ, ROWKB, ROWW = 0, C_Q - C_K, C_KB - C_K, TOKW - C_K
YW = H * RW + P - RW


def spread(ap, n):
    return ap.unsqueeze(len(ap.shape)).broadcast_to([*ap.shape, n])


TAKEN = []


def take(nc, name):
    TAKEN.append(nc.alloc_semaphore(name))
    return TAKEN[-1]


def give_back(nc):
    with nc.Block() as block:
        @block.gpsimd
        def _(pool):
            nc.clear_and_free_semaphores(TAKEN)
    TAKEN.clear()


def kq_rows(tok, at):
    return tok[:, at, C_K:C_K + 2 * (QK + H)].rearrange("p n (a c) -> p n a c", a=2)[:, :, :, 0:QK]


def run_steps(eng, steps, step):
    step(0, True, False)
    with eng.Fori(1, steps - 1) as t:
        step(t, False, False)
    step(steps - 1, False, True)


def stage_project(nc, io, sb, ctx):
    with ExitStack() as st:
        def tmp(name, shp):
            return st.enter_context(nc.sbuf_tensor(name, shp, F32))

        def sem(name):
            return take(nc, name)

        xst = tmp("xst", [P, B, 4, D])
        xT = tmp("xT", [D, B, KC + L])
        conv = tmp("conv", [D, B, 512])
        hT = tmp("hT", [D, B, 512])
        wall = tmp("wall", [D, WID])
        cw = tmp("cw", [D, KC + 1])
        sq = tmp("sq", [P, 2, 2, 2 * QK])
        n2 = tmp("n2", [P, BLOCKS, 2 * H])
        rn = tmp("rn", [P, BLOCKS, 2 * H])
        bl = tmp("bl", [P, BLOCKS, H])
        th = tmp("th", [P, BLOCKS, H])
        psT = [st.enter_context(nc.psum_tensor(f"p_psT{b}", [P, 512], F32)) for b in range(B)]
        psG = [st.enter_context(nc.psum_tensor(f"p_psG{b}", [P, 4, D], F32)) for b in range(B)]
        psP = [st.enter_context(nc.psum_tensor(f"p_psP{i}", [P, 2, 512], F32)) for i in range(2)]

        w_in, cw_in, v_copied = sem("w_in"), sem("cw_in"), sem("v_copied")
        x_in, const = [sem(f"x_in{b}") for b in range(B)], sem("p_const")
        xT_ps, xT_sb = sem("xT_ps"), sem("xT_sb")
        conv_do, conv_done, h_done = [sem(f"conv_do{b}") for b in range(B)], sem("conv_done"), sem("h_done")
        proj, gate_ps, sq_done, gate_done, kq_done, n2_done = (
            sem(n) for n in ("proj", "gate_ps", "sq_done", "gate_done", "kq_done", "n2_done"))
        v_step, a_step, g_step, stored = sem("pv_step"), sem("pa_step"), sem("pg_step"), sem("p_stored")

        x_dram = io["x"].rearrange("b (t k p) d -> p b t k d", p=P, k=4)
        tok, gate, ident = sb["tok"], sb["gate"], sb["ident"]

        with nc.Block() as block:
            @block.sync
            def _(sp):
                for b in range(B):
                    sp.dma_start(xst[:, b], x_dram[:, b, 0]).then_inc(x_in[b], 16)
                sp.dma_start(cw[:, :], io["L0_conv_w"][:, :]).then_inc(cw_in, 16)
                for n, c in (("L0_Wk", 0), ("L0_Wq", QK), ("L0_Wv", 2 * QK), ("L0_Wb", 2 * QK + D), ("L0_Wg", 2 * QK + D + H)):
                    sp.dma_start(wall[:, c:c + io[n].shape[1]], io[n][:, :]).then_inc(w_in, 16)
                with sp.Fori(1, PER // 4) as t:
                    for b in range(B):
                        sp.wait_ge(xT_ps, 2 * t - 1 + b)
                        sp.dma_start(xst[:, b], x_dram[:, b, bass.ds(t, 1)].rearrange("p a k d -> p (a k) d")).then_inc(x_in[b], 16)
                sp.wait_ge(v_step, 4)
                sp.dma_start(io["kb_dram"].rearrange("(n p) c -> p n c", p=P), tok[:, :, C_K:C_K + QK + H]).then_inc(stored, 16)
                sp.wait_ge(stored, 16)
                sp.dma_start(sb["kp"][:, :, :], io["kb_dram"].rearrange("(p i) c -> p i c", i=CH)).then_inc(stored, 16)
                sp.wait_ge(stored, 32)

            @block.gpsimd
            def _(pool):
                pool.memset(ident[:, :], 0.0).then_inc(g_step, 1)
                pool.wait_ge(g_step, 1)
                pool.affine_select(out=ident[:, :], in_=ident[:, :], compare_op=ALU.not_equal, fill=1.0,
                                   base=0, pattern=[[-1, P]], channel_multiplier=1).then_inc(const, 1)
                pool.memset(xT[:, :, 0:KC], 0.0).then_inc(const, 1)
                pool.wait_ge(v_step, 4)
                for b in range(B):
                    s = slice(b * PER, (b + 1) * PER)
                    r = tok[:, s, C_R:C_R + H * RW].rearrange("p n (h c) -> p n h c", h=H)
                    pool.tensor_tensor(r[:, :, :, 0:DV], r[:, :, :, 0:DV],
                                       spread(tok[:, s, C_B:C_B + H], DV), ALU.mult).then_inc(g_step, 1)

            @block.tensor
            def _(pe):
                def transpose(t, b, first=False):
                    pe.wait_ge(x_in[b], t * 16 + 16)
                    if not first:
                        pe.wait_ge(xT_sb, 2 * t - 1 + b)
                    for k in range(4):
                        mm = nc.tensor.transpose(psT[b][:, k * P:(k + 1) * P], xst[:, b, k], ident[:, :])
                    mm.then_inc(xT_ps, 1)

                def project(t, b, first):
                    pe.wait_ge(h_done, 2 * t + b + 1)
                    for half in range(2):
                        if not (first and b == 0):
                            pe.wait_ge(v_copied, 4 * t + 2 * b + half - 1)
                        for j in range(2):
                            k = 2 * half + j
                            mm = nc.tensor.matmul(psP[half][:, j, 0:WID - D], hT[:, b, k * P:(k + 1) * P],
                                                  wall[:, 0:WID - D], start=True, stop=True)
                        mm.then_inc(proj, 1)
                    if not first:
                        pe.wait_ge(gate_done, 2 * t + b - 1)
                    for k in range(4):
                        mm = nc.tensor.matmul(psG[b][:, k], hT[:, b, k * P:(k + 1) * P], wall[:, WID - D:WID],
                                              start=True, stop=True)
                    mm.then_inc(gate_ps, 1)

                def step(t, first, last):
                    if not last:
                        for b in range(B):
                            transpose(t + 1, b)
                    for b in range(B):
                        project(t, b, first)

                pe.wait_ge(const, 2)
                for b in range(B):
                    transpose(0, b, first=True)
                pe.wait_ge(w_in, 16 * 5)
                run_steps(pe, PER // 4, step)

            @block.scalar
            def _(act):
                def copy_x(t, b):
                    act.wait_ge(xT_ps, 2 * t + b + 1)
                    act.activation(xT[:, b, bass.ds(t * 512 + KC, 512)], psT[b][:, :], ACT.Copy).then_inc(xT_sb, 1)

                def step(t, first, last):
                    for b in range(B):
                        act.wait_ge(conv_done, 2 * t + b + 1)
                        if not first:
                            act.wait_ge(gate_ps, 2 * t + b - 1)
                        act.activation(hT[:, b], conv[:, b], ACT.Silu).then_inc(h_done, 1)
                    if not last:
                        for b in range(B):
                            copy_x(t + 1, b)
                    for b in range(B):
                        for half in range(2):
                            n = 4 * t + 2 * b + half
                            at = bass.ds(4 * t + (b * PER + 2 * half), 2)
                            act.wait_ge(kq_done, n + 1)
                            r = tok[:, at, C_R:C_R + H * RW].rearrange("p n (h c) -> p n h c", h=H)
                            for j in range(2):
                                ins = act.activation(r[:, j, :, 0:DV], psP[half][:, j, 2 * QK:2 * QK + D].rearrange("p (h c) -> p h c", h=H),
                                                     ACT.Copy)
                            ins.then_inc(v_copied, 1)
                            if not (first and b == 0):
                                act.wait_ge(n2_done, n - 1)
                            act.activation(sq[:, half].rearrange("p n (a c) -> p n a c", a=2), kq_rows(tok, at), ACT.Square)\
                                .then_inc(sq_done, 1)
                        act.wait_ge(gate_ps, 2 * t + b + 1)
                        act.activation(gate[:, bass.ds(4 * t + b * PER, 4)], psG[b][:, :, :], ACT.Silu).then_inc(gate_done, 1)

                for b in range(B):
                    copy_x(0, b)
                run_steps(act, PER // 4, step)
                act.wait_ge(kq_done, BLOCKS // 2)
                act.activation(th[:, :, :], bl[:, :, :], ACT.Tanh, scale=0.5).then_inc(a_step, 1)
                act.wait_ge(v_step, 1)
                act.activation(rn[:, :, :], n2[:, :, :], ACT.Sqrt).then_inc(a_step, 1)

            @block.vector
            def _(dve):
                def rows(t, u):
                    return bass.ds(4 * t + (u // 2 * PER + 2 * (u % 2)), 2)

                def convolve(t, first=False):
                    for b in range(B):
                        dve.wait_ge(xT_sb, 2 * t + b + 1)
                        if not first:
                            dve.wait_ge(h_done, 2 * t + b - 1)
                        nc.vector.tensor_scalar(conv[:, b], xT[:, b, bass.ds(t * 512, 512)], cw[:, 0:1], None,
                                                ALU.mult).then_inc(conv_do[b], 1)
                    for i in range(1, KC + 1):
                        for b in range(B):
                            dve.wait_ge(conv_do[b], t * KC + i)
                            nc.vector.scalar_tensor_tensor(conv[:, b], xT[:, b, bass.ds(t * 512 + i, 512)], cw[:, i:i + 1],
                                                           conv[:, b], ALU.mult, ALU.add)\
                                .then_inc(conv_do[b] if i < KC else conv_done, 1)

                def step(t, first, last):
                    if not last:
                        convolve(t + 1)
                    for u in range(2 * B + 1):
                        if u < 2 * B:
                            at, ps = rows(t, u), psP[u % 2]
                            dve.wait_ge(proj, 4 * t + u + 1)
                            nc.vector.tensor_copy(kq_rows(tok, at), ps[:, :, 0:2 * QK].rearrange("p n (a c) -> p n a c", a=2))
                            nc.vector.tensor_copy(bl[:, at], ps[:, :, 2 * QK + D:WID - D]).then_inc(kq_done, 1)
                        if u:
                            dve.wait_ge(sq_done, 4 * t + u)
                            nc.vector.tensor_reduce(n2[:, rows(t, u - 1)], sq[:, (u - 1) % 2].rearrange("p n (h c) -> p (n h) c", c=DK),
                                                    AX.X, ALU.add).then_inc(n2_done, 1)

                dve.wait_ge(cw_in, 16)
                dve.wait_ge(const, 2)
                convolve(0, first=True)
                run_steps(dve, PER // 4, step)
                dve.wait_ge(n2_done, BLOCKS // 2)
                nc.vector.tensor_scalar(n2[:, :, :], n2[:, :, :], 1e-24, None, ALU.max).then_inc(v_step, 1)
                dve.wait_ge(a_step, 2)
                nc.vector.reciprocal(n2[:, :, :], rn[:, :, :])
                nc.vector.tensor_scalar(tok[:, :, C_B:C_B + H], th[:, :, :], 0.5, 0.5, ALU.mult, ALU.add).then_inc(v_step, 1)
                dve.wait_ge(v_step, 2)
                for b in range(B):
                    s = slice(b * PER, (b + 1) * PER)
                    k = tok[:, s, C_K:C_K + QK].rearrange("p n (h c) -> p n h c", h=H)
                    last = nc.vector.tensor_tensor(k, k, spread(n2[:, s, 0:H], DK), ALU.mult)
                    last.then_inc(v_step, 1)
                for b in range(B):
                    s = slice(b * PER, (b + 1) * PER)
                    q = tok[:, s, C_Q:C_Q + QK].rearrange("p n (h c) -> p n h c", h=H)
                    nc.vector.tensor_tensor(q, q, spread(n2[:, s, H:2 * H], DK), ALU.mult)
                dve.wait_ge(v_step, 4)
                for b in range(B):
                    s = slice(b * PER, (b + 1) * PER)
                    k = tok[:, s, C_K:C_K + QK].rearrange("p n (h c) -> p n h c", h=H)
                    beta = spread(tok[:, s, C_B:C_B + H], DK)
                    nc.vector.tensor_tensor(tok[:, s, C_KB:C_KB + QK].rearrange("p n (h c) -> p n h c", h=H), k, beta, ALU.mult)
                    r = tok[:, s, C_R:C_R + H * RW].rearrange("p n (h c) -> p n h c", h=H)
                    nc.vector.tensor_tensor(r[:, :, :, DV:RW], k, beta, ALU.mult)


def delta_memory(nc, ctx):
    def tmp(name, shp):
        return ctx.enter_context(nc.sbuf_tensor(name, shp, F32))

    def pair(name, shp):
        return [tmp(f"{name}{b}", shp) for b in range(B)]

    return {
        "row": pair("d_row", [P, ROWW]),
        "kT": pair("kT", [P, P]),
        "qkx": pair("qkx", [P, NC, H, 2, CH]),
        "tbd": pair("tbd", [P, H, P // SUB, SUB]),
        "kc": pair("kc", [P, NC, QK]),
        "pa": pair("pa", [P, H, 2, P]),
        "y0": pair("y0", [P, YW]), "zz": pair("zz", [P, YW]), "uw": pair("uw", [P, YW]),
        "oi": pair("oi", [P, H, DV]), "w": pair("w", [P, QK]),
        "qe": tmp("qe", [P, B, QK]),
        "qeT": pair("qeT", [P, P]),
        "mt": tmp("mt", [P, NC, B, QK]),
        "S": pair("S", [P, H, DV]),
        "mask_g": tmp("mask_g", [P, 2, P]), "mask_bh": tmp("mask_bh", [P, B, H]), "mask_h": tmp("mask_h", [P, H]),
        "mask_m": tmp("mask_m", [P, H, DK]), "mask_c": tmp("mask_c", [P, NC]), "mask_s": tmp("mask_s", [P, P // SUB]),
        "zero": tmp("d_zero", [P, P]),
        "const": take(nc, "d_const"),
    }


DELTA_CONST = 16


def set_up_delta(pool, mem):
    N16 = P // SUB
    const, S, mt, qe, zero = (mem[n] for n in ("const", "S", "mt", "qe", "zero"))
    kT, qkx, qeT, y0, zz, uw = (mem[n] for n in ("kT", "qkx", "qeT", "y0", "zz", "uw"))
    mask_g, mask_bh, mask_c, mask_s = (mem[n] for n in ("mask_g", "mask_bh", "mask_c", "mask_s"))
    made = 6

    def keep_where(ap, base, pattern, mult):
        nonlocal made
        pool.wait_ge(const, made)
        pool.affine_select(out=ap, in_=ap, compare_op=ALU.is_ge, fill=0.0, base=base, pattern=pattern,
                           channel_multiplier=mult).then_inc(const, 1)
        made += 1

    pool.memset(zero[:, :], 0.0)
    for whole in (S[0], S[1], mt, qe):
        pool.memset(whole[:], 0.0)
    for b in range(B):
        for whole in (kT[b], qkx[b], qeT[b], y0[b], zz[b], uw[b]):
            pool.memset(whole[:], 0.0)
    for m, v in ((mask_g, 0.0), (mask_bh, 1.0), (mask_c, 1.0), (mask_s, 1.0)):
        pool.memset(m[:], v).then_inc(const, 1)
    pool.wait_ge(const, 4)
    off = mask_g[:, 1].rearrange("p (c i) -> p c i", c=NC)
    cau = mask_g[:, 0].rearrange("p (c i) -> p c i", c=NC)
    pool.memset(off[:, :, SUB:CH], 1.0).then_inc(const, 1)
    pool.memset(cau, 1.0).then_inc(const, 1)
    keep_where(off, 0, [[-CH, NC], [0, CH]], 1)
    keep_where(off, SUB - 1, [[CH, NC], [0, CH]], -1)
    keep_where(cau, 0, [[-CH, NC], [0, CH]], 1)
    keep_where(cau, 0, [[CH, NC], [1, CH]], -1)
    keep_where(mask_bh[:, :, :], 0, [[-QK, B], [-DK, H]], 1)
    keep_where(mask_bh[:, :, :], DK - 1, [[QK, B], [DK, H]], -1)
    keep_where(mask_c[:, :], 0, [[-CH, NC]], 1)
    keep_where(mask_c[:, :], CH - 1, [[CH, NC]], -1)
    keep_where(mask_s[:, :], 0, [[-SUB, N16]], 1)
    keep_where(mask_s[:, :], SUB - 1, [[SUB, N16]], -1)


def stage_invert(nc, io, sb, mem):
    SU = CH // SUB
    with ExitStack() as st:
        def tmp(name, shp):
            return st.enter_context(nc.sbuf_tensor(name, shp, F32))

        def sem(name):
            return take(nc, name)

        kp = sb["kp"]
        kb = tmp("kb", [P, CH, QK])
        prod = [tmp(f"i_prod{i}", [P, SU, SUB, QK]) for i in range(2)]
        nA = tmp("nA", [P, SU, H, SUB, SUB])
        T = tmp("T", [P, SU, H, SUB, SUB])
        nw = tmp("nw", [P, DV])
        TT = tmp("TT", [P, SU, SUB, H, SUB])
        chain, mul_v, mul_g, red, t_ready, stored, fwd, nw_in = (sem(n) for n in (
            "i_chain", "mul_v", "mul_g", "red", "t_ready", "i_stored", "fwd", "nw_in"))
        t_flat, a_flat = (x.rearrange("p c h i j -> p (c h) i j") for x in (T[:, :, :, :, :], nA[:, :, :, :, :]))
        p_flat = prod[0][:, :, :, :].rearrange("p c i f -> p (c i f)")

        def lagged(eng, lag, signal):
            n = SUB - lag
            for c in range(SU):
                i0 = c * SUB
                ins = eng.tensor_tensor(prod[lag % 2][:, c, 0:n], kb[:, i0 + lag:i0 + SUB], kp[:, i0:i0 + n, 0:QK], ALU.mult)
            ins.then_inc(signal, 1)

        with nc.Block() as block:
            @block.gpsimd
            def _(pool):
                pool.memset(T[:, :, :, :, :], 0.0).then_inc(chain, 1)
                pool.wait_ge(chain, 1)
                pool.memset(T[:, :, :, :, :].rearrange("p c h i j -> p (c h) (i j)")[:, :, 0:SUB * SUB:SUB + 1], 1.0).then_inc(chain, 1)
                pool.wait_ge(mul_v, 1)
                for lag in range(2, SUB, 2):
                    if lag > 2:
                        pool.wait_ge(red, lag - 2)
                    lagged(nc.gpsimd, lag, mul_g)
                set_up_delta(pool, mem)
                pool.wait_ge(nw_in, 16)
                for b in range(B):
                    g = sb["gate"][:, b * PER:(b + 1) * PER].rearrange("p n (h c) -> p (n h) c", c=DV)
                    pool.tensor_tensor(g, g, nw[:, :].unsqueeze(1).broadcast_to([P, PER * H, DV]), ALU.mult).then_inc(chain, 1)

            @block.vector
            def _(dve):
                for h in range(H):
                    last = nc.vector.scalar_tensor_tensor(kb[:, :, h * DK:(h + 1) * DK], kp[:, :, h * DK:(h + 1) * DK], -1.0,
                                                          spread(kp[:, :, QK + h], DK), ALU.mult, ALU.mult)
                last.then_inc(mul_v, 1)
                dve.wait_ge(mul_v, 1)
                for lag in range(1, SUB):
                    n = SUB - lag
                    if lag % 2:
                        if lag > 2:
                            dve.wait_ge(red, lag - 2)
                        lagged(nc.vector, lag, mul_v)
                        dve.wait_ge(mul_v, 1 + (lag + 1) // 2)
                    else:
                        dve.wait_ge(mul_g, lag // 2)
                    for c in range(SU):
                        out = nA[:, c].rearrange("p h i j -> p h (i j)")[:, :, lag * SUB:(n + lag - 1) * SUB + n:SUB + 1]
                        ins = nc.vector.tensor_reduce(out.rearrange("p h i -> p i h"),
                                                      prod[lag % 2][:, c, 0:n].rearrange("p i (h d) -> p i h d", h=H), AX.X, ALU.add)
                    ins.then_inc(red, 1)
                dve.wait_ge(red, SUB - 1)
                dve.wait_ge(chain, 2)
                for i in range(1, SUB):
                    out = p_flat[:, 0:SU * H * i * i].rearrange("p (g j m) -> p g j m", j=i, m=i)
                    nc.vector.tensor_tensor(out, a_flat[:, :, i:i + 1, 0:i].broadcast_to([P, SU * H, i, i]),
                                            t_flat[:, :, 0:i, 0:i].rearrange("p g m j -> p g j m"), ALU.mult).then_inc(fwd, 1)
                    dve.wait_ge(fwd, 2 * i - 1)
                    nc.vector.tensor_reduce(t_flat[:, :, i, 0:i], out, AX.X, ALU.add).then_inc(fwd, 1)
                    dve.wait_ge(fwd, 2 * i)
                for c in range(SU):
                    nc.vector.tensor_copy(TT[:, c], T[:, c].rearrange("p h i j -> p j h i")).then_inc(t_ready, 1)

            @block.sync
            def _(sp):
                sp.dma_start(nw[:, :], io["L0_norm_w"].rearrange("(a n) -> a n", a=1).broadcast_to([P, DV])).then_inc(nw_in, 16)
                sp.wait_ge(t_ready, SU)
                sp.dma_start(io["t_dram"].rearrange("(p i) c -> p (i c)", i=CH), TT[:, :, :, :, :].rearrange("p c j h i -> p (c j h i)")).then_inc(stored, 16)
                sp.wait_ge(stored, 16)
                sp.dma_start(sb["tinv"][:, :, :], io["t_dram"].rearrange("(n p) c -> p n c", p=P)).then_inc(stored, 16)
                sp.wait_ge(stored, 32)


def stage_delta(nc, io, sb, mem):
    N16, HR = P // SUB, H * RW
    with ExitStack() as st:
        def sem(name):
            return take(nc, name)

        def sems(name):
            return [sem(f"{name}{b}") for b in range(B)]

        def bank(name):
            return st.enter_context(nc.psum_tensor(name, [P, 512], F32))

        tok, tinv, o, ident = sb["tok"], sb["tinv"], sb["o"], sb["ident"]
        row, kT, qkx, tbd, kc, pa, y0, zz, uw, oi, w, qe, qeT, mt, S, mask_g, mask_bh, mask_h, mask_m, mask_c, mask_s, zero = (
            mem[n] for n in ("row", "kT", "qkx", "tbd", "kc", "pa", "y0", "zz", "uw", "oi", "w", "qe", "qeT", "mt", "S", "mask_g",
                             "mask_bh", "mask_h", "mask_m", "mask_c", "mask_s", "zero"))
        psT, psG, psY = ([bank(f"d_ps{n}{b}") for b in range(B)] for n in "TGY")
        acc, psX = bank("d_acc"), bank("d_psX")

        const, mask_step = mem["const"], sem("mask_step")
        loaded, t_ps, kq_sb, expanded, kc_done, g_ps, pa_done, y_ps, y_used, w_done = (sems(n) for n in (
            "d_loaded", "t_ps", "kq_sb", "expanded", "kc_done", "g_ps", "pa_done", "y_ps", "y_used", "w_done"))
        qt_ps, qt_sb, m_ps, m_done, s_ps, s_sb, o_ps, o_done = (sem(n) for n in (
            "qt_ps", "qt_sb", "m_ps", "m_done", "s_ps", "s_sb", "o_ps", "o_done"))

        def by_head(t):
            return t[:, 0:HR].rearrange("p (h c) -> p h c", h=H)

        def heads(ps):
            return ps[:, :].rearrange("p (h c) -> p h c", h=H)[:, :, 0:RW]

        def blk(t, b):
            return bass.ds(t + b * PER, 1)

        def run(eng, step):
            step(0, True)
            with eng.Fori(1, PER) as t:
                step(t, False)

        with nc.Block() as block:
            @block.sync
            def _(sp):
                for b in range(B):
                    sp.dma_start(row[b][:, :], tok[:, b * PER, C_K:TOKW]).then_inc(loaded[b], 16)
                with sp.Fori(1, PER) as t:
                    for b in range(B):
                        sp.wait_ge(t_ps[b], t)
                        sp.dma_start(row[b][:, :], tok[:, blk(t, b), C_K:TOKW].rearrange("p a c -> p (a c)"))\
                            .then_inc(loaded[b], 16)
                for b in range(B):
                    sp.wait_ge(t_ps[b], PER)
                    sp.dma_start(row[b][:, :], tok[:, 0, C_K:TOKW]).then_inc(loaded[b], 16)

            @block.gpsimd
            def _(pool):
                def step(t, first):
                    for b in range(B):
                        if not first:
                            pool.wait_ge(y_ps[b], 4 * t - 1)
                        src = tinv[:, blk(t, b)].rearrange("p a (h i) -> p (a h) i", h=H)
                        pool.tensor_tensor(tbd[b][:, :, :, :], src.unsqueeze(2).broadcast_to([P, H, N16, SUB]),
                                           spread(mask_s[:, :], SUB).unsqueeze(1).broadcast_to([P, H, N16, SUB]),
                                           ALU.mult).then_inc(expanded[b], 1)
                    for b in range(B):
                        if not first:
                            pool.wait_ge(s_ps, NC * t)
                        pool.tensor_tensor(kc[b][:, :, :], tok[:, blk(t, b), C_K:C_K + QK].broadcast_to([P, NC, QK]),
                                           spread(mask_c[:, :], QK), ALU.mult).then_inc(kc_done[b], 1)

                run(pool, step)

            @block.tensor
            def _(pe):
                def transpose(t, b):
                    pe.wait_ge(loaded[b], 16 * t + 16)
                    for i, c in enumerate((ROWK, ROWQ, ROWKB)):
                        n = min(P, ROWW - c)
                        mm = nc.tensor.transpose(psT[b][0:n, i * P:(i + 1) * P], row[b][:, c:c + n], ident[:, :])
                    mm.then_inc(t_ps[b], 1)

                def scores(t, b):
                    pe.wait_ge(kq_sb[b], t + 1)
                    for c in range(NC):
                        mm = nc.tensor.matmul(psG[b][c * CH:(c + 1) * CH, 0:H * 2 * CH], kT[b][:, c * CH:(c + 1) * CH],
                                              qkx[b][:, c].rearrange("p h a l -> p (h a l)"), start=True, stop=True)
                    mm.then_inc(g_ps[b], 1)

                def products(t, k, b, left, right):
                    if not (isinstance(t, int) and 4 * t + k == 0):
                        pe.wait_ge(y_used[b], 4 * t + k)
                    for h in range(H):
                        mm = nc.tensor.matmul(psY[b][:, h * P:(h + 1) * P], left(b, h), right(b, h), start=True, stop=True)
                    mm.then_inc(y_ps[b], 1)

                def inverse(b, h):
                    return tbd[b][:, h].rearrange("p s i -> p (s i)")

                def columns(of):
                    return lambda b, h: of[b][:, h * RW:h * RW + P]

                def chunk(t, c):
                    pe.wait_ge(s_sb, NC * t + c + 1)
                    s_now = S[c % 2][:, :, :].rearrange("p h c -> p (h c)")
                    nc.tensor.matmul(acc[:, 0:H * DV], mt[:, c].rearrange("p b k -> p (b k)"), s_now, start=False, stop=True,
                                     skip_group_check=True)
                    for b in range(B):
                        mm = nc.tensor.matmul(acc[b * QK:(b + 1) * QK, 0:H * DV], kc[b][:, c], by_head(uw[b])[:, :, 0:DV],
                                              start=False, stop=True, skip_group_check=True)
                    mm.then_inc(s_ps, 1)
                    for b in range(B):
                        mm = nc.tensor.matmul(psX[c * CH:(c + 1) * CH, b * H * DV:(b + 1) * H * DV],
                                              qeT[b][:, c * CH:(c + 1) * CH], s_now, start=True, stop=True)
                    if c == NC - 1:
                        mm.then_inc(o_ps, 1)

                def transpose_q(t):
                    for b in range(B):
                        pe.wait_ge(y_used[b], 4 * t + 4)
                    pe.wait_ge(m_done, t + 1)
                    nc.tensor.transpose(psX[:, 0:P], qe[:, :, :].rearrange("p b c -> p (b c)"), ident[:, :]).then_inc(qt_ps, 1)

                def step(t, first):
                    if not first:
                        transpose_q(t - 1)
                    pe.wait_ge(expanded[0], t + 1)
                    direct = lambda b, h: tok[:, blk(t, b), h * RW:h * RW + P].rearrange("p a c -> p (a c)")
                    products(t, 0, 0, inverse, direct)
                    if not first:
                        pe.wait_ge(qt_sb, t)
                        chunk(t - 1, 0)
                    pe.wait_ge(expanded[1], t + 1)
                    products(t, 0, 1, inverse, direct)
                    if not first:
                        chunk(t - 1, 1)
                    for b in range(B):
                        pe.wait_ge(pa_done[b], t + 1)
                        products(t, 1, b, lambda b, h: pa[b][:, h, 1], columns(y0))
                        if not first:
                            chunk(t - 1, 2 + b)
                    for b in range(B):
                        transpose(t + 1, b)
                    for b in range(B):
                        products(t, 2, b, inverse, columns(zz))
                    for b in range(B):
                        products(t, 3, b, lambda b, h: pa[b][:, h, 0], columns(uw))
                    pe.wait_ge(o_done, t + 1)
                    for b in range(B):
                        pe.wait_ge(kc_done[b], t + 1)
                        pe.wait_ge(w_done[b], t + 1)
                        mm = nc.tensor.matmul(psX[b * QK:(b + 1) * QK, 0:NC * QK], w[b][:, :], kc[b][:, :, :], start=True, stop=True)
                    mm.then_inc(m_ps, 1)
                    for b in range(B):
                        scores(t + 1, b)

                pe.wait_ge(const, DELTA_CONST)
                nc.tensor.matmul(acc[:, 0:H * DV], zero[:, :], zero[:, :], start=True, stop=True)
                for b in range(B):
                    transpose(0, b)
                for b in range(B):
                    scores(0, b)
                run(pe, step)
                transpose_q(PER - 1)
                pe.wait_ge(qt_sb, PER)
                for c in range(NC):
                    chunk(PER - 1, c)

            @block.scalar
            def _(act):
                def expand(t, b):
                    act.wait_ge(t_ps[b], t + 1)
                    act.activation(kT[b][0:QK], psT[b][0:QK, 0:P], ACT.Copy)
                    src = psT[b][0:QK, P:3 * P].rearrange("p (a c l) -> p c a l", a=2, c=NC)
                    for h in range(H):
                        ins = act.activation(qkx[b][0:QK, :, h], src, ACT.Copy, scale=mask_h[0:QK, h:h + 1])
                    ins.then_inc(kq_sb[b], 1)

                def copy_q(t):
                    act.wait_ge(qt_ps, t + 1)
                    for b in range(B):
                        rows = slice(b * QK, (b + 1) * QK)
                        ins = act.activation(qeT[b][rows], psX[rows, 0:P], ACT.Copy)
                    ins.then_inc(qt_sb, 1)

                def step(t, first):
                    if not first:
                        copy_q(t - 1)
                    for k, dst in ((0, y0), (1, zz)):
                        for b in range(B):
                            act.wait_ge(y_ps[b], 4 * t + k + 1)
                            act.activation(by_head(dst[b]), heads(psY[b]), ACT.Copy).then_inc(y_used[b], 1)
                    expand(t + 1, 0)
                    for b in range(B):
                        act.wait_ge(y_used[b], 4 * t + 3)
                        act.activation(w[b][:, :].rearrange("p (h c) -> p h c", h=H), by_head(uw[b])[:, :, DV:RW], ACT.Copy)\
                            .then_inc(w_done[b], 1)
                    expand(t + 1, 1)

                act.wait_ge(const, DELTA_CONST)
                act.wait_ge(mask_step, 1)
                for b in range(B):
                    expand(0, b)
                run(act, step)
                copy_q(PER - 1)

            @block.vector
            def _(dve):
                def mask_scores(t, b):
                    dve.wait_ge(g_ps[b], t + 1)
                    g = psG[b][:, 0:H * 2 * CH].rearrange("p (h a l) -> p a h l", h=H, a=2)
                    for a in range(2):
                        ins = nc.vector.tensor_tensor(
                            pa[b][:, :, a].rearrange("p h (c l) -> p h c l", c=NC),
                            g[:, a].unsqueeze(2).broadcast_to([P, H, NC, CH]),
                            mask_g[:, a].rearrange("p (c l) -> p c l", c=NC).unsqueeze(1).broadcast_to([P, H, NC, CH]), ALU.mult)
                    ins.then_inc(pa_done[b], 1)

                def state(t, c):
                    dve.wait_ge(s_ps, NC * t + c + 1)
                    nc.vector.tensor_tensor(S[(c + 1) % 2][:, :, :], acc[:, 0:H * DV].rearrange("p (h e) -> p h e", h=H),
                                            spread(mask_h[:, :], DV), ALU.mult).then_inc(s_sb, 1)

                def outputs(t):
                    dve.wait_ge(o_ps, t + 1)
                    for b in range(B):
                        dve.wait_ge(y_used[b], 4 * t + 4)
                        ins = nc.vector.tensor_tensor(o[:, blk(t, b)].rearrange("p a d -> p (a d)"),
                                                      psX[:, b * H * DV:(b + 1) * H * DV],
                                                      oi[b][:, :, :].rearrange("p h c -> p (h c)"), ALU.add)
                    ins.then_inc(o_done, 1)

                def step(t, first):
                    if not first:
                        for c in range(NC):
                            state(t - 1, c)
                        outputs(t - 1)
                    for b in range(B):
                        dve.wait_ge(y_ps[b], 4 * t + 3)
                        nc.vector.tensor_tensor(by_head(uw[b]), by_head(y0[b]), heads(psY[b]), ALU.subtract).then_inc(y_used[b], 1)
                    dve.wait_ge(o_done, t + 1)
                    for b in range(B):
                        dve.wait_ge(y_ps[b], 4 * t + 4)
                        y = heads(psY[b])
                        nc.vector.tensor_copy(oi[b][:, :, :], y[:, :, 0:DV])
                        nc.vector.tensor_tensor(qe[:, b].rearrange("p (h c) -> p h c", h=H),
                                                tok[:, blk(t, b), C_Q:C_Q + QK].rearrange("p a (h c) -> p (a h) c", h=H), y[:, :, DV:RW],
                                                ALU.subtract).then_inc(y_used[b], 1)
                    dve.wait_ge(m_ps, t + 1)
                    for b in range(B):
                        rows = slice(b * QK, (b + 1) * QK)
                        ins = nc.vector.tensor_tensor(mt[rows, :, b], psX[rows, 0:NC * QK].rearrange("p (c d) -> p c d", c=NC),
                                                      mask_m[rows].rearrange("p h d -> p (h d)").unsqueeze(1)
                                                      .broadcast_to([QK, NC, QK]), ALU.mult)
                    ins.then_inc(m_done, 1)
                    for b in range(B):
                        mask_scores(t + 1, b)

                dve.wait_ge(const, DELTA_CONST)
                nc.vector.tensor_tensor(mask_h[:, :], mask_bh[:, 0], mask_bh[:, 1], ALU.add).then_inc(mask_step, 1)
                dve.wait_ge(mask_step, 1)
                nc.vector.tensor_scalar(mask_m[:, :, :], spread(mask_h[:, :], DK), -1.0, None, ALU.mult).then_inc(mask_step, 1)
                dve.wait_ge(mask_step, 2)
                dve.sem_inc(s_sb, 1)
                dve.sem_inc(o_done, 1)
                for b in range(B):
                    mask_scores(0, b)
                run(dve, step)
                for c in range(NC):
                    state(PER - 1, c)
                outputs(PER - 1)


def group(t, b):
    return bass.ds(4 * t + b * PER, 4)


def stage_close_delta(nc, io, sb, ctx):
    with ExitStack() as st:
        def tmp(name, shp):
            return st.enter_context(nc.sbuf_tensor(name, shp, F32))

        def sem(name):
            return take(nc, name)

        def sems(name):
            return [sem(f"{name}{b}") for b in range(B)]

        o, gate, r, ident = sb["o"], sb["gate"], sb["r"], sb["ident"]
        wo = tmp("c_wo", [H * DV, D])
        sq = tmp("c_sq", [P, BLOCKS, D])
        ms, rs = tmp("c_ms", [P, BLOCKS, H]), tmp("c_rs", [P, BLOCKS, H])
        xin = [tmp(f"c_x{b}", [P, 4, D]) for b in range(B)]
        on = [tmp(f"c_on{b}", [P, 4, D]) for b in range(B)]
        og = [tmp(f"c_og{b}", [P, 4, D]) for b in range(B)]
        oT = [tmp(f"c_oT{b}", [P, 4, P]) for b in range(B)]
        psT = [st.enter_context(nc.psum_tensor(f"c_psT{b}", [P, 512], F32)) for b in range(B)]
        psO = [st.enter_context(nc.psum_tensor(f"c_psO{b}", [P, 4, D], F32)) for b in range(B)]
        x_in, t_ps, t_sb, o_ps, r_done, on_done, og_done = (sems(f"c_{n}") for n in (
            "x_in", "t_ps", "t_sb", "o_ps", "r_done", "on_done", "og_done"))
        w_in, squared, rooted, v_step = (sem(f"c_{n}") for n in ("w_in", "squared", "rooted", "v_step"))
        x_dram = io["x"].rearrange("b (t k p) d -> p b t k d", p=P, k=4)

        with nc.Block() as block:
            @block.sync
            def _(sp):
                sp.dma_start(wo[:, :], io["L0_Wo"][:, :]).then_inc(w_in, 16)
                for b in range(B):
                    sp.dma_start(xin[b][:, :, :], x_dram[:, b, 0]).then_inc(x_in[b], 16)
                with sp.Fori(1, PER // 4) as t:
                    for b in range(B):
                        sp.wait_ge(r_done[b], t)
                        sp.dma_start(xin[b][:, :, :], x_dram[:, b, bass.ds(t, 1)].rearrange("p a k d -> p (a k) d"))\
                            .then_inc(x_in[b], 16)

            @block.scalar
            def _(act):
                for b in range(B):
                    act.activation(sq[:, b * PER:(b + 1) * PER], o[:, b * PER:(b + 1) * PER], ACT.Square).then_inc(squared, 1)
                act.wait_ge(v_step, B + 1)
                act.activation(rs[:, :, :], ms[:, :, :], ACT.Sqrt).then_inc(rooted, 1)

                def step(t, first, last):
                    for b in range(B):
                        act.wait_ge(t_ps[b], t + 1)
                        act.activation(oT[b][:, :, :], psT[b][:, :].rearrange("p (k l) -> p k l", k=4), ACT.Copy)\
                            .then_inc(t_sb[b], 1)

                run_steps(act, PER // 4, step)

            @block.vector
            def _(dve):
                for b in range(B):
                    s = slice(b * PER, (b + 1) * PER)
                    dve.wait_ge(squared, b + 1)
                    nc.vector.tensor_reduce(ms[:, s], sq[:, s].rearrange("p n (h c) -> p n h c", h=H), AX.X, ALU.add)\
                        .then_inc(v_step, 1)
                dve.wait_ge(v_step, B)
                nc.vector.tensor_scalar(ms[:, :, :], ms[:, :, :], 1.0 / DV, EPS, ALU.mult, ALU.add).then_inc(v_step, 1)
                dve.wait_ge(rooted, 1)
                nc.vector.reciprocal(rs[:, :, :], rs[:, :, :]).then_inc(v_step, 1)
                dve.wait_ge(v_step, B + 2)

                def residual(t):
                    for b in range(B):
                        dve.wait_ge(o_ps[b], t + 1)
                        dve.wait_ge(x_in[b], 16 * t + 16)
                        nc.vector.tensor_tensor(r[:, group(t, b)], psO[b][:, :, :], xin[b][:, :, :], ALU.add)\
                            .then_inc(r_done[b], 1)

                def step(t, first, last):
                    for b in range(B):
                        heads = on[b][:, :, :].rearrange("p k (h c) -> p k h c", h=H)
                        if not first:
                            dve.wait_ge(og_done[b], t)
                        nc.vector.tensor_tensor(heads, o[:, group(t, b)].rearrange("p k (h c) -> p k h c", h=H),
                                                spread(rs[:, group(t, b)], DV), ALU.mult).then_inc(on_done[b], 1)
                    for b in range(B):
                        dve.wait_ge(on_done[b], t + 1)
                        if not first:
                            dve.wait_ge(t_ps[b], t)
                        nc.vector.tensor_tensor(og[b][:, :, :], on[b][:, :, :], gate[:, group(t, b)], ALU.mult)\
                            .then_inc(og_done[b], 1)
                    if not first:
                        residual(t - 1)

                run_steps(dve, PER // 4, step)
                residual(PER // 4 - 1)

            @block.tensor
            def _(pe):
                pe.wait_ge(w_in, 16)

                def step(t, first, last):
                    for b in range(B):
                        if not first:
                            pe.wait_ge(t_sb[b], t)
                        pe.wait_ge(og_done[b], t + 1)
                        for k in range(4):
                            mm = nc.tensor.transpose(psT[b][:, k * P:(k + 1) * P], og[b][:, k], ident[:, :])
                        mm.then_inc(t_ps[b], 1)
                    for b in range(B):
                        if not first:
                            pe.wait_ge(r_done[b], t)
                        pe.wait_ge(t_sb[b], t + 1)
                        for k in range(4):
                            mm = nc.tensor.matmul(psO[b][:, k], oT[b][:, k], wo[:, :], start=True, stop=True)
                        mm.then_inc(o_ps[b], 1)

                run_steps(pe, PER // 4, step)


def stage_norm(nc, io, sb, tag, router=None, router_in=None, routed=None, pending=()):
    ways, outs = routed if routed is not None else (0, None)
    with ExitStack() as st:
        def tmp(name, shp):
            return st.enter_context(nc.sbuf_tensor(f"{tag}_{name}", shp, F32))

        def sem(name):
            return take(nc, f"{tag}_{name}")

        def sems(name):
            return [sem(f"{name}{b}") for b in range(B)]

        r, x, xT, ident = sb["r"], sb["x"], sb.get("xT"), sb["ident"]
        stats = [tmp(f"stats{b}", [P, 4, 6]) for b in range(B)]
        mean, gap, m2 = ([tmp(f"{n}{b}", [P, 4]) for b in range(B)] for n in ("mean", "gap", "m2"))
        ve = [tmp(f"ve{b}", [P, 4]) for b in range(B)]
        sd = [tmp(f"sd{b}", [P, 4]) for b in range(B)]
        rstd = [tmp(f"rstd{b}", [P, 4]) for b in range(B)]
        xn = [tmp(f"xn{b}", [P, 4, D]) for b in range(B)]
        step_done, rooted, n_done, copied, t_ps, t_sb, t_out, l_ps, l_done, sent = (sems(n) for n in (
            "step", "rooted", "n_done", "copied", "t_ps", "t_sb", "t_out", "l_ps", "l_done", "sent"))
        got, summed = sems("got"), sems("summed")
        y = [tmp(f"y{b}", [P, 4 * ways, D]) for b in range(B)] if ways else None
        rs = [tmp(f"rs{b}", [P, 4, D]) for b in range(B)] if ways else None
        if router is not None:
            xs = [tmp(f"xs{b}", [P, 4, P]) for b in range(B)]
            psT = [st.enter_context(nc.psum_tensor(f"{tag}_psT{b}", [P, 512], F32)) for b in range(B)]
            psL = [st.enter_context(nc.psum_tensor(f"{tag}_psL{b}", [P, 4, P], F32)) for b in range(B)]
            logits = sb["logits"]

        with nc.Block() as block:
            @block.vector
            def _(dve):
                def source(t, b, k):
                    return rs[b][:, k] if ways else r[:, bass.ds(4 * t + (b * PER + k), 1)].rearrange("p a d -> p (a d)")

                def copy_logits(t):
                    for b in range(B):
                        dve.wait_ge(l_ps[b], t + 1)
                        nc.vector.tensor_copy(logits[:, group(t, b)], psL[b][:, :, 0:E]).then_inc(sent[b], 1)

                def step(t, first, last):
                    for b in range(B):
                        if ways:
                            dve.wait_ge(got[b], 64 * ways * t + 64 * ways)
                            if not first:
                                dve.wait_ge(n_done[b], t)
                        for w in range(ways):
                            for k in range(4):
                                at = bass.ds(4 * t + (b * PER + k), 1)
                                base = rs[b][:, k] if w else x[:, at].rearrange("p a d -> p (a d)")
                                ins = nc.vector.scalar_tensor_tensor(rs[b][:, k], y[b][:, 4 * w + k], sb["weight"][w][:, at], base,
                                                                     ALU.mult, ALU.add)
                            ins.then_inc(summed[b], 1)
                            dve.wait_ge(summed[b], ways * t + (w + 1))
                        for k in range(4):
                            ins = nc.vector.bn_stats(stats[b][:, k], source(t, b, k))
                        ins.then_inc(step_done[b], 1)
                    for b in range(B):
                        s4 = stats[b]
                        dve.wait_ge(step_done[b], 4 * t + 1)
                        nc.vector.tensor_tensor(mean[b][:, :], s4[:, :, 1], s4[:, :, 4], ALU.add)
                        nc.vector.tensor_tensor(gap[b][:, :], s4[:, :, 1], s4[:, :, 4], ALU.subtract)
                        nc.vector.tensor_tensor(m2[b][:, :], s4[:, :, 2], s4[:, :, 5], ALU.add).then_inc(step_done[b], 1)
                    for b in range(B):
                        dve.wait_ge(step_done[b], 4 * t + 2)
                        nc.vector.tensor_scalar(mean[b][:, :], mean[b][:, :], 0.5, None, ALU.mult)
                        nc.vector.scalar_tensor_tensor(gap[b][:, :], gap[b][:, :], 0.25, gap[b][:, :], ALU.mult, ALU.mult)
                        nc.vector.tensor_scalar(m2[b][:, :], m2[b][:, :], 1.0 / D, EPS, ALU.mult, ALU.add).then_inc(step_done[b], 1)
                    for b in range(B):
                        dve.wait_ge(step_done[b], 4 * t + 3)
                        nc.vector.tensor_tensor(ve[b][:, :], m2[b][:, :], gap[b][:, :], ALU.add).then_inc(step_done[b], 1)
                    if router is not None and not first:
                        copy_logits(t - 1)
                    for b in range(B):
                        dve.wait_ge(rooted[b], t + 1)
                        nc.vector.reciprocal(rstd[b][:, :], sd[b][:, :]).then_inc(l_done[b], 1)
                    for b in range(B):
                        dve.wait_ge(l_done[b], t + 1)
                        if not first:
                            if router is not None:
                                dve.wait_ge(t_ps[b], t)
                                dve.wait_ge(copied[b], t)
                            else:
                                dve.wait_ge(sent[b], 16 * t)
                        for k in range(4):
                            ins = nc.vector.tensor_scalar(xn[b][:, k], source(t, b, k), mean[b][:, k:k + 1], rstd[b][:, k:k + 1],
                                                          ALU.subtract, ALU.mult)
                        ins.then_inc(n_done[b], 1)

                run_steps(dve, PER // 4, step)
                if router is not None:
                    copy_logits(PER // 4 - 1)

            @block.scalar
            def _(act):
                def step(t, first, last):
                    for b in range(B):
                        act.wait_ge(step_done[b], 4 * t + 4)
                        if not first:
                            act.wait_ge(l_done[b], t)
                        act.activation(sd[b][:, :], ve[b][:, :], ACT.Sqrt).then_inc(rooted[b], 1)
                    if router is not None:
                        for b in range(B):
                            act.wait_ge(t_ps[b], t + 1)
                            act.activation(xs[b][:, :, :].rearrange("p k l -> p (k l)"), psT[b][:, :], ACT.Copy).then_inc(t_sb[b], 1)
                            if xT is not None:
                                act.activation(xT[:, bass.ds(512 * t + b * L, 512)], psT[b][:, :], ACT.Copy).then_inc(t_out[b], 1)
                        for b in range(B):
                            act.activation(x[:, group(t, b)], xn[b][:, :, :], ACT.Copy).then_inc(copied[b], 1)

                run_steps(act, PER // 4, step)

            if ways:
                @block.gpsimd
                def _(pool):
                    for t in range(PER // 4):
                        for b in range(B):
                            if t:
                                pool.wait_ge(summed[b], ways * t)
                            for k in range(4):
                                for w in range(ways):
                                    n = 4 * t + b * PER + k
                                    at = sb["slot"][w][:, n:n + 1]
                                    pool.indirect_dma_start(out=y[b][:, 4 * w + k], out_offset=None, in_=outs,
                                                            in_offset=bass.IndirectOffsetOnAxis(ap=at, axis=0)).then_inc(got[b], 16)

            if router is None:
                @block.sync
                def _(sp):
                    out = io["out"].rearrange("b (t k p) d -> p b t k d", p=P, k=4)
                    with sp.Fori(0, PER // 4) as t:
                        for b in range(B):
                            sp.wait_ge(n_done[b], t + 1)
                            sp.dma_start(out[:, b, bass.ds(t, 1)].rearrange("p a k d -> p (a k) d"), xn[b][:, :, :])\
                                .then_inc(sent[b], 16)
                    for b in range(B):
                        sp.wait_ge(sent[b], 16 * (PER // 4))
            else:
                @block.sync
                def _(sp):
                    for signal, total in pending:
                        sp.wait_ge(signal, total)

                @block.tensor
                def _(pe):
                    if router_in is not None:
                        pe.wait_ge(router_in, 32)
                    def step(t, first, last):
                        for b in range(B):
                            if not first:
                                pe.wait_ge(t_out[b] if xT is not None else t_sb[b], t)
                            pe.wait_ge(n_done[b], t + 1)
                            for k in range(4):
                                mm = nc.tensor.transpose(psT[b][:, k * P:(k + 1) * P], xn[b][:, k], ident[:, :])
                            mm.then_inc(t_ps[b], 1)
                        for b in range(B):
                            if not first:
                                pe.wait_ge(sent[b], t)
                            pe.wait_ge(t_sb[b], t + 1)
                            for k in range(4):
                                mm = nc.tensor.matmul(psL[b][:, k], xs[b][:, k], router[:, :], start=True, stop=True)
                            mm.then_inc(l_ps[b], 1)

                    run_steps(pe, PER // 4, step)


STEPS = [4 * -(-(w * BLOCKS + E - 1) // 4) for w in (1, 2)]
AHEAD = 4


def stage_route(nc, io, sb, tag, ways, rows_dram, zeroed, bias=None):
    tiles = STEPS[ways - 1] + AHEAD
    with ExitStack() as st:
        def tmp(name, shp, dt=F32):
            return st.enter_context(nc.sbuf_tensor(f"{tag}_{name}", shp, dt))

        def sem(name):
            return take(nc, f"{tag}_{name}")

        lg, x = sb["logits"], sb["x"]
        weight, slot = sb["weight"], sb["slot"]
        eq, rank = tmp("eq", [P, BLOCKS, E]), tmp("rank", [P, E])
        sel = [tmp(f"sel{i}", [P, BLOCKS, E]) for i in range(2)]
        both = tmp("both", [P, BLOCKS, E])
        top = [tmp(f"top{i}", [P, BLOCKS]) for i in range(2)]
        key, ex, den = tmp("key", [P, BLOCKS]), tmp("ex", [P, BLOCKS, E]), tmp("den", [P, BLOCKS])
        br = tmp("br", [P, E])
        before, ones = tmp("before", [P, P]), tmp("ones", [P, P])
        seen = [tmp(f"seen{i}", [P, BLOCKS + 1, E]) for i in range(2)]
        place = tmp("place", [P, BLOCKS, E])
        picked = tmp("picked", [P, BLOCKS, E])
        slot_f = tmp("slot_f", [P, BLOCKS])
        steps, filled, first = tmp("steps", [P, BLOCKS]), tmp("filled", [P, E, BLOCKS]), tmp("first", [P, E])
        count, ends, upto = tmp("count", [P, E]), tmp("ends", [P, E]), tmp("upto", [P, E, E])
        tri_e = tmp("tri_e", [P, E, E])
        it, over = tmp("it", [P, tiles]), tmp("over", [P, tiles, E])
        exp_f, packed = tmp("exp_f", [P, tiles]), tmp("packed", [P, tiles // 4 - 1])
        ps_in = st.enter_context(nc.psum_tensor(f"{tag}_in", [P, 512], F32))
        ps_all = st.enter_context(nc.psum_tensor(f"{tag}_all", [P, 512], F32))
        step, exped, const, b_in, chosen, counted, slots, sent = (sem(n) for n in (
            "step", "exped", "const", "b_in", "chosen", "counted", "slots", "sent"))

        def every(ap, n):
            return ap.unsqueeze(1).broadcast_to([P, n, ap.shape[1]])

        with nc.Block() as block:
            @block.gpsimd
            def _(pool):
                pool.iota(steps[:, :], pattern=[[P, BLOCKS]], base=0, channel_multiplier=0, allow_small_or_imprecise_dtypes=True)
                pool.iota(it[:, :], pattern=[[1, tiles]], base=0, channel_multiplier=0, allow_small_or_imprecise_dtypes=True)
                pool.iota(rank[:, :], pattern=[[-1, E]], base=E, channel_multiplier=0, allow_small_or_imprecise_dtypes=True)
                pool.memset(ones[:, :], 1.0)
                pool.memset(before[:, :], 1.0)
                pool.memset(tri_e[:, :, :], 1.0).then_inc(const, 1)
                pool.wait_ge(const, 1)
                pool.affine_select(out=before[:, :], in_=before[:, :], compare_op=ALU.is_ge, fill=0.0, base=-1,
                                   pattern=[[1, P]], channel_multiplier=-1).then_inc(const, 1)
                pool.affine_select(out=tri_e[:, :, :], in_=tri_e[:, :, :], compare_op=ALU.is_ge, fill=0.0, base=0,
                                   pattern=[[1, E], [-1, E]], channel_multiplier=0).then_inc(const, 1)
                pool.wait_ge(const, 3)
                if zeroed is not None:
                    pool.wait_ge(zeroed, 16)
                for w in range(ways):
                    pool.wait_ge(slots, w + 1)
                    for n in range(BLOCKS):
                        pool.indirect_dma_start(out=rows_dram, out_offset=bass.IndirectOffsetOnAxis(ap=slot[w][:, n:n + 1], axis=0),
                                                in_=x[:, n], in_offset=None).then_inc(sent, 16)
                pool.wait_ge(sent, 16 * ways * BLOCKS)

            @block.sync
            def _(sp):
                if bias is not None:
                    sp.dma_start(br[:, :], bias.rearrange("(a e) -> a e", a=1).broadcast_to([P, E])).then_inc(b_in, 16)

            @block.scalar
            def _(act):
                act.wait_ge(exped, 1)
                if ways == 2:
                    act.activation(den[:, :], key[:, :], ACT.Exp).then_inc(exped, 1)
                else:
                    act.activation(ex[:, :, :], ex[:, :, :], ACT.Exp).then_inc(exped, 1)

            @block.tensor
            def _(pe):
                pe.wait_ge(const, 3)
                pe.wait_ge(*((chosen, 1) if ways == 2 else (step, 5 + (bias is not None))))
                rhs = (both if ways == 2 else sel[0])[:, :, :].rearrange("p n e -> p (n e)")
                nc.tensor.matmul(ps_in[:, 0:BLOCKS * E], before[:, :], rhs, start=True, stop=True).then_inc(counted, 1)
                nc.tensor.matmul(ps_all[:, 0:BLOCKS * E], ones[:, :], rhs, start=True, stop=True).then_inc(counted, 1)

            @block.vector
            def _(dve):
                v = nc.vector
                count_v = 0

                def link(ins):
                    nonlocal count_v
                    count_v += 1
                    ins.then_inc(step, 1)
                    dve.wait_ge(step, count_v)

                def choose(i):
                    link(v.tensor_reduce(top[i][:, :], lg[:, :, :], AX.X, ALU.max))
                    link(v.tensor_tensor(eq[:, :, :], lg[:, :, :], spread(top[i][:, :], E), ALU.is_equal))
                    link(v.tensor_tensor(eq[:, :, :], eq[:, :, :], every(rank[:, :], BLOCKS), ALU.mult))
                    link(v.tensor_reduce(key[:, :], eq[:, :, :], AX.X, ALU.max))
                    link(v.tensor_tensor(sel[i][:, :, :], eq[:, :, :], spread(key[:, :], E), ALU.is_equal))

                dve.wait_ge(const, 3)
                if bias is not None:
                    dve.wait_ge(b_in, 16)
                    link(v.tensor_tensor(lg[:, :, :], lg[:, :, :], every(br[:, :], BLOCKS), ALU.add))
                choose(0)
                if ways == 2:
                    link(v.scalar_tensor_tensor(lg[:, :, :], sel[0][:, :, :], -3.0e38, lg[:, :, :], ALU.mult, ALU.add))
                    choose(1)
                    v.tensor_tensor(both[:, :, :], sel[0][:, :, :], sel[1][:, :, :], ALU.add).then_inc(chosen, 1)
                    v.tensor_tensor(key[:, :], top[1][:, :], top[0][:, :], ALU.subtract).then_inc(exped, 1)
                else:
                    v.tensor_tensor(ex[:, :, :], lg[:, :, :], spread(top[0][:, :], E), ALU.subtract).then_inc(exped, 1)
                dve.wait_ge(counted, 2)
                v.memset(seen[0][:, 0], 0.0)
                link(v.tensor_copy(seen[0][:, 1:], ps_all[:, 0:BLOCKS * E].rearrange("p (n e) -> p n e", e=E)))
                a, d = 0, 1
                while d < BLOCKS + 1:
                    v.tensor_copy(seen[1 - a][:, 0:d], seen[a][:, 0:d])
                    link(v.tensor_tensor(seen[1 - a][:, d:], seen[a][:, d:], seen[a][:, 0:BLOCKS + 1 - d], ALU.add))
                    a, d = 1 - a, 2 * d
                total = seen[a][:, BLOCKS]
                link(v.tensor_tensor(filled[:, :, :], spread(total, BLOCKS), every(steps[:, :], E), ALU.is_gt))
                link(v.tensor_reduce(count[:, :], filled[:, :, :], AX.X, ALU.add))
                link(v.tensor_tensor(upto[:, :, :], every(count[:, :], E), tri_e[:, :, :], ALU.mult))
                link(v.tensor_reduce(ends[:, :], upto[:, :, :], AX.X, ALU.add))
                link(v.tensor_tensor(first[:, :], ends[:, :], count[:, :], ALU.subtract))
                link(v.tensor_scalar(first[:, :], first[:, :], float(P), None, ALU.mult))
                link(v.tensor_tensor(place[:, :, :], seen[a][:, 0:BLOCKS], ps_in[:, 0:BLOCKS * E].rearrange("p (n e) -> p n e", e=E),
                                     ALU.add))
                link(v.tensor_tensor(place[:, :, :], place[:, :, :], every(first[:, :], BLOCKS), ALU.add))
                for w in range(ways):
                    link(v.tensor_tensor(picked[:, :, :], place[:, :, :], sel[w][:, :, :], ALU.mult))
                    link(v.tensor_reduce(slot_f[:, :], picked[:, :, :], AX.X, ALU.add))
                    v.tensor_copy(slot[w][:, :], slot_f[:, :]).then_inc(slots, 1)
                if ways == 1:
                    dve.wait_ge(exped, 2)
                    link(v.tensor_reduce(den[:, :], ex[:, :, :], AX.X, ALU.add))
                    link(v.reciprocal(weight[0][:, :], den[:, :]))
                else:
                    dve.wait_ge(exped, 2)
                    link(v.tensor_scalar(top[0][:, :], den[:, :], 1.0, None, ALU.add))
                    link(v.reciprocal(weight[0][:, :], top[0][:, :]))
                    link(v.tensor_tensor(weight[1][:, :], den[:, :], weight[0][:, :], ALU.mult))
                link(v.tensor_tensor(over[:, :, :], spread(it[:, :], E), every(ends[:, :], tiles), ALU.is_ge))
                link(v.tensor_reduce(exp_f[:, :], over[:, :, :], AX.X, ALU.add))
                link(v.tensor_scalar(exp_f[:, :], exp_f[:, :], float(E - 1), None, ALU.min))
                quads = exp_f[:, :].rearrange("p (m j) -> p m j", j=4)
                n = tiles // 4 - 1
                link(v.tensor_copy(packed[:, :], quads[:, 0:n, 0]))
                for j in range(1, 6):
                    link(v.scalar_tensor_tensor(packed[:, :], quads[:, j // 4:j // 4 + n, j % 4], float(E ** j), packed[:, :],
                                                ALU.mult, ALU.add))
                v.tensor_copy(sb["expert_of"][:, n:n + 1], it[:, 0:1])
                link(v.tensor_copy(sb["expert_of"][:, 0:n], packed[:, :]))


def stage_tiles(nc, io, sb, tag, gated, rows_dram, out_dram, w_in, wa, wb, wc=None, b1=None, b2=None):
    tiles = STEPS[int(gated)]
    F = wa.shape[2]
    NF = F // P
    with ExitStack() as st:
        def tmp(name, shp, dt=F32):
            return st.enter_context(nc.sbuf_tensor(f"{tag}_{name}", shp, dt))

        def pair(name, shp):
            return [tmp(f"{name}{i}", shp) for i in range(2)]

        def sem(name):
            return take(nc, f"{tag}_{name}")

        def bank(name):
            return st.enter_context(nc.psum_tensor(f"{tag}_{name}", [P, 512], F32))

        ident, expert_of = sb["ident"], sb["expert_of"]
        row, y = pair("row", [P, 2, D]), pair("y", [P, 2, D])
        xT, pre, h, hT = pair("xT", [D, P]), pair("pre", [P, F]), pair("h", [P, F]), pair("hT", [P, NF, P])
        psX, psH, psT, psY = ([bank(f"{n}{i}") for i in range(2)] for n in ("psX", "psH", "psT", "psY"))
        l_in = [sem(f"l_in{i}") for i in range(2)]
        x_ps, x_sb, h_ps, pre_done, h_done, t_ps, t_sb, y_ps, y_sb = (sem(n) for n in (
            "x_ps", "x_sb", "h_ps", "pre_done", "h_done", "t_ps", "t_sb", "y_ps", "y_sb"))
        stored = [sem(f"stored{i}") for i in range(2)]
        rows_t, out_t = (a.rearrange("(n p) d -> p n d", p=P) for a in (rows_dram, out_dram))

        def experts(eng, m):
            packed = eng.value_load(expert_of[0:1, bass.ds(m, 1)], min_val=0, max_val=E ** 6 - 1)
            return [(packed >> (3 * j)) & (E - 1) for j in range(6)]

        with nc.Block() as block:
            @block.gpsimd
            def _(pool):
                def load(i, q):
                    pool.dma_start(row[q][:, :, :], rows_t[:, bass.ds(i, 2)]).then_inc(l_in[q], 16)

                load(0, 0)
                load(2, 1)
                with pool.Fori(0, tiles // 4) as m:
                    for q in range(2):
                        pool.wait_ge(x_ps, 4 * m + (2 * q + 2))
                        load(4 * m + (4 + 2 * q), q)
                for q in range(2):
                    pool.wait_ge(l_in[q], 4 * tiles + 16)

            @block.sync
            def _(sp):
                for q in range(2):
                    sp.sem_inc(stored[q], 1)
                with sp.Fori(0, tiles // 4) as m:
                    for q in range(2):
                        sp.wait_ge(y_sb, 4 * m + (2 * q + 3))
                        sp.dma_start(out_t[:, bass.ds(4 * m + 2 * q, 2)], y[q][:, :, :]).then_inc(stored[q], 16)
                for q in range(2):
                    sp.wait_ge(stored[q], 4 * tiles + 1)

            @block.tensor
            def _(pe):
                def x_up(m, j):
                    q, turn, p = j // 2 % 2, j // 4, j % 2
                    pe.wait_ge(l_in[q], 16 * m + 16 * (turn + 1))
                    nc.tensor.transpose(psX[p][:, 0:P], row[q][:, p], ident[:, :]).then_inc(x_ps, 1)

                def up(i, p, e):
                    pe.wait_ge(x_sb, i + 1)
                    if gated:
                        nc.tensor.matmul(psH[p][:, 0:F], xT[p][:, :], wa[:, bass.ds(e, 1)].rearrange("p a f -> p (a f)"),
                                         start=True, stop=True)
                        nc.tensor.matmul(psH[p][:, F:2 * F], xT[p][:, :], wc[:, bass.ds(e, 1)].rearrange("p a f -> p (a f)"),
                                         start=True, stop=True).then_inc(h_ps, 1)
                    else:
                        nc.tensor.matmul(psH[p][:, :], xT[p][:, :], wa[:, bass.ds(e, 1)].rearrange("p a f -> p (a f)"),
                                         start=True, stop=True).then_inc(h_ps, 1)

                if w_in is not None:
                    pe.wait_ge(w_in, 16 * 4)
                x_up(0, 0)
                x_up(0, 1)
                whose = experts(pe, 0)
                up(0, 0, whose[0])
                up(1, 1, whose[1])
                x_up(0, 2)
                following = pe.alloc_register(f"{tag}_experts")
                pe.load(following, expert_of[0:1, 0:1])
                with pe.Fori(0, tiles // 4) as m:
                    packed = pe.snap(bass.RuntimeValue.of_register_unchecked(following, min_val=0, max_val=E ** 6 - 1))
                    whose = [(packed >> (3 * j)) & (E - 1) for j in range(6)]
                    for j in range(4):
                        i, p = 4 * m + j, j % 2
                        pe.wait_ge(h_done, i + 1)
                        pe.wait_ge(t_sb, i + 1)
                        for f in range(NF):
                            mm = nc.tensor.transpose(psT[p][:, f * P:(f + 1) * P], h[p][:, f * P:(f + 1) * P], ident[:, :])
                        mm.then_inc(t_ps, 1)
                        x_up(m, j + 3)
                        up(i + 2, p, whose[j + 2])
                        if j == 3:
                            pe.load(following, expert_of[0:1, bass.ds(m + 1, 1)])
                        pe.wait_ge(t_sb, i + 2)
                        pe.wait_ge(y_sb, i + 1)
                        for f in range(NF):
                            mm = nc.tensor.matmul(psY[p][:, 0:D], hT[p][:, f], wb[:, bass.ds(whose[j] * NF + f, 1)].rearrange("p a d -> p (a d)"),
                                                  start=(f == 0), stop=(f == NF - 1))
                        mm.then_inc(y_ps, 1)

            @block.scalar
            def _(act):
                def act_h(i, p):
                    if gated:
                        act.wait_ge(h_ps, i + 1)
                        act.activation(pre[p][:, :], psH[p][:, 0:F], ACT.Silu).then_inc(pre_done, 1)
                    else:
                        act.wait_ge(pre_done, i + 1)
                        act.activation(h[p][:, :], pre[p][:, :], ACT.Gelu).then_inc(h_done, 1)

                act.sem_inc(t_sb, 1)
                act_h(0, 0)
                act_h(1, 1)
                with act.Fori(0, tiles // 4) as m:
                    for j in range(4):
                        i, p = 4 * m + j, j % 2
                        act.wait_ge(t_ps, i + 1)
                        act.activation(hT[p][:, :, :].rearrange("p f l -> p (f l)"), psT[p][:, 0:F], ACT.Copy).then_inc(t_sb, 1)
                        act_h(i + 2, p)

            @block.vector
            def _(dve):
                def x_copy(i, p):
                    dve.wait_ge(x_ps, i + 1)
                    nc.vector.tensor_copy(xT[p][:, :], psX[p][:, 0:P]).then_inc(x_sb, 1)

                def vec_h(i, p, e):
                    if gated:
                        dve.wait_ge(pre_done, i + 1)
                        nc.vector.tensor_tensor(h[p][:, :], pre[p][:, :], psH[p][:, F:2 * F], ALU.mult).then_inc(h_done, 1)
                    else:
                        dve.wait_ge(h_ps, i + 1)
                        nc.vector.tensor_tensor(pre[p][:, :], psH[p][:, :], b1[:, bass.ds(e, 1)].rearrange("p a f -> p (a f)"),
                                                ALU.add).then_inc(pre_done, 1)

                dve.sem_inc(y_sb, 1)
                if w_in is not None:
                    dve.wait_ge(w_in, 16 * 4)
                x_copy(0, 0)
                x_copy(1, 1)
                whose = [None] * 6 if gated else experts(dve, 0)
                vec_h(0, 0, whose[0])
                vec_h(1, 1, whose[1])
                x_copy(2, 0)
                with dve.Fori(0, tiles // 4) as m:
                    if not gated:
                        whose = experts(dve, m)
                    for j in range(4):
                        i, p, q = 4 * m + j, j % 2, j // 2
                        dve.wait_ge(t_ps, i + 1)
                        x_copy(i + 3, 1 - p)
                        vec_h(i + 2, p, whose[j + 2])
                        dve.wait_ge(stored[q], 16 * m + 1)
                        dve.wait_ge(y_ps, i + 1)
                        if gated:
                            nc.vector.tensor_copy(y[q][:, p], psY[p][:, 0:D]).then_inc(y_sb, 1)
                        else:
                            nc.vector.tensor_tensor(y[q][:, p], psY[p][:, 0:D], b2[:, bass.ds(whose[j], 1)].rearrange("p a d -> p (a d)"),
                                                    ALU.add).then_inc(y_sb, 1)


def stage_linear_attention(nc, io, sb):
    NH = 16
    DH = D // NH
    HF = NH // 2 * DH * DH
    with ExitStack() as st:
        def tmp(name, shp):
            return st.enter_context(nc.sbuf_tensor(f"l_{name}", shp, F32))

        def pair(name, shp):
            return [tmp(f"{name}{b}", shp) for b in range(B)]

        def sem(name):
            return take(nc, f"l_{name}")

        def sems(name):
            return [sem(f"{name}{b}") for b in range(B)]

        def bank(name):
            return st.enter_context(nc.psum_tensor(f"l_{name}", [P, 512], F32))

        x, xT, r, ident = sb["x"], sb["xT"], sb["r"], sb["ident"]
        w_raw = tmp("w_raw", [D, 4, D])
        wT = tmp("wT", [D, 4, D])
        b_qkv, b_o = tmp("b_qkv", [P, 3, D]), tmp("b_o", [P, D])
        tri, mask, zero = tmp("tri", [P, P]), tmp("mask", [P, NH, DH]), tmp("zero", [P, P])
        xs, qkv, kv = pair("xs", [P, P]), pair("qkv", [P, 3, D]), pair("kv", [P, 2, HF])
        S, qT, prod = pair("S", [P, NH, DH]), pair("qT", [P, P]), pair("prod", [P, 2, HF])
        intra, out, oT = pair("intra", [P, D]), pair("out", [P, D]), pair("oT", [P, P])
        ps_a, ps_c, ps_s = [bank(f"a{b}") for b in range(B)], [bank(f"c{b}") for b in range(B)], [bank(f"s{b}") for b in range(B)]
        ps_t = st.enter_context(nc.psum_tensor("l_t", [P, 2, 512], F32))
        const, w_in, b_in, w_ps, w_sb, r_init = (sem(n) for n in ("const", "w_in", "b_in", "w_ps", "w_sb", "r_init"))
        (x_in, qkv_ps, qkv_sb, kv_done, t_ps, prod_done, s_ps, s_sb, q_ps, q_sb, c_ps, out_done, o_ps, o_sb, y_ps,
         r_done, red_done) = (sems(n) for n in ("x_in", "qkv_ps", "qkv_sb", "kv_done", "t_ps", "prod_done", "s_ps", "s_sb", "q_ps",
                                                "q_sb", "c_ps", "out_done", "o_ps", "o_sb", "y_ps", "r_done", "red_done"))


        def before_of(t, b):
            return (t, 0) if b else (t - 1, 1)

        def after_of(t, b):
            return (t + 1, 0) if b else (t, 1)

        def flat(ap):
            return ap.rearrange("p a d -> p (a d)")

        def run(eng, step):
            step(0, True)
            with eng.Fori(1, PER) as t:
                step(t, False)

        with nc.Block() as block:
            @block.sync
            def _(sp):
                for i, n in enumerate(("wq", "wk", "wv", "wo")):
                    sp.dma_start(w_raw[:, i], io[f"L1_{n}_w"][:, :]).then_inc(w_in, 16)
                for i, n in enumerate(("wq", "wk", "wv", "wo")):
                    to = b_qkv[:, i] if i < 3 else b_o[:, :]
                    sp.dma_start(to, io[f"L1_{n}_b"].rearrange("(a e) -> a e", a=1).broadcast_to([P, D])).then_inc(b_in, 16)
                for b in range(B):
                    sp.dma_start(xs[b][:, :], xT[:, b * L:b * L + P]).then_inc(x_in[b], 16)
                with sp.Fori(1, PER) as t:
                    for b in range(B):
                        sp.wait_ge(qkv_ps[b], t)
                        sp.dma_start(xs[b][:, :], xT[:, bass.ds(P * t + b * L, P)]).then_inc(x_in[b], 16)
                for b in range(B):
                    sp.wait_ge(qkv_ps[b], PER)
                    sp.dma_start(xs[b][:, :], xT[:, 0:P]).then_inc(x_in[b], 16)

            @block.gpsimd
            def _(pool):
                pool.memset(zero[:, :], 0.0).then_inc(const, 1)
                pool.memset(tri[:, :], 1.0).then_inc(const, 1)
                pool.memset(mask[:, :, :], 1.0).then_inc(const, 1)
                for b in range(B):
                    pool.memset(S[b][:, :, :], 0.0).then_inc(const, 1)
                n = 3 + B
                for ap, base, pattern, mult in ((tri[:, :], 0, [[1, P]], -1), (mask[:, :, :], 0, [[-DH, NH], [0, DH]], 1),
                                                (mask[:, :, :], DH - 1, [[DH, NH], [0, DH]], -1)):
                    pool.wait_ge(const, n)
                    pool.affine_select(out=ap, in_=ap, compare_op=ALU.is_ge, fill=0.0, base=base, pattern=pattern,
                                       channel_multiplier=mult).then_inc(const, 1)
                    n += 1

                def step(t, first):
                    for b in range(B):
                        pool.wait_ge(qkv_sb[b], t + 1)
                        for i in range(2):
                            if not first:
                                pool.wait_ge(t_ps[b], 2 * t - 1 + i)
                            hs = slice(i * D // 2, (i + 1) * D // 2)
                            k = qkv[b][:, 1, hs].rearrange("p (h c) -> p h c", c=DH)
                            v = qkv[b][:, 2, hs].rearrange("p (h c) -> p h c", c=DH)
                            pool.tensor_tensor(kv[b][:, i].rearrange("p (h e d) -> p h e d", e=DH, d=DH),
                                               k.unsqueeze(2).broadcast_to([P, NH // 2, DH, DH]), spread(v, DH), ALU.mult)\
                                .then_inc(kv_done[b], 1)

                run(pool, step)

            @block.tensor
            def _(pe):
                def project(t, b):
                    pe.wait_ge(x_in[b], 16 * t + 16)
                    nc.tensor.matmul(ps_a[b][:, 0:3 * D], xs[b][:, :], wT[:, 0:3].rearrange("p a e -> p (a e)"),
                                     start=True, stop=True).then_inc(qkv_ps[b], 1)

                def transpose_q(t, b):
                    pe.wait_ge(qkv_sb[b], t + 1)
                    nc.tensor.transpose(ps_a[b][:, 0:P], qkv[b][:, 0], ident[:, :]).then_inc(q_ps[b], 1)

                def transpose_out(t, b):
                    pe.wait_ge(out_done[b], t + 1)
                    nc.tensor.transpose(ps_c[b][:, 0:P], out[b][:, :], ident[:, :]).then_inc(o_ps[b], 1)

                def output(t, b):
                    pe.wait_ge(o_sb[b], t + 1)
                    nc.tensor.matmul(ps_c[b][:, 0:D], oT[b][:, :], wT[:, 3], start=True, stop=True).then_inc(y_ps[b], 1)

                def step(t, first):
                    for b in range(B):
                        tp, bp = before_of(t, b)
                        none_before = first and b == 0
                        for i in range(2):
                            if not none_before:
                                pe.wait_ge(prod_done[bp], 2 * tp + 1 + i)
                            pe.wait_ge(kv_done[b], 2 * t + 1 + i)
                            nc.tensor.matmul(ps_t[:, i], tri[:, :], kv[b][:, i], start=True, stop=True).then_inc(t_ps[b], 1)
                        if not none_before:
                            transpose_out(tp, bp)
                        if not first:
                            pe.wait_ge(s_sb[b], t)
                            pe.wait_ge(r_done[b], t)
                        pe.wait_ge(q_sb[b], t + 1)
                        nc.tensor.matmul(ps_c[b][:, 0:D], qT[b][:, :], S[b][:, :, :].rearrange("p h c -> p (h c)"),
                                         start=True, stop=True).then_inc(c_ps[b], 1)
                        nc.tensor.matmul(ps_s[b][:, 0:D], qkv[b][:, 1], qkv[b][:, 2], start=False, stop=True,
                                         skip_group_check=True).then_inc(s_ps[b], 1)
                        transpose_q(*after_of(t, b))
                        project(t + 1, b)
                        if not none_before:
                            output(tp, bp)

                pe.wait_ge(const, 6 + B)
                pe.wait_ge(w_in, 64)
                for i in range(4):
                    mm = nc.tensor.transpose(ps_a[0][:, i * D:(i + 1) * D], w_raw[:, i], ident[:, :])
                mm.then_inc(w_ps, 1)
                for b in range(B):
                    nc.tensor.matmul(ps_s[b][:, 0:D], zero[:, :], zero[:, :], start=True, stop=True)
                pe.wait_ge(w_sb, 1)
                for b in range(B):
                    project(0, b)
                transpose_q(0, 0)
                run(pe, step)
                transpose_out(PER - 1, B - 1)
                output(PER - 1, B - 1)

            @block.scalar
            def _(act):
                def copy_q(t, b):
                    act.wait_ge(q_ps[b], t + 1)
                    act.activation(qT[b][:, :], ps_a[b][:, 0:P], ACT.Copy).then_inc(q_sb[b], 1)

                def copy_out(t, b):
                    act.wait_ge(o_ps[b], t + 1)
                    act.activation(oT[b][:, :], ps_c[b][:, 0:P], ACT.Copy).then_inc(o_sb[b], 1)

                def step(t, first):
                    for b in range(B):
                        copy_q(*after_of(t, b))
                        if not (first and b == 0):
                            copy_out(*before_of(t, b))

                act.wait_ge(w_ps, 1)
                act.activation(wT[:, :, :].rearrange("p a e -> p (a e)"), ps_a[0][:, :], ACT.Copy).then_inc(w_sb, 1)
                copy_q(0, 0)
                run(act, step)
                copy_out(PER - 1, B - 1)

            @block.vector
            def _(dve):
                def add_bias(t, b):
                    dve.wait_ge(qkv_ps[b], t + 1)
                    nc.vector.tensor_tensor(qkv[b][:, :, :], ps_a[b][:, 0:3 * D].rearrange("p (a e) -> p a e", a=3),
                                            b_qkv[:, :, :], ALU.add).then_inc(qkv_sb[b], 1)

                def add_output(t, b):
                    at = bass.ds(t + b * PER, 1)
                    dve.wait_ge(y_ps[b], t + 1)
                    nc.vector.tensor_tensor(flat(r[:, at]), flat(r[:, at]), ps_c[b][:, 0:D], ALU.add).then_inc(r_done[b], 1)

                def step(t, first):
                    for b in range(B):
                        dve.wait_ge(qkv_sb[b], t + 1)
                        if not first:
                            dve.wait_ge(red_done[b], t)
                        for i in range(2):
                            q = qkv[b][:, 0, i * D // 2:(i + 1) * D // 2].rearrange("p (h c) -> p h c", c=DH)
                            dve.wait_ge(t_ps[b], 2 * t + 1 + i)
                            nc.vector.tensor_tensor(prod[b][:, i].rearrange("p (h e d) -> p h e d", e=DH, d=DH),
                                                    ps_t[:, i].rearrange("p (h e d) -> p h e d", e=DH, d=DH),
                                                    q.unsqueeze(2).broadcast_to([P, NH // 2, DH, DH]), ALU.mult)\
                                .then_inc(prod_done[b], 1)
                        dve.wait_ge(c_ps[b], t + 1)
                        dve.wait_ge(s_ps[b], t + 1)
                        nc.vector.tensor_tensor(S[b][:, :, :], ps_s[b][:, 0:D].rearrange("p (h c) -> p h c", c=DH), mask[:, :, :],
                                                ALU.mult).then_inc(s_sb[b], 1)
                        dve.wait_ge(prod_done[b], 2 * t + 2)
                        dve.wait_ge(kv_done[b], 2 * t + 2)
                        add_bias(t + 1, b)
                        nc.vector.tensor_reduce(intra[b][:, :], prod[b][:, :, :].rearrange("p i (g d) -> p (i g) d", d=DH), AX.X,
                                                ALU.add).then_inc(red_done[b], 1)
                        if not (first and b == 0):
                            add_output(*before_of(t, b))
                        dve.wait_ge(red_done[b], t + 1)
                        nc.vector.tensor_tensor(out[b][:, :], intra[b][:, :], ps_c[b][:, 0:D], ALU.add).then_inc(out_done[b], 1)

                dve.wait_ge(b_in, 64)
                dve.wait_ge(const, 6 + B)
                for b in range(B):
                    add_bias(0, b)
                for b in range(B):
                    s = slice(b * PER, (b + 1) * PER)
                    nc.vector.tensor_tensor(r[:, s], x[:, s], b_o[:, :].unsqueeze(1).broadcast_to([P, PER, D]), ALU.add)\
                        .then_inc(r_init, 1)
                dve.wait_ge(r_init, B)
                run(dve, step)
                add_output(PER - 1, B - 1)


_INS = ["L0_attn_hidden_states", "L0_attn_conv_w", "L0_attn_Wq", "L0_attn_Wk", "L0_attn_Wv", "L0_attn_Wb", "L0_attn_Wg",
        "L0_attn_norm_w", "L0_attn_Wo", "L0_ffn_gate_w", "L0_ffn_w1", "L0_ffn_b1", "L0_ffn_w2", "L0_ffn_b2",
        "L1_attn_wq_w", "L1_attn_wq_b", "L1_attn_wk_w", "L1_attn_wk_b", "L1_attn_wv_w", "L1_attn_wv_b",
        "L1_attn_wo_w", "L1_attn_wo_b", "L1_ffn_Wr", "L1_ffn_br", "L1_ffn_W1", "L1_ffn_W3", "L1_ffn_W2"]


def build(nc, io):
    TAKEN.clear()
    io["kb_dram"] = nc.dram_tensor("kb_dram", [B * L, QK + H], F32, kind="Internal").ap()
    io["t_dram"] = nc.dram_tensor("t_dram", [B * L, H * SUB], F32, kind="Internal").ap()
    with ExitStack() as ctx:
        def keep(name, shp):
            return ctx.enter_context(nc.sbuf_tensor(name, shp, F32))

        sb = {"ident": keep("ident", [P, P]), "r": keep("r", [P, BLOCKS, D])}
        with ExitStack() as delta:
            def held(name, shp):
                return delta.enter_context(nc.sbuf_tensor(name, shp, F32))

            sb["tok"] = held("tok", [P, BLOCKS, TOKW])
            sb["gate"] = held("gate", [P, BLOCKS, D])
            sb["kp"] = held("kp", [P, CH, QK + H])
            stage_project(nc, io, sb, delta)
            sb["tinv"] = held("tinv", [P, BLOCKS, H * SUB])
            mem = delta_memory(nc, delta)
            stage_invert(nc, io, sb, mem)
            sb["o"] = held("o", [P, BLOCKS, D])
            stage_delta(nc, io, sb, mem)
            stage_close_delta(nc, io, sb, delta)
        give_back(nc)
        for w, steps in enumerate(STEPS):
            io[f"rows{w}"] = nc.dram_tensor(f"rows{w}_dram", [(steps + AHEAD) * P, D], F32, kind="Internal").ap()
            io[f"outs{w}"] = nc.dram_tensor(f"outs{w}_dram", [steps * P, D], F32, kind="Internal").ap()
        F0, F1 = io["L0_ffn_w1"].shape[2], io["L1_ffn_W1"].shape[2]
        w = {"wa": keep("wa", [D, E, F0]), "wb": keep("wb", [P, E * (F0 // P), D]), "b1": keep("b1", [P, E, F0]), "b2": keep("b2", [P, E, D])}
        v = {"wa": keep("va", [D, E, F1]), "wc": keep("vc", [D, E, F1]), "wb": keep("vb", [P, E * (F1 // P), D])}
        zero = keep("zero", [P, D])
        router = [keep(f"router{i}", [D, P]) for i in range(2)]
        w_in, v_in, router_in, zeroed = stage_weights(nc, io, w, v, router, zero)
        sb["x"], sb["logits"] = keep("x", [P, BLOCKS, D]), keep("logits", [P, BLOCKS, E])
        sb["weight"] = [keep(f"weight{i}", [P, BLOCKS]) for i in range(2)]
        for name, shp, dt in (("slot0", [P, BLOCKS], U32), ("slot1", [P, BLOCKS], U32), ("expert_of", [P, STEPS[1] // 4 + 1], I32)):
            sb[name] = ctx.enter_context(nc.sbuf_tensor(name, shp, dt))
        sb["slot"] = [sb["slot0"], sb["slot1"]]
        stage_norm(nc, io, sb, "n0", router[0], router_in=router_in)
        stage_route(nc, io, sb, "g0", 1, io["rows0"], zeroed[0])
        stage_tiles(nc, io, sb, "e0", False, io["rows0"], io["outs0"], w_in, **w)
        with ExitStack() as attention:
            sb["xT"] = attention.enter_context(nc.sbuf_tensor("xT_all", [D, B * L], F32))
            stage_norm(nc, io, sb, "n1", router[1], routed=(1, io["outs0"]), pending=((v_in, 16 * 3), (zeroed[1], 16)))
            give_back(nc)
            stage_linear_attention(nc, io, sb)
            del sb["xT"]
        give_back(nc)
        stage_norm(nc, io, sb, "n2", router[1])
        stage_route(nc, io, sb, "g1", 2, io["rows1"], None, bias=io["L1_ffn_br"])
        stage_tiles(nc, io, sb, "e1", True, io["rows1"], io["outs1"], None, **v)
        give_back(nc)
        stage_norm(nc, io, sb, "n3", routed=(2, io["outs1"]))


def stage_weights(nc, io, w, v, router, zero):
    w_in, v_in, router_in, const = (take(nc, n) for n in ("m_w_in", "m_v_in", "router_in", "zero_set"))
    zeroed = [take(nc, f"zeroed{i}") for i in range(2)]

    def zero_rows(sp, i):
        to = io[f"rows{i}"].rearrange("(n p) d -> p n d", p=P)
        sp.dma_start(to, zero[:, :].unsqueeze(1).broadcast_to([P, STEPS[i] + AHEAD, D])).then_inc(zeroed[i], 16)

    with nc.Block() as block:
        @block.gpsimd
        def _(pool):
            pool.memset(zero[:, :], 0.0)
            for i in range(2):
                ins = pool.memset(router[i][:, :], 0.0)
            ins.then_inc(const, 1)

        @block.sync
        def _(sp):
            sp.wait_ge(const, 1)
            for to, name in zip(router, ("L0_ffn_gate_w", "L1_ffn_Wr")):
                sp.dma_start(to[:, 0:E], io[name][:, :]).then_inc(router_in, 16)
            zero_rows(sp, 0)
            for to, name in ((w["b1"], "L0_ffn_b1"), (w["b2"], "L0_ffn_b2")):
                sp.dma_start(to[:, :, :], io[name].unsqueeze(0).broadcast_to([P, *io[name].shape])).then_inc(w_in, 16)
            sp.dma_start(w["wa"][:, :, :], io["L0_ffn_w1"].rearrange("e d f -> d e f")).then_inc(w_in, 16)
            sp.dma_start(w["wb"][:, :, :], io["L0_ffn_w2"].rearrange("e (f p) d -> p (e f) d", p=P)).then_inc(w_in, 16)
            sp.dma_start(v["wa"][:, :, :], io["L1_ffn_W1"].rearrange("e d f -> d e f")).then_inc(v_in, 16)
            sp.dma_start(v["wc"][:, :, :], io["L1_ffn_W3"].rearrange("e d f -> d e f")).then_inc(v_in, 16)
            sp.dma_start(v["wb"][:, :, :], io["L1_ffn_W2"].rearrange("e (f p) d -> p (e f) d", p=P)).then_inc(v_in, 16)
            zero_rows(sp, 1)
    return w_in, v_in, router_in, zeroed


def kernel(**inputs):
    import numpy as _np
    import concourse.bacc as _bacc
    from concourse.bass_utils import run_bass_kernel_spmd as _run

    nc = _bacc.Bacc("TRN2", target_bir_lowering=False, num_devices=1)
    arrays, io = {}, {}
    for name in _INS:
        a = _np.ascontiguousarray(inputs[name])
        arrays[f"in_{name}"] = a
        short = name.replace("_attn_", "_").replace("L0_hidden_states", "x")
        io[short] = nc.dram_tensor(f"in_{name}", a.shape, mybir.dt.from_np(a.dtype), kind="ExternalInput").ap()
    io["out"] = nc.dram_tensor("out_0", (B, L, D), F32, kind="ExternalOutput").ap()
    build(nc, io)
    r = _run(nc, [arrays], core_ids=[0])
    return r.results[0]["out_0"]
```
